# Optimizing a Trainium2 kernel written in Bass

```python
import numpy as np
import jax
import jax.numpy as jnp

def _softmax(x, axis=-1):
    return jax.nn.softmax(x, axis=axis)

def _gelu(x):
    return jax.nn.gelu(x, approximate=True)

def _silu(x):
    return jax.nn.silu(x)

def _sigmoid(x):
    return jax.nn.sigmoid(x)

def _layernorm(x, axis=-1, eps=1e-05):
    m = jnp.mean(x, axis=axis, keepdims=True)
    v = jnp.var(x, axis=axis, keepdims=True)
    return (x - m) / jnp.sqrt(v + eps)

def _scatter_add(tgt, idx, src, axis=0):
    return tgt.at[idx].add(src)

def _segment_sum(src, seg, n):
    return jax.ops.segment_sum(src, seg, n)
kernel_name = 'mk_xattn_ffn_d2_seqx_r8_73e73a'

def setup_inputs(seed: int=0):
    np.random.seed(seed)
    _w = jnp.asarray

    def _rec_inputs():
        import jax
        import jax.numpy as jnp
        _rk = jax.random.key(seed)
        x = -0.0002928 + 1 * jax.random.normal(jax.random.fold_in(_rk, 1), (16, 128, 256), jnp.float32)
        _lenS = 128 - jax.random.randint(jax.random.fold_in(_rk, 7), (16,), 0, max(1, 128 // 4) + 1, jnp.int32)
        _lenS2 = 128 - jax.random.randint(jax.random.fold_in(_rk, 8), (16,), 0, max(1, 128 // 4) + 1, jnp.int32)
        _ctx_2048P = jax.random.normal(jax.random.fold_in(_rk, 11), (16, 16, 256), jnp.float32)
        _ctx_2048c = jax.random.dirichlet(jax.random.fold_in(_rk, 511), 0.3 * jnp.ones((16,), jnp.float32), (16, 128))
        _ctx_2048t = jnp.einsum('bsk,bkd->bsd', _ctx_2048c, _ctx_2048P)
        _ctx_2048t = _ctx_2048t * jax.lax.rsqrt(jnp.mean(jnp.square(_ctx_2048t)) + 1e-12) * 0.953939
        ctx_2048 = -1.39393e-06 + 0.999914 * (_ctx_2048t + 0.3 * jax.random.normal(jax.random.fold_in(_rk, 611), (16, 128, 256), jnp.float32))
        _validS = jnp.arange(128)[None, :] < _lenS[:, None]
        _validS2 = jnp.arange(128)[None, :] < _lenS2[:, None]
        _causal = jnp.tril(jnp.ones((128, 128), dtype=bool))
        mask_Bx1x2048_fk1 = jnp.where(jnp.ones((16, 1, 256), dtype=bool), 1.0, 0.0).astype(jnp.float32)
        return (x, ctx_2048, mask_Bx1x2048_fk1)
    x, ctx_2048, mask_Bx1x2048_fk1 = _rec_inputs()

    def _L0_xattn_setup():
        import math
        import jax, jax.numpy as jnp
        import numpy as np
        SIZE = 128
        HEADS = 16
        HEAD_DIM = SIZE // HEADS
        B, T, S = (2, 256, 256)
        NEG = 1000000.0
        key = jax.random.key(seed)
        ks = jax.random.split(key, 10)
        target = jax.random.normal(ks[0], (B, SIZE, T), dtype=jnp.float32)
        source = jax.random.normal(ks[1], (B, SIZE, S), dtype=jnp.float32)
        target_mask = (jax.random.uniform(ks[2], (B, 1, T)) > 0.1).astype(jnp.float32)
        source_mask = (jax.random.uniform(ks[3], (B, 1, S)) > 0.1).astype(jnp.float32)
        scale = 1.0 / math.sqrt(SIZE)
        Wq = jax.random.normal(ks[4], (SIZE, SIZE), dtype=jnp.float32) * scale
        Wk = jax.random.normal(ks[5], (SIZE, SIZE), dtype=jnp.float32) * scale
        Wv = jax.random.normal(ks[6], (SIZE, SIZE), dtype=jnp.float32) * scale
        bq = jax.random.normal(ks[7], (SIZE,), dtype=jnp.float32) * 0.01
        bk = jax.random.normal(ks[8], (SIZE,), dtype=jnp.float32) * 0.01
        bv = jax.random.normal(ks[9], (SIZE,), dtype=jnp.float32) * 0.01
        return {'target': target, 'source': source, 'target_mask': target_mask, 'source_mask': source_mask, 'Wq': Wq, 'bq': bq, 'Wk': Wk, 'bk': bk, 'Wv': Wv, 'bv': bv}
    _L0_xattn_all = _L0_xattn_setup()
    _L0_xattn_in = {k: v for k, v in _L0_xattn_all.items() if k in ('Wq', 'bq', 'Wk', 'bk', 'Wv', 'bv')}
    del _L0_xattn_all

    def _L0_ffn_setup():
        import jax, jax.numpy as jnp
        import numpy as np
        D_MODEL, D_FF, NS, NR, KR = (256, 176, 2, 16, 4)
        B, S = (4, 256)

        def _moe_forward(u, shared_w1, shared_b1, shared_w2, shared_b2, routed_w1, routed_b1, routed_w2, routed_b2, centroids, bias):
            b, s, d = u.shape
            flat = u.reshape(-1, d)
            T = flat.shape[0]
            h = jax.nn.relu(jnp.einsum('td,ndf->ntf', flat, shared_w1) + shared_b1[:, None, :])
            shared_out = jnp.einsum('ntf,nfd->td', h, shared_w2) + shared_b2.sum(0)
            out = flat + shared_out
            scores = jax.nn.sigmoid(flat @ centroids.T) + bias
            vals, idx = jax.lax.top_k(scores, KR)
            gating = jnp.zeros_like(scores).at[jnp.arange(T)[:, None], idx].set(vals)
            gating = gating / jnp.clip(gating.sum(-1, keepdims=True), 1e-08)

            def step(acc, ew):
                w1, b1, w2, b2, g = ew
                hj = jax.nn.relu(flat @ w1 + b1)
                yj = hj @ w2 + b2
                return (acc + yj * g[:, None], None)
            rout0 = jnp.zeros_like(flat)
            rout, _ = jax.lax.scan(step, rout0, (routed_w1, routed_b1, routed_w2, routed_b2, gating.T))
            return (out + rout).reshape(b, s, d)
        key = jax.random.key(seed)
        ks = jax.random.split(key, 10)
        s1 = 1.0 / np.sqrt(D_MODEL)
        s2 = 1.0 / np.sqrt(D_FF)
        return {'u': jax.random.normal(ks[0], (B, S, D_MODEL), dtype=jnp.float32), 'shared_w1': jax.random.normal(ks[1], (NS, D_MODEL, D_FF), dtype=jnp.float32) * s1, 'shared_b1': jnp.zeros((NS, D_FF), dtype=jnp.float32), 'shared_w2': jax.random.normal(ks[2], (NS, D_FF, D_MODEL), dtype=jnp.float32) * s2, 'shared_b2': jnp.zeros((NS, D_MODEL), dtype=jnp.float32), 'routed_w1': jax.random.normal(ks[3], (NR, D_MODEL, D_FF), dtype=jnp.float32) * s1, 'routed_b1': jnp.zeros((NR, D_FF), dtype=jnp.float32), 'routed_w2': jax.random.normal(ks[4], (NR, D_FF, D_MODEL), dtype=jnp.float32) * s2, 'routed_b2': jnp.zeros((NR, D_MODEL), dtype=jnp.float32), 'centroids': jax.random.normal(ks[5], (NR, D_MODEL), dtype=jnp.float32) * s1, 'bias': jnp.zeros((NR,), dtype=jnp.float32)}
    _L0_ffn_all = _L0_ffn_setup()
    _L0_ffn_in = {k: v for k, v in _L0_ffn_all.items() if k in ('shared_w1', 'shared_b1', 'shared_w2', 'shared_b2', 'routed_w1', 'routed_b1', 'routed_w2', 'routed_b2', 'centroids', 'bias')}
    del _L0_ffn_all

    def _L1_xattn_setup():
        import jax, jax.numpy as jnp
        import numpy as np
        from jax import lax
        LN_EPS = 1e-05
        key = jax.random.key(seed)
        ks = jax.random.split(key, 8)
        B, S, T, D = (4, 128, 256, 256)
        scale = 0.02
        return {'Z': jax.random.normal(ks[0], (B, S, D), dtype=jnp.float32), 'kv': jax.random.normal(ks[1], (B, T, D), dtype=jnp.float32), 'decay': jnp.float32(0.9), 'W_in': jax.random.normal(ks[2], (D, D), dtype=jnp.float32) * scale, 'b_in': jnp.zeros((D,), dtype=jnp.float32), 'W_out': jax.random.normal(ks[3], (D, D), dtype=jnp.float32) * scale, 'b_out': jnp.zeros((D,), dtype=jnp.float32), 'gamma': jnp.ones((D,), dtype=jnp.float32), 'beta': jnp.zeros((D,), dtype=jnp.float32)}
    _L1_xattn_all = _L1_xattn_setup()
    _L1_xattn_in = {k: v for k, v in _L1_xattn_all.items() if k in ('decay', 'W_in', 'b_in', 'W_out', 'b_out', 'gamma', 'beta')}
    del _L1_xattn_all

    def _L1_ffn_setup():
        import jax, jax.numpy as jnp
        import numpy as np
        HIDDEN = 256
        INTER = 1024
        RETRIEVAL = 128
        NUM_EXPERTS = 512
        NUM_KEYS = 64
        TOP_K = 8
        B, S = (4, 256)
        key = jax.random.key(seed)
        ks = jax.random.split(key, 8)
        sc = 0.02
        return {'hidden_states': jax.random.normal(ks[0], (B, S, HIDDEN), jnp.float32), 'W_q': jax.random.normal(ks[1], (HIDDEN, RETRIEVAL), jnp.float32) * sc, 'keys': jax.random.normal(ks[2], (2, RETRIEVAL // 2, NUM_KEYS), jnp.float32) * sc, 'down_embed': jax.random.normal(ks[3], (NUM_EXPERTS, HIDDEN), jnp.float32) * sc, 'up_embed': jax.random.normal(ks[4], (NUM_EXPERTS, HIDDEN), jnp.float32) * sc, 'gate_w': jax.random.normal(ks[5], (HIDDEN, INTER), jnp.float32) * sc, 'up_w': jax.random.normal(ks[6], (HIDDEN, INTER), jnp.float32) * sc, 'down_w': jax.random.normal(ks[7], (INTER, HIDDEN), jnp.float32) * sc}
    _L1_ffn_all = _L1_ffn_setup()
    _L1_ffn_in = {k: v for k, v in _L1_ffn_all.items() if k in ('W_q', 'keys', 'down_embed', 'up_embed', 'gate_w', 'up_w', 'down_w')}
    del _L1_ffn_all
    return {'x': x, 'ctx_2048': ctx_2048, 'mask_Bx1x2048_fk1': mask_Bx1x2048_fk1, 'L0_xattn_Wq': _L0_xattn_in['Wq'], 'L0_xattn_bq': _L0_xattn_in['bq'], 'L0_xattn_Wk': _L0_xattn_in['Wk'], 'L0_xattn_bk': _L0_xattn_in['bk'], 'L0_xattn_Wv': _L0_xattn_in['Wv'], 'L0_xattn_bv': _L0_xattn_in['bv'], 'L0_ffn_shared_w1': _L0_ffn_in['shared_w1'], 'L0_ffn_shared_b1': _L0_ffn_in['shared_b1'], 'L0_ffn_shared_w2': _L0_ffn_in['shared_w2'], 'L0_ffn_shared_b2': _L0_ffn_in['shared_b2'], 'L0_ffn_routed_w1': _L0_ffn_in['routed_w1'], 'L0_ffn_routed_b1': _L0_ffn_in['routed_b1'], 'L0_ffn_routed_w2': _L0_ffn_in['routed_w2'], 'L0_ffn_routed_b2': _L0_ffn_in['routed_b2'], 'L0_ffn_centroids': _L0_ffn_in['centroids'], 'L0_ffn_bias': _L0_ffn_in['bias'], 'L1_xattn_decay': _L1_xattn_in['decay'], 'L1_xattn_W_in': _L1_xattn_in['W_in'], 'L1_xattn_b_in': _L1_xattn_in['b_in'], 'L1_xattn_W_out': _L1_xattn_in['W_out'], 'L1_xattn_b_out': _L1_xattn_in['b_out'], 'L1_xattn_gamma': _L1_xattn_in['gamma'], 'L1_xattn_beta': _L1_xattn_in['beta'], 'L1_ffn_W_q': _L1_ffn_in['W_q'], 'L1_ffn_keys': _L1_ffn_in['keys'], 'L1_ffn_down_embed': _L1_ffn_in['down_embed'], 'L1_ffn_up_embed': _L1_ffn_in['up_embed'], 'L1_ffn_gate_w': _L1_ffn_in['gate_w'], 'L1_ffn_up_w': _L1_ffn_in['up_w'], 'L1_ffn_down_w': _L1_ffn_in['down_w']}

def reference(x, ctx_2048, mask_Bx1x2048_fk1, L0_xattn_Wq, L0_xattn_bq, L0_xattn_Wk, L0_xattn_bk, L0_xattn_Wv, L0_xattn_bv, L0_ffn_shared_w1, L0_ffn_shared_b1, L0_ffn_shared_w2, L0_ffn_shared_b2, L0_ffn_routed_w1, L0_ffn_routed_b1, L0_ffn_routed_w2, L0_ffn_routed_b2, L0_ffn_centroids, L0_ffn_bias, L1_xattn_decay, L1_xattn_W_in, L1_xattn_b_in, L1_xattn_W_out, L1_xattn_b_out, L1_xattn_gamma, L1_xattn_beta, L1_ffn_W_q, L1_ffn_keys, L1_ffn_down_embed, L1_ffn_up_embed, L1_ffn_gate_w, L1_ffn_up_w, L1_ffn_down_w):
    import jax
    import jax.numpy as jnp

    def _L0_xattn_ref(target, source, target_mask, source_mask, Wq, bq, Wk, bk, Wv, bv):
        import math
        import jax, jax.numpy as jnp
        import numpy as np
        SIZE = 128
        HEADS = 16
        HEAD_DIM = SIZE // HEADS
        B, T, S = (2, 256, 256)
        NEG = 1000000.0
        b, _, t = target.shape
        s = source.shape[-1]
        q = jnp.einsum('oc,bct->bot', Wq, target) + bq[None, :, None]
        k = jnp.einsum('oc,bcs->bos', Wk, source) + bk[None, :, None]
        v = jnp.einsum('oc,bcs->bos', Wv, source) + bv[None, :, None]
        q = q.reshape(b, HEADS, HEAD_DIM, t)
        k = k.reshape(b, HEADS, HEAD_DIM, s)
        v = v.reshape(b, HEADS, HEAD_DIM, s)
        dot = jnp.einsum('bhdt,bhds->bhts', q, k) / math.sqrt(HEAD_DIM)
        mask = target_mask[:, :, :, None] * source_mask[:, :, None, :]
        dot = mask * dot - (1.0 - mask) * NEG
        amap = jax.nn.softmax(dot, axis=-1) * mask
        out = jnp.einsum('bhts,bhds->bhdt', amap, v)
        return out.reshape(b, HEADS * HEAD_DIM, t)

    def _L0_ffn_ref(u, shared_w1, shared_b1, shared_w2, shared_b2, routed_w1, routed_b1, routed_w2, routed_b2, centroids, bias):
        import jax, jax.numpy as jnp
        import numpy as np
        D_MODEL, D_FF, NS, NR, KR = (256, 176, 2, 16, 4)
        B, S = (4, 256)

        def _moe_forward(u, shared_w1, shared_b1, shared_w2, shared_b2, routed_w1, routed_b1, routed_w2, routed_b2, centroids, bias):
            b, s, d = u.shape
            flat = u.reshape(-1, d)
            T = flat.shape[0]
            h = jax.nn.relu(jnp.einsum('td,ndf->ntf', flat, shared_w1) + shared_b1[:, None, :])
            shared_out = jnp.einsum('ntf,nfd->td', h, shared_w2) + shared_b2.sum(0)
            out = flat + shared_out
            scores = jax.nn.sigmoid(flat @ centroids.T) + bias
            vals, idx = jax.lax.top_k(scores, KR)
            gating = jnp.zeros_like(scores).at[jnp.arange(T)[:, None], idx].set(vals)
            gating = gating / jnp.clip(gating.sum(-1, keepdims=True), 1e-08)

            def step(acc, ew):
                w1, b1, w2, b2, g = ew
                hj = jax.nn.relu(flat @ w1 + b1)
                yj = hj @ w2 + b2
                return (acc + yj * g[:, None], None)
            rout0 = jnp.zeros_like(flat)
            rout, _ = jax.lax.scan(step, rout0, (routed_w1, routed_b1, routed_w2, routed_b2, gating.T))
            return (out + rout).reshape(b, s, d)
        return _moe_forward(u, shared_w1, shared_b1, shared_w2, shared_b2, routed_w1, routed_b1, routed_w2, routed_b2, centroids, bias)

    def _L1_xattn_ref(Z, kv, decay, W_in, b_in, W_out, b_out, gamma, beta):
        import jax, jax.numpy as jnp
        import numpy as np
        from jax import lax
        LN_EPS = 1e-05
        B, T, D = kv.shape
        K = jax.nn.sigmoid(decay)
        x = jnp.einsum('btd,ed->bte', kv, W_in) + b_in

        def scan_fn(s, xt):
            s = K * s + xt
            return (s, s)
        s0 = jnp.zeros((B, D), dtype=kv.dtype)
        _, states = lax.scan(scan_fn, s0, jnp.swapaxes(x, 0, 1))
        states = jnp.swapaxes(states, 0, 1)
        proj = jnp.einsum('btd,ed->bte', states, W_out) + b_out
        summary = jnp.mean(proj, axis=1, keepdims=True)
        y = Z + summary
        mu = jnp.mean(y, axis=-1, keepdims=True)
        var = jnp.mean((y - mu) ** 2, axis=-1, keepdims=True)
        return (y - mu) / jnp.sqrt(var + LN_EPS) * gamma + beta

    def _L1_ffn_ref(hidden_states, W_q, keys, down_embed, up_embed, gate_w, up_w, down_w):
        import jax, jax.numpy as jnp
        import numpy as np
        HIDDEN = 256
        INTER = 1024
        RETRIEVAL = 128
        NUM_EXPERTS = 512
        NUM_KEYS = 64
        TOP_K = 8
        B, S = (4, 256)
        b, s, h = hidden_states.shape
        n = b * s
        queries = (hidden_states @ W_q).reshape(2, n, RETRIEVAL // 2)
        routing = jnp.einsum('tnd,tdk->tnk', queries, keys)
        scores2, idx2 = jax.lax.top_k(routing, TOP_K)
        sx, sy = (scores2[0], scores2[1])
        ix, iy = (idx2[0], idx2[1])
        all_scores = (sx[:, :, None] + sy[:, None, :]).reshape(n, TOP_K * TOP_K)
        all_idx = (ix[:, :, None] * NUM_KEYS + iy[:, None, :]).reshape(n, TOP_K * TOP_K)
        scores, pk = jax.lax.top_k(all_scores, TOP_K)
        indices = jnp.take_along_axis(all_idx, pk, axis=-1)
        de = down_embed[indices]
        ue = up_embed[indices]
        x = hidden_states.reshape(n, h)
        ew = jnp.einsum('nh,nkh->nk', x, de)
        ew = jax.nn.silu(ew) * jax.nn.softmax(scores, axis=-1)
        experts_states = jnp.einsum('nk,nkh->nh', ew, ue).reshape(b, s, h)
        mlp = jax.nn.silu(x @ gate_w) * (x @ up_w) @ down_w
        return mlp.reshape(b, s, h) + experts_states
    x = x + _L0_xattn_ref(_layernorm(x, axis=-1), ctx_2048, mask_Bx1x2048_fk1, mask_Bx1x2048_fk1, L0_xattn_Wq, L0_xattn_bq, L0_xattn_Wk, L0_xattn_bk, L0_xattn_Wv, L0_xattn_bv)
    x = x + _L0_ffn_ref(_layernorm(x, axis=-1), L0_ffn_shared_w1, L0_ffn_shared_b1, L0_ffn_shared_w2, L0_ffn_shared_b2, L0_ffn_routed_w1, L0_ffn_routed_b1, L0_ffn_routed_w2, L0_ffn_routed_b2, L0_ffn_centroids, L0_ffn_bias)
    x = x + _L1_xattn_ref(_layernorm(x, axis=-1), ctx_2048, L1_xattn_decay, L1_xattn_W_in, L1_xattn_b_in, L1_xattn_W_out, L1_xattn_b_out, L1_xattn_gamma, L1_xattn_beta)
    x = x + _L1_ffn_ref(_layernorm(x, axis=-1), L1_ffn_W_q, L1_ffn_keys, L1_ffn_down_embed, L1_ffn_up_embed, L1_ffn_gate_w, L1_ffn_up_w, L1_ffn_down_w)
    return x

_drawn_inputs = setup_inputs


def setup_inputs(seed=0):
    import zlib

    import numpy as np

    out = dict(_drawn_inputs(seed))
    spreads = {'L0_ffn_shared_b1': (0.0, 0.1),
     'L0_ffn_shared_b2': (0.0, 0.1),
     'L0_ffn_routed_b1': (0.0, 0.551),
     'L0_ffn_routed_b2': (0.0, 0.377),
     'L0_ffn_bias': (0.0, 0.1),
     'L1_xattn_b_in': (0.0, 0.277),
     'L1_xattn_b_out': (0.0, 0.1),
     'L1_xattn_gamma': (1.0, 0.2),
     'L1_xattn_beta': (0.0, 0.267)}
    factors = {'L0_xattn_bq': 21.732,
     'L0_xattn_bk': 64.0,
     'L0_xattn_bv': 40.498,
     'L1_ffn_W_q': 52.606,
     'L1_ffn_keys': 42.623,
     'L1_ffn_down_embed': 8.0,
     'L1_ffn_up_embed': 8.0,
     'L1_ffn_gate_w': 5.594,
     'L1_ffn_up_w': 5.555,
     'L1_ffn_down_w': 5.563}
    for name, (base, spread) in spreads.items():
        noise = np.random.default_rng([zlib.crc32(name.encode()), seed]).standard_normal(out[name].shape)
        drawn = base * np.exp(spread * noise) if base else spread * noise
        out[name] = jnp.asarray(drawn.astype(out[name].dtype))
    for name, factor in factors.items():
        out[name] = (out[name] * factor).astype(out[name].dtype)
    return out
```

```python
from contextlib import ExitStack

import concourse.bass as bass
from concourse import mybir
from concourse.bass import ds

F32 = mybir.dt.float32
F16 = mybir.dt.float16
BF16 = mybir.dt.bfloat16
U32 = mybir.dt.uint32
ALU = mybir.AluOpType
ACT = mybir.ActivationFunctionType
AX = mybir.AxisListType

P = 128
NB = 16
D = 256
HEADS = 16
HD = P // HEADS
ST = D // P
EPS = 1e-5
NEG = 1e6 * HD ** 0.5

TERMS = ((0, 0), (0, 1), (0, 2), (1, 0), (1, 1), (2, 0))
MASK_ROW = 64
MAX_ROW = 65
ROWS = 68
STACK_DMAS = 2 * len(TERMS) + 1
RING = 4


def wait(eng, sem, value):
    if not (isinstance(value, int) and value <= 0):
        eng.wait_ge(sem, value)


def wait_alone(eng, sem, value, seen):
    wait(eng, sem, value)
    if not isinstance(value, int):
        eng.sem_inc(seen, 1)


class Sems:

    def __init__(self, ctx, nc, prefix):
        self._ctx, self._nc, self._prefix, self._made = ctx, nc, prefix, {}

    def __getitem__(self, name):
        if name not in self._made:
            self._made[name] = self._ctx.enter_context(self._nc.semaphore(f"{self._prefix}_{name}"))
        return self._made[name]


def setup_phase(nc, dram, t, scratch):
    with ExitStack() as ctx:
        s = Sems(ctx, nc, "setup")
        w_rows = ctx.enter_context(nc.sbuf_tensor("w_rows", [P, 3, P], F32))
        mask_rows = ctx.enter_context(nc.sbuf_tensor("mask_rows", [NB, D], F32))
        penalty = ctx.enter_context(nc.sbuf_tensor("penalty", [NB, D], BF16))
        stats = ctx.enter_context(nc.sbuf_tensor("stats", [P, NB, 6], F32))
        base = ctx.enter_context(nc.sbuf_tensor("base", [P, NB], F32))
        power = ctx.enter_context(nc.sbuf_tensor("power", [P, NB], F32))
        turned = ctx.enter_context(nc.psum_tensor("turned", [P, 3, P], F32))
        turned_mask = ctx.enter_context(nc.psum_tensor("turned_mask", [P, ST, NB], F32))
        names = ["x_in", "w_in", "mask_in", "other_in", "ident", "ident_zero", "w_turned", "w_copied",
                 "mask_turned", "mask_copied", "stats", "moments", "base", "rstd", "penalty", "penalty_out",
                 "clear", "ones"]
        for n in names:
            s[n]
        block = ctx.enter_context(nc.Block())

        @block.sync
        def _(sp):
            for i, name in enumerate(("L0_xattn_Wq", "L0_xattn_Wk", "L0_xattn_Wv")):
                sp.dma_start(w_rows[:, i, :], dram[name]).then_inc(s["w_in"], 16)
            sp.dma_start(mask_rows[:], dram["mask_Bx1x2048_fk1"].rearrange("b o t -> (b o) t")).then_inc(s["mask_in"], 16)
            sp.dma_start(t["x"][:], dram["x"].rearrange("b p d -> p b d")).then_inc(s["x_in"], 16)
            for i, name in enumerate(("L0_xattn_bq", "L0_xattn_bk")):
                sp.dma_start(t["b_qk"][:, i:i + 1], dram[name].rearrange("(p o) -> p o", o=1)).then_inc(s["other_in"], 16)
            sp.dma_start(t["bv_rows"][:], dram["L0_xattn_bv"].partition_broadcast(P)).then_inc(s["other_in"], 16)
            sp.dma_start(t["mask_all"][:], dram["mask_Bx1x2048_fk1"].rearrange("b o t -> b (o t)").partition_broadcast(P)).then_inc(s["other_in"], 16)
            sp.wait_ge(s["penalty"], 1)
            sp.dma_start(scratch["penalty"], penalty[:]).then_inc(s["penalty_out"], 16)
            sp.wait_ge(s["penalty_out"], 16)
            sp.wait_ge(s["x_in"], 16)
            sp.wait_ge(s["other_in"], 64)

        @block.gpsimd
        def _(pool):
            pool.memset(t["ident"][:], 0.0).then_inc(s["ident_zero"], 1)
            pool.memset(power[:], -0.5).then_inc(s["ident_zero"], 1)
            pool.wait_ge(s["ident_zero"], 2)
            pool.affine_select(out=t["ident"][:], in_=t["ident"][:], compare_op=ALU.not_equal, fill=1.0,
                               base=0, pattern=[[-1, P]], channel_multiplier=1).then_inc(s["ident"], 1)
            pool.wait_ge(s["base"], 1)
            pool.tensor_tensor(t["rstd"][:], base[:], power[:], ALU.pow).then_inc(s["rstd"], 1)

        @block.tensor
        def _(pe):
            pe.wait_ge(s["ident"], 1)
            pe.wait_ge(s["w_in"], 48)
            for i in range(3):
                turn = pe.transpose(turned[:, i, :], w_rows[:, i, :], t["ident"][:])
            turn.then_inc(s["w_turned"], 1)
            pe.wait_ge(s["mask_in"], 16)
            for h in range(ST):
                turn = pe.transpose(turned_mask[:, h, :], mask_rows[:, h * P:(h + 1) * P], t["ident"][0:NB, 0:NB])
            turn.then_inc(s["mask_turned"], 1)

        @block.scalar
        def _(act):
            act.wait_ge(s["w_turned"], 1)
            act.activation(t["w_qkv"][:], turned[:], ACT.Copy).then_inc(s["w_copied"], 1)
            act.wait_ge(s["mask_turned"], 1)
            act.activation(t["mask_cols"][:], turned_mask[:], ACT.Copy).then_inc(s["mask_copied"], 1)
            act.wait_ge(s["mask_copied"], 1)

        @block.vector
        def _(dve):
            dve.memset(t["stack"][32:64].bitcast(U32), 0)
            dve.memset(t["stack"][64:ROWS], 1.0)
            dve.memset(t["v_wide"][:], 0.0)
            dve.memset(t["ones_wide"][:], 0.0).then_inc(s["clear"], 1)
            dve.wait_ge(s["clear"], 1)
            for g in range(4):
                dve.memset(t["ones_wide"][:, g, g * HD:(g + 1) * HD], 1.0).then_inc(s["ones"], 1)
            dve.wait_ge(s["mask_in"], 16)
            dve.tensor_scalar(penalty[:], mask_rows[:], -1.0, NEG, ALU.add, ALU.mult).then_inc(s["penalty"], 1)
            dve.wait_ge(s["x_in"], 16)
            for b in range(NB):
                dve.bn_stats(stats[:, b, :], t["x"][:, b, :]).then_inc(s["stats"], 1)
            for b in range(NB):
                dve.wait_ge(s["stats"], b + 1)
                dve.bn_aggr(t["moments"][:, b, :], stats[:, b, :]).then_inc(s["moments"], 1)
            dve.wait_ge(s["moments"], NB)
            dve.tensor_scalar(base[:], t["moments"][:, :, 1], EPS, None, ALU.add).then_inc(s["base"], 1)
            dve.wait_ge(s["ones"], 4)


def attention_phase(nc, dram, t, scratch):
    LAST = NB - 1
    with ExitStack() as ctx:
        s = Sems(ctx, nc, "att")

        def sb(name, shape, dt):
            return ctx.enter_context(nc.sbuf_tensor(name, shape, dt))

        context = sb("context", [P, RING, D], F32)
        xn = sb("xn", [P, RING, D], F32)
        qk = sb("qk", [P, 2, D], F32)
        part = sb("part", [P, 3, 2, D], BF16)
        rest1 = sb("rest1", [P, 2, D], F32)
        v_rows = sb("v_rows", [P, ST, P], F32)
        neg_max = sb("neg_max", [P, 2, ST * HEADS], F32)
        max_part = sb("max_part", [ST * HEADS, 3, P], BF16)
        max_rest = sb("max_rest", [ST * HEADS, 2, P], F32)
        probs = sb("probs", [P, 2, 4, ST, D], F32)
        out_sums = sb("out_sums", [P, 2, D], F32)
        inverse = sb("inverse", [P, D], F32)
        ratio = sb("ratio", [P, D], F32)
        masked = sb("masked", [P, D], F32)
        stack, v_wide = t["stack"], t["v_wide"]

        def ps(name, shape):
            return ctx.enter_context(nc.psum_tensor(name, shape, F32))

        scores = ps("scores", [P, 2, 2 * D])
        scores_t = ps("scores_t", [P, 2, 2 * D])
        sums = ps("sums", [P, 2, 2 * D])
        ps_qk = ps("ps_qk", [P, 2, D])
        ps_v = ps("ps_v", [P, 2 * D])
        for n in ["ctx_in0", "ctx_in1", "ctx_in2", "ctx_in3", "xn", "qk_mm", "qk_evac", "rest1", "part1", "part2", "parts_out",
                  "stack_in", "v_mm", "v_bias", "v_done", "max_mm", "max_done", "max_turned", "max_cut",
                  "max_out", "max_in", "score_mm", "prob_mm", "exp", "av_done",
                  "sums_evac", "inverse", "ratio", "masked", "x1"]:
            s[n]
        block = ctx.enter_context(nc.Block())

        def on(n, j):
            return 0 <= n <= LAST if j is None else True

        def steps(eng, step):
            for k in range(-4, 4):
                step(k, k % RING, None)
            with eng.Fori(1, 3) as j:
                for r in range(RING):
                    step(j * RING + r, r, j)
            for k in range(12, 17):
                step(k, k % RING, None)

        def group(k, r, j, ahead):
            return (k + ahead) // RING if j is None else j + (r + ahead) // RING

        def head(u):
            return (u % 4) * 4 + u // 4

        @block.sync
        def _(sp):
            def step(k, r, j):
                n = k + 4
                if on(n, j):
                    if j is not None or k >= 0:
                        wait_alone(sp, s["v_mm"], k + 1, s["seen"])
                        wait_alone(sp, s["qk_mm"], k + 1, s["seen"])
                    sp.dma_start(context[:, r, :], dram["ctx_2048"][ds(n, 1)].rearrange("b c s -> (b c) s")).then_inc(s[f"ctx_in{r}"], 16)
                n = k + 1
                if on(n, j):
                    slot = (r + 1) % RING
                    wait_alone(sp, s["max_cut"], 4 * n + 4, s["seen"])
                    sp.dma_start(scratch["maxima"].rearrange("a h s t -> h s a t")[:, 0], max_part[0:HEADS]).then_inc(s["max_out"], 16)
                    sp.dma_start(scratch["maxima"].rearrange("a h s t -> h s a t")[:, 1], max_part[HEADS:2 * HEADS]).then_inc(s["max_out"], 16)
                    wait_alone(sp, s["max_out"], 32 * (n + 1), s["seen"])
                    sp.dma_start(stack[MAX_ROW:MAX_ROW + 3, slot, 0],
                                 scratch["maxima"].rearrange("a h s t -> a h (s t)")).then_inc(s["max_in"], 16)
                    wait_alone(sp, s["max_in"], 16 * (n + 1), s["seen"])

                n = k + 3
                if on(n, j):
                    slot = (r + 3) % RING
                    wait_alone(sp, s["part2"], n + 1, s["seen"])
                    wait_alone(sp, s["stack_in"], STACK_DMAS * 16 * n, s["seen"])
                    sp.dma_start(scratch["parts"].rearrange("h d a e t -> (h d) a e t"), part[:]).then_inc(s["parts_out"], 16)
                    wait_alone(sp, s["parts_out"], 16 * n + 16, s["seen"])
                    if j is not None or n >= RING:
                        wait_alone(sp, s["prob_mm"], 16 * (n - RING) + 16, s["seen"])
                    for i, (a, b) in enumerate(TERMS):
                        for e, which in ((0, a), (1, b)):
                            sp.dma_start(stack[i * HD:(i + 1) * HD, slot, e],
                                         scratch["parts"][:, :, which, e].rearrange("h d t -> d h t")).then_inc(s["stack_in"], 16)
                    sp.dma_start(stack[MASK_ROW:MASK_ROW + 1, slot, 1],
                                 scratch["penalty"][ds(n, 1)].unsqueeze(1).broadcast_to([1, HEADS, D])).then_inc(s["stack_in"], 16)

            steps(sp, step)

        @block.tensor
        def _(pe):
            def values(u0, n, r):
                g = u0 // 4
                wait(pe, s["exp"], 16 * n + u0 + 4)
                if g == 0:
                    wait(pe, s["sums_evac"], n)
                    wait(pe, s["v_done"], n + 1)
                for which, lhs in ((0, None), (1, t["ones_wide"])):
                    for st in range(ST):
                        for q in range(4):
                            h = q * 4 + g
                            w = v_wide[:, r, st, h, :] if lhs is None else lhs[:, g, :]
                            mm = pe.matmul(sums[32 * q:32 * q + 32, which, 0:D], w, probs[:, g % 2, q, st, :],
                                           start=(g == 0 and st == 0), stop=(g == 3 and st == ST - 1))
                mm.then_inc(s["av_done"], 1)

            def step(k, r, j):
                n = k + 3
                if on(n, j):
                    wait(pe, s["xn"], n + 1)
                    slot = (r + 3) % RING
                    wait(pe, s[f"ctx_in{slot}"], 16 * (group(k, r, j, 3) + 1))
                    wait(pe, s["qk_evac"], n)
                    pe.matmul(ps_qk[:, 0, :], t["w_qkv"][:, 0, :], xn[:, slot, :], start=True, stop=True)
                    pe.matmul(ps_qk[:, 1, :], t["w_qkv"][:, 1, :], context[:, slot, :], start=True, stop=True).then_inc(s["qk_mm"], 1)
                for u in range(HEADS):
                    h = head(u)
                    n = k + 2
                    if on(n, j):
                        if u == 0:
                            wait(pe, s["stack_in"], STACK_DMAS * 16 * (n + 1))
                        wait(pe, s["max_done"], 16 * n + u - 1)
                        slot = (r + 2) % RING
                        for tt in range(ST):
                            mm = pe.matmul(scores[:, u % 2, tt * D:(tt + 1) * D],
                                           stack[0:MASK_ROW + 1, slot, 0, h, tt * P:(tt + 1) * P],
                                           stack[0:MASK_ROW + 1, slot, 1, h, :], start=True, stop=True)
                        mm.then_inc(s["score_mm"], 1)
                    n = k
                    if on(n, j):
                        if u == 0:
                            wait(pe, s["max_in"], 16 * (n + 1))
                        wait(pe, s["exp"], 16 * n + u - 1)
                        for st in range(ST):
                            mm = pe.matmul(scores_t[:, u % 2, st * D:(st + 1) * D],
                                           stack[0:ROWS, r, 1, h, st * P:(st + 1) * P],
                                           stack[0:ROWS, r, 0, h, :], start=True, stop=True)
                        mm.then_inc(s["prob_mm"], 1)
                        if u % 4 == 1 and u > 4:
                            values(u - 5, n, r)
                    n = k - 1
                    if on(n, j) and u == 1:
                        values(12, n, (r + 3) % RING)
                    n = k + 1
                    if on(n, j) and u == 1:
                        wait(pe, s["max_done"], 16 * (n + 1))
                        wait(pe, s["v_done"], n)
                        pe.transpose(ps_v[0:ST * HEADS, 256:256 + P], neg_max[:, (r + 1) % 2, :], t["ident"][:]).then_inc(s["max_turned"], 1)
                    if on(n, j) and u == 5:
                        wait(pe, s["max_cut"], 4 * n + 2)
                        for st in range(ST):
                            mm = pe.matmul(ps_v[:, st * P:(st + 1) * P], context[:, (r + 1) % RING, st * P:(st + 1) * P],
                                           t["w_qkv"][:, 2, :], start=True, stop=True)
                        mm.then_inc(s["v_mm"], 1)

            steps(pe, step)

        @block.scalar
        def _(act):
            def step(k, r, j):
                for u in range(HEADS):
                    n = k + 3
                    if u == 1 and on(n, j):
                        wait(act, s["qk_mm"], n + 1)
                        wait(act, s["parts_out"], 16 * n)
                        wait(act, s["rest1"], n)
                        for e in range(2):
                            act.activation(qk[:, e, :], ps_qk[:, e, :], ACT.Identity, bias=t["b_qk"][:, e:e + 1])
                            mm = act.activation(part[:, 0, e, :], ps_qk[:, e, :], ACT.Identity, bias=t["b_qk"][:, e:e + 1])
                        mm.then_inc(s["qk_evac"], 1)
                    n = k
                    if on(n, j):
                        wait(act, s["prob_mm"], 16 * n + u + 1)
                        if u % 4 == 0:
                            wait(act, s["av_done"], 4 * n + u // 4 - 1)
                        act.activation(probs[:, (u // 4) % 2, u % 4], scores_t[:, u % 2, :].rearrange("p (s t) -> p s t", s=ST),
                                       ACT.Exp, scale=HD ** -0.5).then_inc(s["exp"], 1)
                    n = k - 1
                    if u == 3 and on(n, j):
                        wait(act, s["av_done"], 4 * n + 4)
                        wait(act, s["ratio"], n)
                        act.activation(out_sums[:], sums[:, :, 0:D], ACT.Copy).then_inc(s["sums_evac"], 1)

            steps(act, step)

        @block.vector
        def _(dve):
            def step(k, r, j):
                for u in range(HEADS):
                    n = k + 2
                    if on(n, j):
                        wait(dve, s["score_mm"], 16 * n + u + 1)
                        if u == 0:
                            wait(dve, s["max_turned"], n - 1)
                        h = head(u)
                        dve.tensor_reduce(neg_max[:, r % 2, h::HEADS],
                                          scores[:, u % 2, :].rearrange("p (s t) -> p s t", s=ST),
                                          AX.X, ALU.max, negate=True).then_inc(s["max_done"], 1)
                    n = k + 1
                    if on(n, j) and u == 2:
                        turned = ps_v[0:ST * HEADS, 256:256 + P]
                        wait(dve, s["max_turned"], n + 1)
                        wait(dve, s["max_out"], 32 * n)
                        dve.tensor_copy(max_part[:, 0, :], turned).then_inc(s["max_cut"], 1)
                        wait(dve, s["max_cut"], 4 * n + 1)
                        dve.tensor_tensor(max_rest[:, 0, :], turned, max_part[:, 0, :], ALU.subtract).then_inc(s["max_cut"], 1)
                        wait(dve, s["max_cut"], 4 * n + 2)
                        dve.tensor_copy(max_part[:, 1, :], max_rest[:, 0, :]).then_inc(s["max_cut"], 1)
                        wait(dve, s["max_cut"], 4 * n + 3)
                        dve.tensor_tensor(max_part[:, 2, :], max_rest[:, 0, :], max_part[:, 1, :], ALU.subtract).then_inc(s["max_cut"], 1)
                    n = k + 3
                    if on(n, j) and u == 3:
                        wait(dve, s["qk_evac"], n + 1)
                        wait(dve, s["part2"], n)
                        dve.tensor_tensor(rest1[:], qk[:], part[:, 0], ALU.subtract).then_inc(s["rest1"], 1)
                        wait(dve, s["rest1"], n + 1)
                        wait(dve, s["parts_out"], 16 * n)
                        dve.tensor_copy(part[:, 1], rest1[:]).then_inc(s["part1"], 1)
                    n = k + 1
                    if on(n, j) and u == 8:
                        slot = (r + 1) % RING
                        wait(dve, s["v_mm"], n + 1)
                        wait(dve, s["v_done"], n)
                        dve.tensor_tensor(v_rows[:], ps_v[:, 0:2 * P].rearrange("p (s c) -> p s c", s=ST),
                                          t["bv_rows"][:].unsqueeze(1).broadcast_to([P, ST, P]), ALU.add).then_inc(s["v_bias"], 1)
                        wait(dve, s["v_bias"], n + 1)
                        if j is not None or n >= RING:
                            wait(dve, s["av_done"], 4 * (n - RING) + 4)
                        for st in range(ST):
                            for q in range(4):
                                src = v_rows[:, st, :].rearrange("p (a q d) -> p a q d", q=4, d=HD)[:, :, q, :]
                                dst = v_wide[:, slot, st, q::4, q * HD:(q + 1) * HD]
                                mm = dve.tensor_scalar(dst, src, t["mask_cols"][:, st, ds(n, 1)], None, ALU.mult)
                        mm.then_inc(s["v_done"], 1)
                    n = k + 4
                    if on(n, j) and u == 10:
                        if j is not None or n >= RING:
                            wait(dve, s["qk_mm"], n - RING + 1)
                        dve.tensor_scalar(xn[:, r, :], t["x"][:, ds(n, 1), :].rearrange("p o d -> p (o d)"),
                                          t["moments"][:, ds(n, 1), 0], t["rstd"][:, ds(n, 1)], ALU.subtract, ALU.mult).then_inc(s["xn"], 1)
                    n = k - 1
                    if on(n, j) and u == 12:
                        wait(dve, s["sums_evac"], n + 1)
                        wait(dve, s["ratio"], n)
                        dve.reciprocal(inverse[:], out_sums[:, 1, :]).then_inc(s["inverse"], 1)
                        wait(dve, s["inverse"], n + 1)
                        wait(dve, s["masked"], n)
                        dve.tensor_tensor(ratio[:], out_sums[:, 0, :], inverse[:], ALU.mult).then_inc(s["ratio"], 1)

            steps(dve, step)

        @block.gpsimd
        def _(pool):
            def step(k, r, j):
                n = k + 3
                if on(n, j):
                    wait(pool, s["part1"], n + 1)
                    wait(pool, s["parts_out"], 16 * n)
                    pool.tensor_tensor(part[:, 2], rest1[:], part[:, 1], ALU.subtract).then_inc(s["part2"], 1)
                n = k - 1
                if on(n, j):
                    wait(pool, s["ratio"], n + 1)
                    wait(pool, s["x1"], n)
                    pool.tensor_tensor(masked[:], ratio[:], t["mask_all"][:, ds(n, 1), :].rearrange("p o d -> p (o d)"), ALU.mult).then_inc(s["masked"], 1)
                    wait(pool, s["masked"], n + 1)
                    x = t["x"][:, ds(n, 1), :].rearrange("p o d -> p (o d)")
                    pool.tensor_tensor(x, x, masked[:], ALU.add).then_inc(s["x1"], 1)

            steps(pool, step)


def lasting_tensors(ctx, nc):
    def sb(name, shape, dt=F32):
        return ctx.enter_context(nc.sbuf_tensor(name, shape, dt))

    return {
        "x": sb("x", [P, NB, D]),
        "ident": sb("ident", [P, P]),
        "moments": sb("moments", [P, NB, 2]),
        "rstd": sb("rstd", [P, NB]),
    }


def attention_tensors(ctx, nc):
    def sb(name, shape, dt=F32):
        return ctx.enter_context(nc.sbuf_tensor(name, shape, dt))

    return {
        "b_qk": sb("b_qk", [P, 2]),
        "bv_rows": sb("bv_rows", [P, P]),
        "mask_all": sb("mask_all", [P, NB, D]),
        "mask_cols": sb("mask_cols", [P, ST, NB]),
        "w_qkv": sb("w_qkv", [P, 3, P]),
        "stack": sb("stack", [ROWS, RING, 2, HEADS, D], BF16),
        "v_wide": sb("v_wide", [P, RING, ST, HEADS, 32]),
        "ones_wide": sb("ones_wide", [P, 4, 32]),
    }


def scratch_tensors(nc):
    def room(name, shape, dt):
        return nc.dram_tensor(name, shape, dt, kind="Internal").ap()

    return {
        "penalty": room("penalty_rows", [NB, D], BF16),
        "parts": room("parts_room", [HEADS, HD, 3, 2, D], BF16),
        "maxima": room("maxima_room", [3, HEADS, ST, P], BF16),
        "summary": room("summary_room", [NB, D], F32),
    }


HIGH_LOW = ((0, 0), (0, 1), (1, 0))
UP = 64.0
DOWN = 1.0 / UP
C = D // P
CHUNK = 512
TOKENS = NB * P
CHUNKS = TOKENS // CHUNK
TILES = CHUNK // P
EXPERTS, SHARED, FF = 16, 2, 176
ROUTED_K = EXPERTS * FF // P
SHARED_F = SHARED * FF
SHARED_M = (P, P, SHARED_F - 2 * P)
TOP = 4
INTER = 1024
INTER_K = INTER // P
TABLE = 512
TABLE_K = TABLE // P
KEYS = 64
KDIM = 64


def weight_tensors(ctx, nc):
    def sb(name, shape, dt=F16):
        return ctx.enter_context(nc.sbuf_tensor(name, shape, dt))

    return {
        "w1": sb("w1", [P, 2, C, ROUTED_K * P]),
        "w2": sb("w2", [P, 2, ROUTED_K * D]),
        "ws1": sb("ws1", [P, 2, C, SHARED_F]),
        "ws2": sb("ws2", [P, 2, 3, D]),
        "gate": sb("gate", [P, 2, C, INTER]),
        "up": sb("up", [P, 2, C, INTER]),
        "down": sb("down", [P, 2, INTER_K * D]),
        "table_down": sb("table_down", [P, 2, C, TABLE]),
        "table_up": sb("table_up", [P, 2, TABLE_K, D]),
        "centroids": sb("centroids", [P, 2, C, EXPERTS]),
        "query": sb("query", [P, 2, C, 2, P]),
        "keys": sb("keys", [P, 2, 2, KEYS]),
        "b2": sb("b2", [P, 2, D]),
        "b1": sb("b1", [P, ROUTED_K], F32),
        "bs1": sb("bs1", [P, 3], F32),
        "bs2": sb("bs2", [P, 2, D], F32),
        "router_bias": sb("router_bias", [P, EXPERTS], F32),
        "gamma": sb("gamma", [P, D], F32),
        "beta": sb("beta", [P, D], F32),
    }


def weights_phase(nc, dram, t, w):
    ROOM = ROUTED_K * D
    with ExitStack() as ctx:
        s = Sems(ctx, nc, "weights")
        stage = [ctx.enter_context(nc.sbuf_tensor(f"stage{i}", [P, ROOM if i < 2 else C * SHARED_F + 3 * D], F32)) for i in range(3)]
        small = ctx.enter_context(nc.sbuf_tensor("small", [P, C * 2 * P + 2 * KEYS + D], F32))
        rows = ctx.enter_context(nc.sbuf_tensor("rows", [P, TABLE_K + 1, D], F32))
        turned = ctx.enter_context(nc.psum_tensor("turned_table", [P, C, TABLE], F32))
        turned_c = ctx.enter_context(nc.psum_tensor("turned_centroids", [P, C, EXPERTS], F32))
        for n in ["small_in", "rows_in", "turned", "high", "low"] + [f"in{i}" for i in range(3)]:
            s[n]

        def flat(name):
            return dram[name]

        loads = []
        v = stage[0][:, 0:C * EXPERTS * FF].rearrange("p (c e f) -> p c e f", c=C, e=EXPERTS)
        src = dram["L0_ffn_routed_w1"].rearrange("e (p c) f -> c p e f", c=C)
        loads.append(([(v[:, c], src[c]) for c in range(C)],
                      [(v[:, c].rearrange("p e f -> p (e f)").rearrange("p (q i) -> p q i", i=ROUTED_K),
                        [w["w1"][:, a, c].rearrange("p (i q) -> p q i", i=ROUTED_K) for a in range(2)]) for c in range(C)]))
        v = stage[1][:]
        loads.append(([(v, dram["L0_ffn_routed_w2"].rearrange("e f d -> (e f) d").rearrange("(p i) d -> p (i d)", p=P))],
                      [(v, [w["w2"][:, a] for a in range(2)])]))
        v = stage[2][:, 0:C * SHARED_F].rearrange("p (c n f) -> p c n f", c=C, n=SHARED)
        src = dram["L0_ffn_shared_w1"].rearrange("n (p c) f -> c p n f", c=C)
        v2 = stage[2][:, C * SHARED_F:C * SHARED_F + 3 * D].rearrange("p (k d) -> p k d", k=3)
        s2 = dram["L0_ffn_shared_w2"].rearrange("n f d -> (n f) d")
        loads.append(([(v[:, c], src[c]) for c in range(C)]
                      + [(v2[:, 0:2], s2[0:2 * P].rearrange("(k p) d -> p k d", p=P)), (v2[0:SHARED_M[2], 2], s2[2 * P:SHARED_F])],
                      [(v.rearrange("p c n f -> p (c n f)"), [w["ws1"][:, a].rearrange("p c f -> p (c f)") for a in range(2)]),
                       (v2[:, 0:2], [w["ws2"][:, a, 0:2] for a in range(2)]),
                       (v2[0:SHARED_M[2], 2], [w["ws2"][0:SHARED_M[2], a, 2] for a in range(2)])]))
        moves, cuts = [], []
        for k, name in enumerate(("gate", "up")):
            v = stage[0][:, k * C * INTER:(k + 1) * C * INTER]
            moves.append((v, dram[f"L1_ffn_{name}_w"].rearrange("(p c) f -> p (c f)", c=C)))
            v = v.rearrange("p (c q i) -> p c q i", c=C, i=INTER_K)
            cuts += [(v[:, c], [w[name][:, a, c].rearrange("p (i q) -> p q i", i=INTER_K) for a in range(2)]) for c in range(C)]
        loads.append((moves, cuts))
        v = stage[1][:, 0:INTER_K * D]
        v2 = stage[1][:, INTER_K * D:INTER_K * D + TABLE_K * D].rearrange("p (k d) -> p k d", d=D)
        loads.append(([(v, dram["L1_ffn_down_w"].rearrange("(p i) d -> p (i d)", p=P)),
                       (v2, dram["L1_ffn_up_embed"].rearrange("(k p) d -> p k d", p=P))],
                      [(v, [w["down"][:, a] for a in range(2)]), (v2, [w["table_up"][:, a] for a in range(2)])]))
        q = small[:, 0:C * 2 * P].rearrange("p (c r m) -> p c r m", c=C, r=2)
        ky = small[:, C * 2 * P:C * 2 * P + 2 * KEYS].rearrange("p (s k) -> p s k", s=2)
        b2 = small[:, C * 2 * P + 2 * KEYS:]
        small_moves = []
        for c in range(C):
            for half in range(2):
                small_moves.append((q[:, c, :, half * KDIM:(half + 1) * KDIM],
                                    dram["L1_ffn_W_q"].rearrange("(p c) (r m) -> c p r m", c=C, r=2)[c]))
        for half in range(2):
            small_moves.append((ky[half * KDIM:(half + 1) * KDIM], dram["L1_ffn_keys"].rearrange("s k n -> k s n")))
        small_moves.append((b2, dram["L0_ffn_routed_b2"].unsqueeze(1).broadcast_to([EXPERTS, P // EXPERTS, D])))
        small_moves += [
            (w["b1"][:], dram["L0_ffn_routed_b1"].rearrange("e f -> (e f)").rearrange("(p i) -> p i", p=P)),
            (w["bs2"][:], dram["L0_ffn_shared_b2"].partition_broadcast(P)),
            (w["router_bias"][:], dram["L0_ffn_bias"].partition_broadcast(P)),
            (w["gamma"][:], dram["L1_xattn_gamma"].partition_broadcast(P)),
            (w["beta"][:], dram["L1_xattn_beta"].partition_broadcast(P)),
        ]
        bs1 = dram["L0_ffn_shared_b1"].rearrange("n f -> (n f)")
        for k, m in enumerate(SHARED_M):
            small_moves.append((w["bs1"][0:m, k:k + 1], bs1[k * P:k * P + m].rearrange("(p o) -> p o", o=1)))
        small_cuts = [(small[:, 0:C * 2 * P], [w["query"][:, a].rearrange("p c r m -> p (c r m)") for a in range(2)], UP),
                      (ky, [w["keys"][:, a] for a in range(2)], UP),
                      (b2, [w["b2"][:, a] for a in range(2)], UP * EXPERTS / P)]
        turned_cuts = [(turned[:, c], [w["table_down"][:, a, c] for a in range(2)], UP) for c in range(C)]
        turned_cuts += [(turned_c[:], [w["centroids"][:, a] for a in range(2)], UP)]
        order = [((f"in{n % 3}", 16 * len(moves) + (16 * len(loads[n - 3][0]) if n >= 3 else 0)), cut + (UP,), n)
                 for n, (moves, cuts) in enumerate(loads) for cut in cuts]
        order += [(("small_in", 16 * len(small_moves)), cut, None) for cut in small_cuts]
        order += [(("turned", 1), cut, None) for cut in turned_cuts]
        last_of = {n: i + 1 for i, (_, _, n) in enumerate(order)}
        block = ctx.enter_context(nc.Block())

        @block.sync
        def _(sp):
            for n, (moves, _) in enumerate(loads):
                if n >= 3:
                    sp.wait_ge(s["low"], last_of[n - 3])
                for dst, src in moves:
                    sp.dma_start(dst, src).then_inc(s[f"in{n % 3}"], 16)
                if n == 2:
                    sp.dma_start(rows[:, 0:TABLE_K], dram["L1_ffn_down_embed"].rearrange("(k p) d -> p k d", p=P)).then_inc(s["rows_in"], 16)
                    sp.dma_start(rows[0:EXPERTS, TABLE_K], dram["L0_ffn_centroids"]).then_inc(s["rows_in"], 16)
                    for dst, src in small_moves:
                        sp.dma_start(dst, src).then_inc(s["small_in"], 16)

        @block.tensor
        def _(pe):
            pe.wait_ge(s["rows_in"], 32)
            for c in range(C):
                for k in range(TABLE_K):
                    pe.transpose(turned[:, c, k * P:(k + 1) * P], rows[:, k, c::C], t["ident"][:])
            for c in range(C):
                turn = pe.transpose(turned_c[:, c, :], rows[0:EXPERTS, TABLE_K, c::C], t["ident"][0:EXPERTS, 0:EXPERTS])
            turn.then_inc(s["turned"], 1)

        @block.scalar
        def _(act):
            for (name, count), (src, dst, scale), n in order:
                act.wait_ge(s[name], count)
                act.activation(dst[0], src, ACT.Copy, scale=scale).then_inc(s["high"], 1)

        @block.vector
        def _(dve):
            for i, ((name, count), (src, dst, scale), n) in enumerate(order):
                dve.wait_ge(s["high"], i + 1)
                dve.scalar_tensor_tensor(out=dst[1], in0=src, scalar=scale, in1=dst[0],
                                         op0=ALU.mult, op1=ALU.subtract).then_inc(s["low"], 1)
            dve.wait_ge(s["low"], len(order))


def summary_phase(nc, dram, t, scratch, sums_all):
    with ExitStack() as ctx:
        s = Sems(ctx, nc, "sum")

        def sb(name, shape, dt=F32):
            return ctx.enter_context(nc.sbuf_tensor(name, shape, dt))

        context = sb("context2", [P, NB, D])
        decay = sb("decay", [P, 1])
        keep = sb("keep", [P, 8])
        runs = sb("runs", [P, P])
        anti = sb("anti", [P, P])
        picked = sb("picked", [P, P])
        weight = sb("weight", [P, 1])
        total = sb("total", [1, 2])
        spread = sb("spread", [P, NB, NB])
        w_rows = sb("w_rows2", [P, 2, C, D])
        w_cols = sb("w_cols2", [P, 2, C, D])
        biases = sb("biases", [1, 2, D])
        factors = sb("factors", [1, 2, NB])
        mean = sb("mean", [NB, 3, D])
        mean_t = sb("mean_t", [P, 2, C, NB])
        ps_w = ctx.enter_context(nc.psum_tensor("ps_w", [P, 2, C, D], F32))
        ps_m = ctx.enter_context(nc.psum_tensor("ps_m", [NB, 3, 2 * D], F32))
        ps_t = ctx.enter_context(nc.psum_tensor("ps_t", [P, 2, 2 * D], F32))
        for n in ["decay_in", "ctx_in", "w_in", "b_in", "zero", "anti", "keep", "runs", "picked", "weight", "spread",
                  "total", "factors", "w_turned", "w_cols", "mean", "mean_sb", "turned", "turned_sb", "out", "keep_s"]:
            s[n]
        block = ctx.enter_context(nc.Block())

        @block.sync
        def _(sp):
            sp.dma_start(decay[:], dram["L1_xattn_decay"].partition_broadcast(P)).then_inc(s["decay_in"], 16)
            for i, name in enumerate(("L1_xattn_W_in", "L1_xattn_W_out")):
                sp.dma_start(w_rows[:, i], dram[name].rearrange("(k p) d -> p k d", p=P)).then_inc(s["w_in"], 16)
            for i, name in enumerate(("L1_xattn_b_in", "L1_xattn_b_out")):
                sp.dma_start(biases[:, i, :], dram[name].rearrange("(o d) -> o d", o=1)).then_inc(s["b_in"], 16)
            sp.dma_start(context[:], dram["ctx_2048"].rearrange("b p d -> p b d")).then_inc(s["ctx_in"], 16)
            sp.wait_ge(s["mean_sb"], 3)
            sp.dma_start(scratch["summary"], mean[:, 2, :]).then_inc(s["out"], 16)
            sp.wait_ge(s["out"], 16)
            sp.dma_start(sums_all[:], scratch["summary"].partition_broadcast(P)).then_inc(s["out"], 16)
            sp.wait_ge(s["out"], 32)

        @block.gpsimd
        def _(pool):
            pool.memset(anti[:], 0.0).then_inc(s["zero"], 1)
            pool.wait_ge(s["zero"], 1)
            pool.affine_select(out=anti[:], in_=anti[:], compare_op=ALU.not_equal, fill=1.0 / P,
                               base=-(P - 1), pattern=[[1, P]], channel_multiplier=1).then_inc(s["anti"], 1)

        @block.scalar
        def _(act):
            act.wait_ge(s["decay_in"], 16)
            act.activation(keep[:, 0:1], decay[:], ACT.Sigmoid).then_inc(s["keep_s"], 1)
            act.wait_ge(s["w_turned"], 1)
            act.activation(w_cols[:], ps_w[:], ACT.Copy).then_inc(s["w_cols"], 1)

        @block.vector
        def _(dve):
            dve.memset(spread[:], 0.0).then_inc(s["spread"], 1)
            dve.memset(runs[:, 0:1], 1.0).then_inc(s["runs"], 1)
            dve.memset(factors[:, 1, :], 1.0).then_inc(s["factors"], 1)
            dve.wait_ge(s["keep_s"], 1)
            n = 1
            for i in range(7):
                dve.wait_ge(s["runs"], i + 1)
                if i:
                    dve.wait_ge(s["keep"], i)
                dve.tensor_scalar(runs[:, n:2 * n], runs[:, 0:n], keep[:, i:i + 1], runs[:, n - 1:n],
                                  ALU.mult, ALU.add).then_inc(s["runs"], 1)
                dve.tensor_tensor(keep[:, i + 1:i + 2], keep[:, i:i + 1], keep[:, i:i + 1], ALU.mult).then_inc(s["keep"], 1)
                n *= 2
            dve.wait_ge(s["runs"], 8)
            dve.wait_ge(s["anti"], 1)
            dve.tensor_tensor(picked[:], runs[:], anti[:], ALU.mult).then_inc(s["picked"], 1)
            dve.wait_ge(s["picked"], 1)
            dve.tensor_reduce(weight[:], picked[:], AX.X, ALU.add).then_inc(s["weight"], 1)
            dve.tensor_reduce(total[:, 0:1], runs[0:1, :], AX.X, ALU.add).then_inc(s["total"], 1)
            dve.wait_ge(s["weight"], 1)
            dve.wait_ge(s["spread"], 1)
            for b in range(NB):
                dve.tensor_copy(spread[:, b, b:b + 1], weight[:]).then_inc(s["spread"], 1)
            dve.wait_ge(s["total"], 1)
            dve.wait_ge(s["factors"], 1)
            dve.tensor_scalar(factors[:, 0, :], factors[:, 1, :], total[:, 0:1], 1.0 / P, ALU.mult, ALU.mult).then_inc(s["factors"], 1)
            for i in range(3):
                dve.wait_ge(s["mean"], i + 1)
                dve.tensor_copy(mean[:, i, :], ps_m[:, i, 0:D]).then_inc(s["mean_sb"], 1)
                if i < 2:
                    dve.wait_ge(s["turned"], i + 1)
                    dve.tensor_copy(mean_t[:, i], ps_t[:, i, 0:C * NB].rearrange("p (c b) -> p c b", c=C)).then_inc(s["turned_sb"], 1)

        @block.tensor
        def _(pe):
            pe.wait_ge(s["w_in"], 32)
            for i in range(2):
                for k in range(C):
                    for c in range(C):
                        turn = pe.transpose(ps_w[:, i, c, k * P:(k + 1) * P], w_rows[:, i, k, c * P:(c + 1) * P], t["ident"][:])
            turn.then_inc(s["w_turned"], 1)
            pe.wait_ge(s["ctx_in"], 16)
            pe.wait_ge(s["spread"], 1 + NB)
            for b in range(NB):
                mm = pe.matmul(ps_m[:, 0, 0:D], spread[:, b, :], context[:, b, :], start=(b == 0), stop=(b == NB - 1))
            mm.then_inc(s["mean"], 1)
            pe.wait_ge(s["w_cols"], 1)
            pe.wait_ge(s["b_in"], 32)
            pe.wait_ge(s["factors"], 2)
            for i in range(2):
                pe.wait_ge(s["mean_sb"], i + 1)
                for c in range(C):
                    turn = pe.transpose(ps_t[:, i, c * NB:(c + 1) * NB], mean[:, i, c * P:(c + 1) * P], t["ident"][0:NB, 0:NB])
                turn.then_inc(s["turned"], 1)
                pe.wait_ge(s["turned_sb"], i + 1)
                for c in range(C):
                    pe.matmul(ps_m[:, i + 1, 0:D], mean_t[:, i, c, :], w_cols[:, i, c, :], start=(c == 0), stop=False)
                pe.matmul(ps_m[:, i + 1, 0:D], factors[:, i, :], biases[:, i, :], start=False, stop=True).then_inc(s["mean"], 1)


def norm_phase(nc, t, s, call):
    done = call * NB
    with ExitStack() as ctx:
        stats = ctx.enter_context(nc.sbuf_tensor(f"stats{call}", [P, NB, 6], F32))
        base = ctx.enter_context(nc.sbuf_tensor(f"base{call}", [P, NB], F32))
        power = ctx.enter_context(nc.sbuf_tensor(f"power{call}", [P, NB], F32))
        block = ctx.enter_context(nc.Block())

        @block.gpsimd
        def _(pool):
            pool.memset(power[:], -0.5).then_inc(s["power"], 1)
            pool.wait_ge(s["power"], call + 1)
            pool.wait_ge(s["base"], call + 1)
            pool.tensor_tensor(t["rstd"][:], base[:], power[:], ALU.pow).then_inc(s["rstd"], 1)

        @block.vector
        def _(dve):
            for b in range(NB):
                dve.bn_stats(stats[:, b, :], t["x"][:, b, :]).then_inc(s["stats"], 1)
            for b in range(NB):
                dve.wait_ge(s["stats"], done + b + 1)
                dve.bn_aggr(t["moments"][:, b, :], stats[:, b, :]).then_inc(s["moments"], 1)
            dve.wait_ge(s["moments"], done + NB)
            dve.tensor_scalar(base[:], t["moments"][:, :, 1], EPS, None, ALU.add).then_inc(s["base"], 1)
            dve.wait_ge(s["rstd"], call + 1)


def turn_phase(nc, t, w, x_t, s, call, router=None):
    done = call * NB
    with ExitStack() as ctx:
        normed = ctx.enter_context(nc.sbuf_tensor(f"normed{call}", [P, 2, D], F32))
        bias = ctx.enter_context(nc.sbuf_tensor(f"bias{call}", [P, D], F32))
        turned = ctx.enter_context(nc.psum_tensor(f"turned{call}", [P, 2, C, D], F32))
        block = ctx.enter_context(nc.Block())

        @block.vector
        def _(dve):
            if router is not None:
                dve.tensor_tensor(bias[:], w["bs2"][:, 0], w["bs2"][:, 1], ALU.add).then_inc(s["bias"], 1)
            for b in range(NB + 1):
                if b < NB:
                    if b >= 2:
                        dve.wait_ge(s["turned"], done + b - 1)
                    if router is not None:
                        wait(dve, s["based"], b - 1)
                    dve.tensor_scalar(normed[:, b % 2], t["x"][:, b, :], t["moments"][:, b, 0:1], t["rstd"][:, b:b + 1],
                                      ALU.subtract, ALU.mult).then_inc(s["normed"], 1)
                if b > 0:
                    n = b - 1
                    dve.wait_ge(s["high"], done + n + 1)
                    dve.tensor_tensor(x_t[:, 1, :, n * P:(n + 1) * P], turned[:, n % 2, :, 0:P],
                                      x_t[:, 0, :, n * P:(n + 1) * P], ALU.subtract).then_inc(s["low"], 1)
            dve.wait_ge(s["low"], done + NB)

        @block.scalar
        def _(act):
            for b in range(NB):
                act.wait_ge(s["turned"], done + b + 1)
                act.activation(x_t[:, 0, :, b * P:(b + 1) * P], turned[:, b % 2, :, 0:P], ACT.Copy).then_inc(s["high"], 1)

        @block.gpsimd
        def _(pool):
            if router is not None:
                pool.wait_ge(s["bias"], 1)
                for b in range(NB):
                    pool.wait_ge(s["normed"], b + 1)
                    pool.tensor_tensor(t["x"][:, b, :], t["x"][:, b, :], bias[:], ALU.add).then_inc(s["biased"], 1)
                    pool.wait_ge(s["biased"], b + 1)
                    pool.tensor_tensor(t["x"][:, b, :], t["x"][:, b, :], normed[:, b % 2, :], ALU.add).then_inc(s["based"], 1)
                pool.wait_ge(s["based"], NB)

        @block.tensor
        def _(pe):
            for b in range(NB + 1):
                if b < NB:
                    if b >= 2:
                        pe.wait_ge(s["low"], done + b - 1)
                    pe.wait_ge(s["normed"], done + b + 1)
                    for c in range(C):
                        turn = pe.transpose(turned[:, b % 2, c, 0:P], normed[:, b % 2, c::C], t["ident"][:])
                    turn.then_inc(s["turned"], 1)
                if b > 0 and router is not None:
                    n = b - 1
                    pe.wait_ge(s["low"], n + 1)
                    products = [(a, b2, c) for a, b2 in HIGH_LOW for c in range(C)]
                    for i, (a, b2, c) in enumerate(products):
                        mm = pe.matmul(router[:, n, :], x_t[:, a, c, n * P:(n + 1) * P], w["centroids"][:, b2, c, :],
                                       start=(i == 0), stop=(i == len(products) - 1))
                    mm.then_inc(s["router"], 1)
            if router is not None:
                pe.wait_ge(s["router"], NB)


def gating_phase(nc, t, w, router, gates):
    with ExitStack() as ctx:
        s = Sems(ctx, nc, "gating")

        def sb(name, shape, dt=F32):
            return ctx.enter_context(nc.sbuf_tensor(name, shape, dt))

        sig = sb("sig", [P, NB, EXPERTS])
        score = sb("score", [P, NB, EXPERTS])
        best = sb("best", [P, NB, 8])
        place = sb("place", [P, NB, 8], U32)
        place_f = sb("place_f", [P, NB, TOP])
        number = sb("number", [P, EXPERTS])
        hit = sb("hit", [P, NB, TOP, EXPERTS])
        member = sb("member", [P, NB, EXPERTS])
        kept = sb("kept", [P, NB, EXPERTS])
        total = sb("total2", [P, NB])
        floor = sb("floor", [P, NB])
        inverse = sb("inverse2", [P, NB])
        gate = sb("gate_rows", [P, NB, EXPERTS, P // EXPERTS])
        turned = ctx.enter_context(nc.psum_tensor("turned_gates", [P, 4, 4, P], F32))
        for n in ["sig", "score", "best", "place", "number", "step", "gate", "turned", "out"]:
            s[n]
        block = ctx.enter_context(nc.Block())

        @block.gpsimd
        def _(pool):
            pool.iota(number[:], [[1, EXPERTS]], base=0, channel_multiplier=0, allow_small_or_imprecise_dtypes=True).then_inc(s["number"], 1)
            pool.wait_ge(s["number"], 1)

        @block.scalar
        def _(act):
            act.activation(sig[:], router[:], ACT.Sigmoid, scale=DOWN).then_inc(s["sig"], 1)
            for i in range(4):
                act.wait_ge(s["turned"], i + 1)
                act.activation(gates[:, i * CHUNK:(i + 1) * CHUNK], turned[:, i].rearrange("p b m -> p (b m)"), ACT.Copy).then_inc(s["out"], 1)
            act.wait_ge(s["out"], 4)

        @block.vector
        def _(dve):
            dve.wait_ge(s["sig"], 1)
            dve.tensor_tensor(score[:], sig[:], w["router_bias"][:].unsqueeze(1).broadcast_to([P, NB, EXPERTS]), ALU.add).then_inc(s["score"], 1)
            dve.wait_ge(s["score"], 1)
            for b in range(NB):
                dve.max(best[:, b, :], score[:, b, :]).then_inc(s["best"], 1)
            for b in range(NB):
                dve.wait_ge(s["best"], b + 1)
                dve.max_index(place[:, b, :], best[:, b, :], score[:, b, :]).then_inc(s["place"], 1)
            dve.wait_ge(s["place"], NB)
            dve.tensor_copy(place_f[:], place[:, :, 0:TOP]).then_inc(s["step"], 1)
            dve.wait_ge(s["step"], 1)
            dve.wait_ge(s["number"], 1)
            for j in range(TOP):
                dve.tensor_tensor(hit[:, :, j, :], number[:].unsqueeze(1).broadcast_to([P, NB, EXPERTS]),
                                  place_f[:, :, j:j + 1].broadcast_to([P, NB, EXPERTS]), ALU.is_equal).then_inc(s["step"], 1)
            dve.wait_ge(s["step"], TOP + 1)
            dve.tensor_reduce(member[:], hit[:].rearrange("p b j e -> p b e j"), AX.X, ALU.add).then_inc(s["step"], 1)
            dve.wait_ge(s["step"], TOP + 2)
            dve.tensor_tensor(kept[:], score[:], member[:], ALU.mult).then_inc(s["step"], 1)
            dve.wait_ge(s["step"], TOP + 3)
            dve.tensor_reduce(total[:], kept[:], AX.X, ALU.add).then_inc(s["step"], 1)
            dve.wait_ge(s["step"], TOP + 4)
            dve.tensor_scalar(floor[:], total[:], 1e-8, None, ALU.max).then_inc(s["step"], 1)
            dve.wait_ge(s["step"], TOP + 5)
            dve.reciprocal(inverse[:], floor[:]).then_inc(s["step"], 1)
            dve.wait_ge(s["step"], TOP + 6)
            for b in range(NB):
                dve.tensor_scalar(gate[:, b], kept[:, b, :].unsqueeze(2).broadcast_to([P, EXPERTS, P // EXPERTS]),
                                  inverse[:, b:b + 1], None, ALU.mult).then_inc(s["gate"], 1)

        @block.tensor
        def _(pe):
            for b in range(NB):
                pe.wait_ge(s["gate"], b + 1)
                turn = pe.transpose(turned[:, b // 4, b % 4, :], gate[:, b].rearrange("p e r -> p (e r)"), t["ident"][:])
                if b % 4 == 3:
                    turn.then_inc(s["turned"], 1)


def experts_phase(nc, t, w, x_t, gates):
    UNITS = 3 + ROUTED_K
    AHEAD = 3
    with ExitStack() as ctx:
        s = Sems(ctx, nc, "moe")

        def sb(name, shape, dt=F32):
            return ctx.enter_context(nc.sbuf_tensor(name, shape, dt))

        relu = sb("relu", [P, 4, CHUNK])
        gated = sb("gated", [P, 3, CHUNK])
        hidden = sb("hidden", [P, 4, 2, CHUNK], F16)
        gate_part = sb("gate_part", [P, 2, TOKENS], F16)
        ps_h = ctx.enter_context(nc.psum_tensor("ps_h", [P, 4, CHUNK], F32))
        ps_o = ctx.enter_context(nc.psum_tensor("ps_o", [P, TILES, 2 * D], F32))
        for n in ["gate_high", "gate_low", "up_mm", "relu", "gated", "high", "low", "down_mm", "added"]:
            s[n]
        block = ctx.enter_context(nc.Block())

        class Tile:

            def __init__(self, j, base, v):
                self.n = j * UNITS + v * 3 + base
                self.buf = (base - 1) % 3 if base else 3
                self.rows = P if base >= 3 else SHARED_M[base]
                self.shared = base if base < 3 else None
                self.routed = v * 3 + (base - 3) if base >= 3 else None

        def tiles(eng, j, body):
            for base in range(3):
                body(base, 0)
            with eng.Fori(0, 6) as v:
                for base in range(3, 6):
                    body(base, v)
            for base in range(21, UNITS):
                body(base, 0)

        @block.tensor
        def _(pe):
            pe.wait_ge(s["gate_low"], 1)
            pe.sem_inc(s["down_mm"], AHEAD)

            def up(i, j):
                pe.wait_ge(s["relu"], i.n + 1)
                m = i.rows
                for k, (a, b) in enumerate(HIGH_LOW):
                    for c in range(C):
                        if i.shared is None:
                            lhs = w["w1"][:, a, c, ds(i.routed * P, P)]
                        else:
                            lhs = w["ws1"][:, a, c, i.shared * P:i.shared * P + m]
                        mm = pe.matmul(ps_h[0:m, i.buf, :], lhs, x_t[:, b, c, ds(j * CHUNK, CHUNK)],
                                       start=(k == 0 and c == 0), stop=(k == 2 and c == C - 1))
                mm.then_inc(s["up_mm"], 1)

            def down(i, j, first=False, last=False):
                pe.wait_ge(s["low"], i.n + 1 + AHEAD)
                m = i.rows
                for q in range(TILES):
                    if first:
                        for k, (a, b) in enumerate(HIGH_LOW):
                            pe.matmul(ps_o[:, q, 0:D], gate_part[:, a, ds(j * CHUNK + q * P, P)], w["b2"][:, b, :],
                                      start=(k == 0), stop=False, skip_group_check=True)
                    for k, (a, b) in enumerate(HIGH_LOW):
                        rhs = w["w2"][:, b, ds(i.routed * D, D)] if i.shared is None else w["ws2"][0:m, b, i.shared, :]
                        mm = pe.matmul(ps_o[:, q, 0:D], hidden[0:m, i.buf, a, q * P:(q + 1) * P], rhs,
                                       start=False, stop=(last and k == 2), skip_group_check=True)
                mm.then_inc(s["down_mm"], 1)

            with pe.Fori(0, CHUNKS) as j:
                up(Tile(j, 0, 0), j)
                up(Tile(j, 1, 0), j)

                def body(base, v):
                    if base + 2 < UNITS:
                        up(Tile(j, base + 2, v), j)
                    if base == 0:
                        pe.wait_ge(s["added"], j * TILES + 1)
                    down(Tile(j, base, v), j, first=(base == 0), last=(base == UNITS - 1))

                tiles(pe, j, body)

        @block.scalar
        def _(act):
            act.activation(gate_part[:, 0, :], gates[:], ACT.Copy).then_inc(s["gate_high"], 1)
            act.sem_inc(s["relu"], AHEAD)

            def relu_of(i):
                act.wait_ge(s["up_mm"], i.n + 1)
                act.wait_ge(s["low"], i.n + 1)
                m = i.rows
                bias = w["bs1"][0:m, i.shared:i.shared + 1] if i.shared is not None else w["b1"][:, ds(i.routed, 1)]
                act.activation(relu[0:m, i.buf, :], ps_h[0:m, i.buf, :], ACT.Relu, bias=bias, scale=DOWN).then_inc(s["relu"], 1)

            def high(i, j):
                m = i.rows
                act.wait_ge(s["down_mm"], i.n + 1)
                if i.shared is None:
                    act.wait_ge(s["gated"], j * ROUTED_K + i.routed + 1)
                else:
                    act.wait_ge(s["relu"], i.n + 1 + AHEAD)
                src = gated if i.shared is None else relu
                act.activation(hidden[0:m, i.buf, 0, :], src[0:m, i.buf, :], ACT.Copy).then_inc(s["high"], 1)

            with act.Fori(0, CHUNKS) as j:
                relu_of(Tile(j, 0, 0))

                def body(base, v):
                    if base + 1 < UNITS:
                        relu_of(Tile(j, base + 1, v))
                    high(Tile(j, base, v), j)

                tiles(act, j, body)

        @block.vector
        def _(dve):
            dve.wait_ge(s["gate_high"], 1)
            dve.tensor_tensor(gate_part[:, 1, :], gates[:], gate_part[:, 0, :], ALU.subtract).then_inc(s["gate_low"], 1)

            with dve.Fori(0, CHUNKS) as j:
                def body(base, v):
                    i = Tile(j, base, v)
                    if i.shared is None:
                        dve.wait_ge(s["relu"], i.n + 1 + AHEAD)
                        dve.wait_ge(s["low"], i.n + 1)
                        dve.tensor_tensor(gated[:, i.buf, :], relu[:, i.buf, :], gates[:, ds(j * CHUNK, CHUNK)],
                                          ALU.mult).then_inc(s["gated"], 1)

                tiles(dve, j, body)
                dve.wait_ge(s["down_mm"], j * UNITS + (UNITS + AHEAD))
                for q in range(TILES):
                    x = t["x"][:, ds(j * TILES + q, 1), :].rearrange("p o d -> p (o d)")
                    dve.scalar_tensor_tensor(out=x, in0=ps_o[:, q, 0:D], scalar=DOWN, in1=x,
                                             op0=ALU.mult, op1=ALU.add).then_inc(s["added"], 1)
            dve.wait_ge(s["added"], 1 + NB)

        @block.gpsimd
        def _(pool):
            pool.sem_inc(s["low"], AHEAD)
            pool.sem_inc(s["added"], 1)

            with pool.Fori(0, CHUNKS) as j:
                def body(base, v):
                    i = Tile(j, base, v)
                    pool.wait_ge(s["high"], i.n + 1)
                    src = gated if i.shared is None else relu
                    pool.tensor_tensor(hidden[0:i.rows, i.buf, 1, :], src[0:i.rows, i.buf, :], hidden[0:i.rows, i.buf, 0, :],
                                       ALU.subtract).then_inc(s["low"], 1)

                tiles(pool, j, body)


def mix_phase(nc, t, w, sums_all):
    with ExitStack() as ctx:
        s = Sems(ctx, nc, "mix")

        def sb(name, shape, dt=F32):
            return ctx.enter_context(nc.sbuf_tensor(name, shape, dt))

        y = sb("y", [P, NB, D])
        scaled = sb("scaled", [P, 2, D])
        stats = sb("mix_stats", [P, NB, 6])
        moments = sb("mix_moments", [P, NB, 2])
        base = sb("mix_base", [P, NB])
        power = sb("mix_power", [P, NB])
        rstd = sb("mix_rstd", [P, NB])
        for n in ["normed", "shifted", "stats", "moments", "base", "rstd", "power", "scaled", "beta", "out"]:
            s[n]
        block = ctx.enter_context(nc.Block())

        @block.gpsimd
        def _(pool):
            pool.memset(power[:], -0.5).then_inc(s["power"], 1)
            for b in range(NB):
                pool.wait_ge(s["normed"], b + 1)
                pool.tensor_tensor(y[:, b, :], y[:, b, :], sums_all[:, b, :], ALU.add).then_inc(s["shifted"], 1)
            pool.wait_ge(s["power"], 1)
            pool.wait_ge(s["base"], 1)
            pool.tensor_tensor(rstd[:], base[:], power[:], ALU.pow).then_inc(s["rstd"], 1)
            for b in range(NB):
                pool.tensor_tensor(t["x"][:, b, :], t["x"][:, b, :], w["beta"][:], ALU.add).then_inc(s["beta"], 1)

        @block.vector
        def _(dve):
            for b in range(NB):
                dve.tensor_scalar(y[:, b, :], t["x"][:, b, :], t["moments"][:, b, 0:1], t["rstd"][:, b:b + 1],
                                  ALU.subtract, ALU.mult).then_inc(s["normed"], 1)
            for b in range(NB):
                dve.wait_ge(s["shifted"], b + 1)
                dve.bn_stats(stats[:, b, :], y[:, b, :]).then_inc(s["stats"], 1)
            for b in range(NB):
                dve.wait_ge(s["stats"], b + 1)
                dve.bn_aggr(moments[:, b, :], stats[:, b, :]).then_inc(s["moments"], 1)
            dve.wait_ge(s["moments"], NB)
            dve.tensor_scalar(base[:], moments[:, :, 1], EPS, None, ALU.add).then_inc(s["base"], 1)
            dve.wait_ge(s["rstd"], 1)
            for b in range(NB + 1):
                if b < NB:
                    wait(dve, s["out"], b - 1)
                    dve.scalar_tensor_tensor(out=scaled[:, b % 2], in0=y[:, b, :], scalar=moments[:, b, 0:1], in1=w["gamma"][:],
                                             op0=ALU.subtract, op1=ALU.mult).then_inc(s["scaled"], 1)
                if b > 0:
                    n = b - 1
                    dve.wait_ge(s["scaled"], n + 1)
                    dve.wait_ge(s["beta"], n + 1)
                    dve.scalar_tensor_tensor(out=t["x"][:, n, :], in0=scaled[:, n % 2], scalar=rstd[:, n:n + 1], in1=t["x"][:, n, :],
                                             op0=ALU.mult, op1=ALU.add).then_inc(s["out"], 1)
            dve.wait_ge(s["out"], NB)


def query_phase(nc, t, w, x_t, routing):
    SETS = 2 * TOKENS // P
    with ExitStack() as ctx:
        s = Sems(ctx, nc, "query")
        q = ctx.enter_context(nc.sbuf_tensor("q_line", [P, 2 * TOKENS], F16))
        ps_q = ctx.enter_context(nc.psum_tensor("ps_q", [P, 2, CHUNK], F32))
        ps_r = ctx.enter_context(nc.psum_tensor("ps_r", [P, 4, CHUNK], F32))
        for n in ["query_mm", "high", "low", "key_mm", "out"]:
            s[n]
        block = ctx.enter_context(nc.Block())
        line = q[:].rearrange("p (n r) -> p r n", r=2)

        @block.tensor
        def _(pe):
            for n in range(2 * CHUNKS):
                j, r = n // 2, n % 2
                wait(pe, s["low"], n - 1)
                for k, (a, b) in enumerate(HIGH_LOW):
                    for c in range(C):
                        mm = pe.matmul(ps_q[:, n % 2, :], w["query"][:, a, c, r, :], x_t[:, b, c, j * CHUNK:(j + 1) * CHUNK],
                                       start=(k == 0 and c == 0), stop=(k == 2 and c == C - 1))
                mm.then_inc(s["query_mm"], 1)
            pe.wait_ge(s["low"], 2 * CHUNKS)
            for n in range(SETS):
                for a in range(2):
                    mm = pe.matmul(ps_r[:, n // 8, (n % 8) * KEYS:(n % 8 + 1) * KEYS], q[:, n * P:(n + 1) * P],
                                   w["keys"][:, a, n // NB, :], start=(a == 0), stop=(a == 1))
                if n % 8 == 7:
                    mm.then_inc(s["key_mm"], 1)

        @block.scalar
        def _(act):
            for n in range(2 * CHUNKS):
                j, r = n // 2, n % 2
                act.wait_ge(s["query_mm"], n + 1)
                act.activation(line[:, r, j * CHUNK:(j + 1) * CHUNK], ps_q[:, n % 2, :], ACT.Copy, scale=DOWN).then_inc(s["high"], 1)
            act.wait_ge(s["high"], 2 * CHUNKS)
            for n in range(4):
                act.wait_ge(s["key_mm"], n + 1)
                act.activation(routing[:, n * 8:(n + 1) * 8, :], ps_r[:, n, :].rearrange("p (g k) -> p g k", g=8),
                               ACT.Copy, scale=DOWN).then_inc(s["out"], 1)
            act.wait_ge(s["out"], 4)

        @block.vector
        def _(dve):
            for n in range(2 * CHUNKS):
                j, r = n // 2, n % 2
                dve.wait_ge(s["high"], n + 1)
                part = line[KDIM:P, r, j * CHUNK:(j + 1) * CHUNK]
                dve.scalar_tensor_tensor(out=part, in0=ps_q[KDIM:P, n % 2, :], scalar=DOWN, in1=part,
                                         op0=ALU.mult, op1=ALU.subtract).then_inc(s["low"], 1)
            dve.wait_ge(s["low"], 2 * CHUNKS)


def retrieval_phase(nc, t, w, routing, picks, inverse):
    with ExitStack() as ctx:
        s = Sems(ctx, nc, "retrieve")

        def sb(name, shape, dt=F32):
            return ctx.enter_context(nc.sbuf_tensor(name, shape, dt))

        best = sb("best_keys", [P, 2 * NB, 8])
        pairs = sb("pairs", [P, NB, 8, 8])
        top = sb("top", [P, NB, 8])
        lowered = sb("lowered", [P, NB, 8])
        exps = sb("exps", [P, NB, 8])
        neg = sb("neg", [P, NB])
        total = sb("total3", [P, NB])
        listed = sb("listed", [P, NB])
        dense = sb("dense", [P, 2, 8, KEYS])
        dense_exp = sb("dense_exp", [P, 2, TABLE])
        for n in ["best", "pairs", "top", "neg", "lowered", "exps", "total", "inverse", "dense", "dense_exp", "picks", "last"]:
            s[n]
        block = ctx.enter_context(nc.Block())

        @block.vector
        def _(dve):
            for n in range(2 * NB):
                dve.max(best[:, n, :], routing[:, n, :]).then_inc(s["best"], 1)
            dve.wait_ge(s["best"], 2 * NB)
            for i in range(8):
                dve.tensor_tensor(pairs[:, :, i, :], best[:, NB:2 * NB, :], best[:, 0:NB, i:i + 1].broadcast_to([P, NB, 8]),
                                  ALU.add).then_inc(s["pairs"], 1)
            dve.wait_ge(s["pairs"], 8)
            for b in range(NB):
                dve.max(top[:, b, :], pairs[:, b]).then_inc(s["top"], 1)
            dve.wait_ge(s["top"], NB)
            dve.tensor_scalar(neg[:], top[:, :, 0], -1.0, None, ALU.mult).then_inc(s["neg"], 1)
            dve.tensor_tensor(lowered[:], top[:], top[:, :, 0:1].broadcast_to([P, NB, 8]), ALU.subtract).then_inc(s["lowered"], 1)
            dve.wait_ge(s["exps"], 1)
            dve.tensor_reduce(total[:], exps[:], AX.X, ALU.add).then_inc(s["total"], 1)
            dve.wait_ge(s["total"], 1)
            dve.reciprocal(inverse[:], total[:]).then_inc(s["inverse"], 1)
            for b in range(NB + 1):
                if b < NB:
                    wait(dve, s["picks"], b - 1)
                    dve.tensor_tensor(dense[:, b % 2], routing[:, b, 0:8].unsqueeze(2).broadcast_to([P, 8, KEYS]),
                                      routing[:, NB + b, :].unsqueeze(1).broadcast_to([P, 8, KEYS]), ALU.add).then_inc(s["dense"], 1)
                if b > 0:
                    n = b - 1
                    dve.wait_ge(s["dense_exp"], n + 1)
                    flat = dense[:, n % 2].rearrange("p i j -> p (i j)")
                    dve.scalar_tensor_tensor(out=picks[:, n, 0:TABLE - 1], in0=flat[:, 0:TABLE - 1], scalar=top[:, n, 7:8],
                                             in1=dense_exp[:, n % 2, 0:TABLE - 1], op0=ALU.is_ge, op1=ALU.mult,
                                             accum_out=listed[:, n:n + 1]).then_inc(s["picks"], 1)
            dve.wait_ge(s["picks"], NB)
            dve.tensor_tensor(picks[:, :, TABLE - 1], total[:], listed[:], ALU.subtract).then_inc(s["last"], 1)
            dve.wait_ge(s["last"], 1)
            dve.wait_ge(s["inverse"], 1)

        @block.scalar
        def _(act):
            act.wait_ge(s["lowered"], 1)
            act.activation(exps[:], lowered[:], ACT.Exp).then_inc(s["exps"], 1)
            for b in range(NB):
                act.wait_ge(s["dense"], b + 1)
                wait(act, s["picks"], b - 1)
                act.activation(dense_exp[:, b % 2, :], dense[:, b % 2].rearrange("p i j -> p (i j)"), ACT.Exp,
                               bias=neg[:, b:b + 1]).then_inc(s["dense_exp"], 1)


def ffn_phase(nc, dram, t, w, x_t, picks, inverse):
    with ExitStack() as ctx:
        s = Sems(ctx, nc, "ffn")

        def sb(name, shape, dt=F32):
            return ctx.enter_context(nc.sbuf_tensor(name, shape, dt))

        act_g = sb("act_g", [P, 2, CHUNK])
        prod = sb("prod", [P, 2, CHUNK])
        hidden = sb("hidden2", [P, 2, 2, CHUNK], F16)
        act_e = sb("act_e", [P, 2, TABLE])
        weight = sb("weight2", [P, 2, TABLE])
        weight_t = sb("weight_t", [P, 2, 2, TABLE_K, P], F16)
        ps_g = ctx.enter_context(nc.psum_tensor("ps_g", [P, 2, 2, CHUNK], F32))
        ps_e = ctx.enter_context(nc.psum_tensor("ps_e", [P, 2, TABLE], F32))
        ps_o = ctx.enter_context(nc.psum_tensor("ps_out", [P, TILES // 2, 2, D], F32))
        for n in ["gate_mm", "up_mm", "act_g", "prod", "high", "low", "down_mm", "table_mm", "act_e", "weight",
                  "turned", "wt_high", "wt_low", "row_mm", "added", "stored"]:
            s[n]
        block = ctx.enter_context(nc.Block())
        K = INTER_K

        @block.tensor
        def _(pe):
            def product(out, lhs, rhs, start, stop):
                for k, (a, b) in enumerate(HIGH_LOW):
                    for c in range(C):
                        mm = pe.matmul(out, lhs(a, c), rhs(b, c), start=(start and k == 0 and c == 0), stop=(stop and k == 2 and c == C - 1))
                return mm

            def up(i, j):
                n = j * K + i
                pe.wait_ge(s["prod"], n + 1)
                for which, name in ((0, "gate"), (1, "up")):
                    product(ps_g[:, i % 2, which, :], lambda a, c: w[name][:, a, c, i * P:(i + 1) * P],
                            lambda b, c: x_t[:, b, c, ds(j * CHUNK, CHUNK)], True, True).then_inc(s[name + "_mm"], 1)

            def down(i, j):
                n = j * K + i
                pe.wait_ge(s["low"], n + 2)
                if i == 0:
                    pe.wait_ge(s["added"], j * TILES + 1)
                for q in range(TILES):
                    for k, (a, b) in enumerate(HIGH_LOW):
                        mm = pe.matmul(ps_o[:, q // 2, q % 2, :], hidden[:, i % 2, a, q * P:(q + 1) * P],
                                       w["down"][:, b, i * D:(i + 1) * D], start=(i == 0 and k == 0 and q % 2 == 0),
                                       stop=False, skip_group_check=True)
                mm.then_inc(s["down_mm"], 1)

            def table(q, j):
                n = j * TILES + q
                pe.wait_ge(s["wt_low"], n + 1)
                product(ps_e[:, q % 2, :], lambda a, c: x_t[:, a, c, ds(j * CHUNK + q * P, P)],
                        lambda b, c: w["table_down"][:, b, c, :], True, True).then_inc(s["table_mm"], 1)

            def turn(q, j):
                pe.wait_ge(s["weight"], j * TILES + q + 2)
                for k in range(TABLE_K):
                    mm = pe.transpose(ps_e[:, q % 2, k * P:(k + 1) * P], weight[:, q % 2, k * P:(k + 1) * P], t["ident"][:])
                mm.then_inc(s["turned"], 1)

            def rows(q, j):
                pe.wait_ge(s["wt_low"], j * TILES + q + 3)
                for k, (a, b) in enumerate(HIGH_LOW):
                    for i in range(TABLE_K):
                        mm = pe.matmul(ps_o[:, q // 2, q % 2, :], weight_t[:, q % 2, a, i, :], w["table_up"][:, b, i, :],
                                       start=False, stop=(q % 2 == 1 and k == 2 and i == TABLE_K - 1), skip_group_check=True)
                mm.then_inc(s["row_mm"], 1)

            with pe.Fori(0, CHUNKS) as j:
                up(0, j)
                for i in range(K):
                    if i % 2 == 0:
                        table(i // 2, j)
                    if i + 1 < K:
                        up(i + 1, j)
                    if i % 2 == 1:
                        turn(i // 2, j)
                    down(i, j)
                    if i % 2 == 0 and i > 0:
                        rows(i // 2 - 1, j)
                rows(TILES - 1, j)

        @block.scalar
        def _(act):
            with act.Fori(0, CHUNKS) as j:
                for i in range(K):
                    n = j * K + i
                    act.wait_ge(s["gate_mm"], n + 1)
                    act.wait_ge(s["prod"], n + 1)
                    act.activation(act_g[:, i % 2, :], ps_g[:, i % 2, 0, :], ACT.Silu, scale=DOWN).then_inc(s["act_g"], 1)
                    if i % 2 == 0:
                        q = i // 2
                        m = j * TILES + q
                        act.wait_ge(s["table_mm"], m + 1)
                        act.wait_ge(s["weight"], m + 1)
                        act.activation(act_e[:, q % 2, :], ps_e[:, q % 2, :], ACT.Silu, scale=DOWN).then_inc(s["act_e"], 1)
                    act.wait_ge(s["prod"], n + 3)
                    act.wait_ge(s["down_mm"], n + 1)
                    act.activation(hidden[:, i % 2, 0, :], prod[:, i % 2, :], ACT.Copy).then_inc(s["high"], 1)
                    if i % 2 == 1:
                        q = i // 2
                        m = j * TILES + q
                        act.wait_ge(s["turned"], m + 2)
                        act.wait_ge(s["row_mm"], m + 1)
                        act.activation(weight_t[:, q % 2, 0].rearrange("p k n -> p (k n)"), ps_e[:, q % 2, :], ACT.Copy).then_inc(s["wt_high"], 1)

        @block.vector
        def _(dve):
            dve.sem_inc(s["prod"], 2)
            dve.sem_inc(s["down_mm"], 2)
            dve.sem_inc(s["row_mm"], 2)
            dve.sem_inc(s["wt_low"], 2)
            dve.sem_inc(s["added"], 1)
            dve.sem_inc(s["weight"], 1)
            dve.sem_inc(s["turned"], 1)
            dve.sem_inc(s["low"], 1)
            with dve.Fori(0, CHUNKS) as j:
                for i in range(K):
                    n = j * K + i
                    if i % 2 == 0:
                        q = i // 2
                        m = j * TILES + q
                        dve.wait_ge(s["act_e"], m + 1)
                        dve.wait_ge(s["turned"], m + 1)
                        dve.scalar_tensor_tensor(out=weight[:, q % 2, :], in0=picks[:, ds(m, 1), :].rearrange("p o e -> p (o e)"),
                                                 scalar=inverse[:, ds(m, 1)], in1=act_e[:, q % 2, :],
                                                 op0=ALU.mult, op1=ALU.mult).then_inc(s["weight"], 1)
                    dve.wait_ge(s["act_g"], n + 1)
                    dve.wait_ge(s["up_mm"], n + 1)
                    dve.wait_ge(s["low"], n + 1)
                    dve.scalar_tensor_tensor(out=prod[:, i % 2, :], in0=ps_g[:, i % 2, 1, :], scalar=DOWN, in1=act_g[:, i % 2, :],
                                             op0=ALU.mult, op1=ALU.mult).then_inc(s["prod"], 1)
                    if i % 2 == 1:
                        q = i // 2
                        m = j * TILES + q
                        dve.wait_ge(s["wt_high"], m + 1)
                        dve.tensor_tensor(weight_t[:, q % 2, 1].rearrange("p k n -> p (k n)"), ps_e[:, q % 2, :],
                                          weight_t[:, q % 2, 0].rearrange("p k n -> p (k n)"), ALU.subtract).then_inc(s["wt_low"], 1)
                dve.wait_ge(s["row_mm"], j * TILES + TILES + 2)
                for q in range(TILES):
                    x = t["x"][:, ds(j * TILES + q, 1), :].rearrange("p o d -> p (o d)")
                    dve.scalar_tensor_tensor(out=x, in0=ps_o[:, q // 2, q % 2, :], scalar=DOWN, in1=x,
                                             op0=ALU.mult, op1=ALU.add).then_inc(s["added"], 1)

        @block.gpsimd
        def _(pool):
            with pool.Fori(0, CHUNKS) as j:
                for i in range(K):
                    n = j * K + i
                    pool.wait_ge(s["high"], n + 1)
                    pool.tensor_tensor(hidden[:, i % 2, 1, :], prod[:, i % 2, :], hidden[:, i % 2, 0, :], ALU.subtract).then_inc(s["low"], 1)

        @block.sync
        def _(sp):
            with sp.Fori(0, CHUNKS) as j:
                wait_alone(sp, s["added"], j * TILES + (TILES + 1), s["seen"])
                sp.dma_start(dram["out"][ds(j * TILES, TILES)].rearrange("b p d -> p b d"), t["x"][:, ds(j * TILES, TILES), :]).then_inc(s["stored"], 16)
            sp.wait_ge(s["stored"], 16 * CHUNKS)


def rest_of_program(nc, dram, t, scratch):
    with ExitStack() as ctx:
        w = weight_tensors(ctx, nc)
        norm = Sems(ctx, nc, "norm")
        for n in ["power", "base", "rstd", "stats", "moments"]:
            norm[n]
        turn = Sems(ctx, nc, "turn")
        for n in ["normed", "turned", "high", "low", "router", "bias", "biased", "based"]:
            turn[n]
        x_t = ctx.enter_context(nc.sbuf_tensor("x_t", [P, 2, C, TOKENS], F16))
        weights_phase(nc, dram, t, w)
        with ExitStack() as inner:
            sums_all = inner.enter_context(nc.sbuf_tensor("sums_all", [P, NB, D], F32))
            summary_phase(nc, dram, t, scratch, sums_all)
            with nc.sbuf_tensor("gates", [P, TOKENS], F32) as gates:
                norm_phase(nc, t, norm, 0)
                with nc.psum_tensor("router", [P, NB, EXPERTS], F32) as router:
                    turn_phase(nc, t, w, x_t, turn, 0, router)
                    gating_phase(nc, t, w, router, gates)
                experts_phase(nc, t, w, x_t, gates)
            norm_phase(nc, t, norm, 1)
            mix_phase(nc, t, w, sums_all)
        norm_phase(nc, t, norm, 2)
        turn_phase(nc, t, w, x_t, turn, 1)
        with ExitStack() as inner:
            picks = inner.enter_context(nc.sbuf_tensor("picks", [P, NB, TABLE], F32))
            inverse = inner.enter_context(nc.sbuf_tensor("inverse3", [P, NB], F32))
            with nc.sbuf_tensor("routing", [P, 2 * NB, KEYS], F32) as routing:
                query_phase(nc, t, w, x_t, routing)
                retrieval_phase(nc, t, w, routing, picks, inverse)
            ffn_phase(nc, dram, t, w, x_t, picks, inverse)


def two_layers(nc, dram):
    scratch = scratch_tensors(nc)
    with ExitStack() as ctx:
        t = lasting_tensors(ctx, nc)
        with ExitStack() as inner:
            attention = dict(t, **attention_tensors(inner, nc))
            setup_phase(nc, dram, attention, scratch)
            attention_phase(nc, dram, attention, scratch)
        rest_of_program(nc, dram, t, scratch)


INPUTS = [
    "x", "ctx_2048", "mask_Bx1x2048_fk1", "L0_xattn_Wq", "L0_xattn_bq", "L0_xattn_Wk",
    "L0_xattn_bk", "L0_xattn_Wv", "L0_xattn_bv", "L0_ffn_shared_w1", "L0_ffn_shared_b1",
    "L0_ffn_shared_w2", "L0_ffn_shared_b2", "L0_ffn_routed_w1", "L0_ffn_routed_b1",
    "L0_ffn_routed_w2", "L0_ffn_routed_b2", "L0_ffn_centroids", "L0_ffn_bias", "L1_xattn_decay",
    "L1_xattn_W_in", "L1_xattn_b_in", "L1_xattn_W_out", "L1_xattn_b_out", "L1_xattn_gamma",
    "L1_xattn_beta", "L1_ffn_W_q", "L1_ffn_keys", "L1_ffn_down_embed", "L1_ffn_up_embed",
    "L1_ffn_gate_w", "L1_ffn_up_w", "L1_ffn_down_w"]


def kernel(**inputs):
    import numpy as np
    import concourse.bacc as bacc
    from concourse.bass_utils import run_bass_kernel_spmd

    nc = bacc.Bacc("TRN2", target_bir_lowering=False, num_devices=1)
    arrays, dram = {}, {}
    for name in INPUTS:
        a = np.ascontiguousarray(inputs[name])
        if a.ndim == 0:
            a = a.reshape(1)
        arrays[f"in_{name}_dram"] = a
        dram[name] = nc.dram_tensor(f"in_{name}_dram", a.shape, mybir.dt.from_np(a.dtype), kind="ExternalInput").ap()
    dram["out"] = nc.dram_tensor("out_0_dram", (NB, P, D), F32, kind="ExternalOutput").ap()
    two_layers(nc, dram)
    return run_bass_kernel_spmd(nc, [arrays], core_ids=[0]).results[0]["out_0_dram"]
```

```python
from contextlib import ExitStack

import concourse.bass as bass
from concourse import mybir
from concourse.bass import ds

F32 = mybir.dt.float32
F16 = mybir.dt.float16
BF16 = mybir.dt.bfloat16
U32 = mybir.dt.uint32
ALU = mybir.AluOpType
ACT = mybir.ActivationFunctionType
AX = mybir.AxisListType

P = 128
NB = 16
D = 256
HEADS = 16
HD = P // HEADS
ST = D // P
EPS = 1e-5
NEG = 1e6 * HD ** 0.5

TERMS = ((0, 0), (0, 1), (0, 2), (1, 0), (1, 1), (2, 0))
MASK_ROW = 64
MAX_ROW = 65
ROWS = 68
SAME = ((0, 3, 0), (3, 2, 1), (5, 1, 2))
STACK_DMAS = 2 * len(SAME) + 1
RING = 4
PAIR_OF_ONES = 1.0 + 0x3F80 / 2 ** 23


HIGH_LOW = ((0, 0), (0, 1), (1, 0))
UP = 64.0
DOWN = 1.0 / UP
C = D // P
CHUNK = 512
TOKENS = NB * P
CHUNKS = TOKENS // CHUNK
TILES = CHUNK // P
EXPERTS, SHARED, FF = 16, 2, 176
ROUTED_K = EXPERTS * FF // P
SHARED_F = SHARED * FF
SHARED_M = (P, P, SHARED_F - 2 * P)
TOP = 4
INTER = 1024
INTER_K = INTER // P
TABLE = 512
TABLE_K = TABLE // P
KEYS = 64
KDIM = 64


def wait(eng, sem, value):
    if not (isinstance(value, int) and value <= 0):
        eng.wait_ge(sem, value)


def wait_alone(eng, sem, value, seen):
    wait(eng, sem, value)
    if not isinstance(value, int):
        eng.sem_inc(seen, 1)


class Sems:

    def __init__(self, ctx, nc, prefix):
        self._ctx, self._nc, self._prefix, self._made = ctx, nc, prefix, {}

    def __getitem__(self, name):
        if name not in self._made:
            self._made[name] = self._nc.alloc_semaphore(f"{self._prefix}_{name}")
        return self._made[name]

    def clear(self):
        self._nc.clear_and_free_semaphores(list(self._made.values()))
        self._nc.all_engine_barrier()


def setup_phase(nc, dram, t, scratch, w):
    with ExitStack() as ctx:
        s = Sems(ctx, nc, "setup")

        def sb(name, shape, dt=F32):
            return ctx.enter_context(nc.sbuf_tensor(name, shape, dt))

        w_rows = sb("w_rows", [P, 3, P])
        mask_rows = sb("mask_rows", [NB, D])
        penalty = sb("penalty", [NB, D], BF16)
        stats = sb("stats", [P, NB, 6])
        base = sb("base", [P, NB])
        power = sb("power", [P, NB])
        rows = sb("rows", [P, TABLE_K + 1, D])
        context = sb("context2", [P, NB, D])
        decay = sb("decay", [P, 1])
        keep = sb("keep", [P, 8])
        runs = sb("runs", [P, P])
        anti = sb("anti", [P, P])
        picked = sb("picked", [P, P])
        weight = sb("weight", [P, 1])
        total = sb("total", [1, 2])
        spread = sb("spread", [P, NB, NB])
        proj_rows = sb("proj_rows", [P, 2, C, D])
        proj_cols = sb("proj_cols", [P, 2, C, D])
        biases = sb("biases", [1, 2, D])
        factors = sb("factors", [1, 2, NB])
        mean = sb("mean", [NB, 3, D])
        mean_t = sb("mean_t", [P, 2, C, NB])
        turned = ctx.enter_context(nc.psum_tensor("turned", [P, 2 * D], F32))
        turned_small = ctx.enter_context(nc.psum_tensor("turned_small", [P, 4, P], F32))
        turned_proj = ctx.enter_context(nc.psum_tensor("turned_proj", [P, 2, C, D], F32))
        ps_mean = ctx.enter_context(nc.psum_tensor("ps_mean", [NB, 4, D], F32))
        turned_table = ctx.enter_context(nc.psum_tensor("turned_table", [P, C, TABLE], F32))
        turned_mask = turned_small[:, 0, 0:ST * NB].rearrange("p (s b) -> p s b", s=ST)
        turned_c = turned_small[:, 1, 0:C * EXPERTS].rearrange("p (c e) -> p c e", c=C)
        for n in ["x_in", "w_in", "mask_in", "other_in", "ident", "w_turned", "w_copied",
                  "mask_turned", "mask_copied", "stats", "moments", "base", "rstd", "shift", "penalty", "penalty_out",
                  "clear", "ones", "small_in", "rows_in", "table_turned", "high", "low",
                  "decay_in", "ctx_in", "proj_in", "bias_in", "anti", "keep", "runs", "weight", "spread",
                  "total", "factors", "proj_turned", "proj_cols", "mean_mm", "mean", "mean_turned", "mean_t"]:
            s[n]
        small_moves = [(w["b1"][:], dram["L0_ffn_routed_b1"].rearrange("e f -> (e f)").rearrange("(p i) -> p i", p=P)),
                       (w["bs2"][:], dram["L0_ffn_shared_b2"].partition_broadcast(P)),
                       (w["router_bias"][:], dram["L0_ffn_bias"].partition_broadcast(P))]
        bs1 = dram["L0_ffn_shared_b1"].rearrange("n f -> (n f)")
        for k, m in enumerate(SHARED_M):
            small_moves.append((w["bs1"][0:m, k:k + 1], bs1[k * P:k * P + m].rearrange("(p o) -> p o", o=1)))
        turned_cuts = [(turned_table[:, c], [w["table_down"][:, a, c] for a in range(2)]) for c in range(C)]
        turned_cuts += [(turned_c, [w["centroids"][:, a] for a in range(2)])]
        block = ctx.enter_context(nc.Block())

        @block.sync
        def _(sp):
            for i, name in enumerate(("L0_xattn_Wq", "L0_xattn_Wk", "L0_xattn_Wv")):
                sp.dma_start(w_rows[:, i, :], dram[name]).then_inc(s["w_in"], 16)
            sp.dma_start(mask_rows[:], dram["mask_Bx1x2048_fk1"].rearrange("b o t -> (b o) t")).then_inc(s["mask_in"], 16)
            sp.dma_start(decay[:], dram["L1_xattn_decay"].partition_broadcast(P)).then_inc(s["decay_in"], 16)
            sp.dma_start(t["x"][:], dram["x"].rearrange("b p d -> p b d")).then_inc(s["x_in"], 16)
            sp.dma_start(context[:], dram["ctx_2048"].rearrange("b p d -> p b d")).then_inc(s["ctx_in"], 16)
            for i, name in enumerate(("L1_xattn_W_in", "L1_xattn_W_out")):
                sp.dma_start(proj_rows[:, i], dram[name].rearrange("(k p) d -> p k d", p=P)).then_inc(s["proj_in"], 16)
            for i, name in enumerate(("L1_xattn_b_in", "L1_xattn_b_out")):
                sp.dma_start(biases[:, i, :], dram[name].rearrange("(o d) -> o d", o=1)).then_inc(s["bias_in"], 16)
            sp.dma_start(rows[:, 0:TABLE_K], dram["L1_ffn_down_embed"].rearrange("(k p) d -> p k d", p=P)).then_inc(s["rows_in"], 16)
            sp.dma_start(rows[0:EXPERTS, TABLE_K], dram["L0_ffn_centroids"]).then_inc(s["rows_in"], 16)
            for i, name in enumerate(("L0_xattn_bq", "L0_xattn_bk")):
                sp.dma_start(t["b_qk"][:, i:i + 1], dram[name].rearrange("(h d) -> d h", d=HD),
                             allow_slow_non_contiguous=True).then_inc(s["other_in"], 16)
            sp.dma_start(t["bv_rows"][:], dram["L0_xattn_bv"].partition_broadcast(P)).then_inc(s["other_in"], 16)
            for dst, src in small_moves:
                sp.dma_start(dst, src).then_inc(s["small_in"], 16)
            sp.wait_ge(s["penalty"], 1)
            sp.dma_start(scratch["penalty"], penalty[:]).then_inc(s["penalty_out"], 16)
            sp.wait_ge(s["mean"], 3)
            sp.dma_start(scratch["summary"], mean[:, 2, :]).then_inc(s["penalty_out"], 16)
            sp.wait_ge(s["penalty_out"], 32)
            sp.wait_ge(s["x_in"], 16)
            sp.wait_ge(s["other_in"], 48)
            sp.wait_ge(s["small_in"], 16 * len(small_moves))

        @block.gpsimd
        def _(pool):
            pool.memset(t["ident"][:], 0.0).then_inc(s["ident"], 1)
            pool.memset(anti[:], 0.0).then_inc(s["anti"], 1)
            pool.wait_ge(s["ident"], 1)
            pool.affine_select(out=t["ident"][:], in_=t["ident"][:], compare_op=ALU.not_equal, fill=1.0,
                               base=0, pattern=[[-1, P]], channel_multiplier=1).then_inc(s["ident"], 1)
            pool.wait_ge(s["anti"], 1)
            pool.affine_select(out=anti[:], in_=anti[:], compare_op=ALU.not_equal, fill=1.0 / P,
                               base=-(P - 1), pattern=[[1, P]], channel_multiplier=1).then_inc(s["anti"], 1)
            pool.memset(power[:], -0.5).then_inc(s["clear"], 1)
            pool.wait_ge(s["clear"], 1)
            pool.memset(t["v_wide"][:], 0.0).then_inc(s["clear"], 1)
            pool.wait_ge(s["clear"], 2)
            pool.memset(t["stack"][32:64].bitcast(F32), 0.0).then_inc(s["clear"], 1)
            pool.wait_ge(s["clear"], 3)
            pool.wait_ge(s["base"], 1)
            pool.tensor_tensor(t["rstd"][:], base[:], power[:], ALU.pow).then_inc(s["rstd"], 1)

        @block.tensor
        def _(pe):
            pe.wait_ge(s["ident"], 2)
            pe.wait_ge(s["w_in"], 48)
            for i in range(3):
                turn = pe.transpose(turned[:, i * P:(i + 1) * P], w_rows[:, i, :], t["ident"][:])
            turn.then_inc(s["w_turned"], 1)
            pe.wait_ge(s["mask_in"], 16)
            for h in range(ST):
                turn = pe.transpose(turned_mask[:, h, :], mask_rows[:, h * P:(h + 1) * P], t["ident"][0:NB, 0:NB])
            turn.then_inc(s["mask_turned"], 1)
            pe.wait_ge(s["proj_in"], 32)
            for i in range(2):
                for k in range(C):
                    for c in range(C):
                        turn = pe.transpose(turned_proj[:, i, c, k * P:(k + 1) * P], proj_rows[:, i, k, c * P:(c + 1) * P], t["ident"][:])
            turn.then_inc(s["proj_turned"], 1)
            pe.wait_ge(s["rows_in"], 32)
            for c in range(C):
                for k in range(TABLE_K):
                    pe.transpose(turned_table[:, c, k * P:(k + 1) * P], rows[:, k, c::C], t["ident"][:])
            pe.wait_ge(s["mask_copied"], 1)
            for c in range(C):
                turn = pe.transpose(turned_c[:, c, :], rows[0:EXPERTS, TABLE_K, c::C], t["ident"][0:EXPERTS, 0:EXPERTS])
            turn.then_inc(s["table_turned"], 1)
            pe.wait_ge(s["ctx_in"], 16)
            pe.wait_ge(s["spread"], 1 + NB)
            for b in range(NB):
                mm = pe.matmul(ps_mean[:, 0, :], spread[:, b, :], context[:, b, :], start=(b == 0), stop=(b == NB - 1))
            mm.then_inc(s["mean_mm"], 1)
            pe.wait_ge(s["proj_cols"], 1)
            pe.wait_ge(s["bias_in"], 32)
            pe.wait_ge(s["factors"], 2)
            pe.wait_ge(s["w_copied"], 3)
            for i in range(2):
                pe.wait_ge(s["mean"], i + 1)
                for c in range(C):
                    turn = pe.transpose(turned[:, c * NB:(c + 1) * NB], mean[:, i, c * P:(c + 1) * P], t["ident"][0:NB, 0:NB])
                turn.then_inc(s["mean_turned"], 1)
                pe.wait_ge(s["mean_t"], i + 1)
                for c in range(C):
                    pe.matmul(ps_mean[:, i + 1, :], mean_t[:, i, c, :], proj_cols[:, i, c, :], start=(c == 0), stop=False)
                pe.matmul(ps_mean[:, i + 1, :], factors[:, i, :], biases[:, i, :], start=False, stop=True).then_inc(s["mean_mm"], 1)

        @block.scalar
        def _(act):
            act.wait_ge(s["decay_in"], 16)
            act.activation(keep[:, 0:1], decay[:], ACT.Sigmoid).then_inc(s["keep"], 1)
            act.wait_ge(s["w_turned"], 1)
            for i in range(2):
                act.activation(t["w_qkv"][:, i].rearrange("p (d h) -> p h d", d=HD),
                               turned[:, i * P:(i + 1) * P].rearrange("p (h d) -> p h d", d=HD), ACT.Copy).then_inc(s["w_copied"], 1)
            act.activation(t["w_qkv"][:, 2], turned[:, 2 * P:3 * P], ACT.Copy).then_inc(s["w_copied"], 1)
            act.wait_ge(s["mask_turned"], 1)
            act.activation(t["mask_cols"][:], turned_mask, ACT.Copy).then_inc(s["mask_copied"], 1)
            act.wait_ge(s["proj_turned"], 1)
            act.activation(proj_cols[:], turned_proj[:], ACT.Copy).then_inc(s["proj_cols"], 1)
            act.wait_ge(s["table_turned"], 1)
            for src, dst in turned_cuts:
                act.activation(dst[0], src, ACT.Copy, scale=UP).then_inc(s["high"], 1)
            act.wait_ge(s["mask_copied"], 1)
            act.wait_ge(s["w_copied"], 3)

        @block.vector
        def _(dve):
            dve.memset(spread[:], 0.0).then_inc(s["spread"], 1)
            dve.memset(runs[:, 0:1], 1.0).then_inc(s["runs"], 1)
            dve.memset(factors[:, 1, :], 1.0).then_inc(s["factors"], 1)
            dve.memset(t["ones_wide"][:], 0.0).then_inc(s["ones"], 1)
            dve.wait_ge(s["ones"], 1)
            for g in range(4):
                dve.memset(t["ones_wide"][:, g, g * HD:(g + 1) * HD], 1.0).then_inc(s["ones"], 1)
            dve.memset(t["stack"][64:ROWS].bitcast(F32), PAIR_OF_ONES).then_inc(s["ones"], 1)
            dve.wait_ge(s["mask_in"], 16)
            dve.tensor_scalar(penalty[:], mask_rows[:], -1.0, NEG, ALU.add, ALU.mult).then_inc(s["penalty"], 1)
            n = 1
            for i in range(7):
                dve.wait_ge(s["runs"], i + 1)
                dve.wait_ge(s["keep"], i + 1)
                dve.tensor_scalar(runs[:, n:2 * n], runs[:, 0:n], keep[:, i:i + 1], runs[:, n - 1:n],
                                  ALU.mult, ALU.add).then_inc(s["runs"], 1)
                dve.tensor_tensor(keep[:, i + 1:i + 2], keep[:, i:i + 1], keep[:, i:i + 1], ALU.mult).then_inc(s["keep"], 1)
                n *= 2
            dve.wait_ge(s["runs"], 8)
            dve.wait_ge(s["anti"], 2)
            dve.tensor_tensor(picked[:], runs[:], anti[:], ALU.mult).then_inc(s["weight"], 1)
            dve.wait_ge(s["weight"], 1)
            dve.tensor_reduce(weight[:], picked[:], AX.X, ALU.add).then_inc(s["weight"], 1)
            dve.tensor_reduce(total[:, 0:1], runs[0:1, :], AX.X, ALU.add).then_inc(s["total"], 1)
            dve.wait_ge(s["weight"], 2)
            dve.wait_ge(s["spread"], 1)
            for b in range(NB):
                dve.tensor_copy(spread[:, b, b:b + 1], weight[:]).then_inc(s["spread"], 1)
            dve.wait_ge(s["total"], 1)
            dve.wait_ge(s["factors"], 1)
            dve.tensor_scalar(factors[:, 0, :], factors[:, 1, :], total[:, 0:1], 1.0 / P, ALU.mult, ALU.mult).then_inc(s["factors"], 1)
            dve.wait_ge(s["x_in"], 16)
            for b in range(NB):
                dve.bn_stats(stats[:, b, :], t["x"][:, b, :]).then_inc(s["stats"], 1)
            for b in range(NB):
                dve.wait_ge(s["stats"], b + 1)
                dve.bn_aggr(t["moments"][:, b, :], stats[:, b, :]).then_inc(s["moments"], 1)
            dve.wait_ge(s["moments"], NB)
            dve.tensor_scalar(base[:], t["moments"][:, :, 1], EPS, None, ALU.add).then_inc(s["base"], 1)
            dve.wait_ge(s["rstd"], 1)
            dve.scalar_tensor_tensor(out=t["shift"][:], in0=t["moments"][:, :, 0], scalar=-1.0, in1=t["rstd"][:],
                                     op0=ALU.mult, op1=ALU.mult).then_inc(s["shift"], 1)
            for i in range(3):
                dve.wait_ge(s["mean_mm"], i + 1)
                dve.tensor_copy(mean[:, i, :], ps_mean[:, i, :]).then_inc(s["mean"], 1)
                if i < 2:
                    dve.wait_ge(s["mean_turned"], i + 1)
                    dve.tensor_copy(mean_t[:, i], turned[:, 0:C * NB].rearrange("p (c b) -> p c b", c=C)).then_inc(s["mean_t"], 1)
            for i, (src, dst) in enumerate(turned_cuts):
                dve.wait_ge(s["high"], i + 1)
                dve.scalar_tensor_tensor(out=dst[1], in0=src, scalar=UP, in1=dst[0],
                                         op0=ALU.mult, op1=ALU.subtract).then_inc(s["low"], 1)
            dve.wait_ge(s["shift"], 1)
            dve.wait_ge(s["ones"], 6)
            dve.wait_ge(s["low"], len(turned_cuts))


def attention_phase(nc, dram, t, scratch, w, s):
    LAST = NB - 1
    with ExitStack() as ctx:

        def sb(name, shape, dt):
            return ctx.enter_context(nc.sbuf_tensor(name, shape, dt))

        context = sb("context", [P, RING, D], F32)
        xn = sb("xn", [P, 2, D], F32)
        mask_t = sb("mask_t", [P, 2, D], F32)
        qk = sb("qk", [P, 2, D], F32)
        part = sb("part", [P, 2, 3, D], BF16)
        rest1 = sb("rest1", [P, 2, D], F32)
        v_rows = sb("v_rows", [P, ST, P], F32)
        neg_max = sb("neg_max", [P, 2, ST * HEADS], F32)
        max_part = sb("max_part", [ST * HEADS, 3, P], BF16)
        max_rest = sb("max_rest", [ST * HEADS, 2, P], F32)
        probs = sb("probs", [P, 2, 4, ST, D], F32)
        out_sums = sb("out_sums", [P, 2, D], F32)
        inverse = sb("inverse", [P, D], F32)
        ratio = sb("ratio", [P, D], F32)
        masked = sb("masked", [P, D], F32)
        stage = sb("stage", [P, 2, STAGE], F32)
        stack, v_wide = t["stack"], t["v_wide"]

        def ps(name, shape):
            return ctx.enter_context(nc.psum_tensor(name, shape, F32))

        scores = ps("scores", [P, 2, 2 * D])
        scores_t = ps("scores_t", [P, 2, 2 * D])
        sums = ps("sums", [P, 2, 2, D])
        ps_qk = ps("ps_qk", [P, 2, D])
        ps_v = ps("ps_v", [P, 2 * D])
        for n in ["ctx_in0", "ctx_in1", "ctx_in2", "ctx_in3", "xn", "qk_mm", "qk_evac", "rest1", "part1", "part2", "parts_out",
                  "stack_in", "v_mm", "v_bias", "v_done", "max_mm", "max_done", "max_turned", "max_cut",
                  "max_out", "max_in", "score_mm", "prob_mm", "exp", "av_done",
                  "sums_evac", "inverse", "ratio", "masked", "x1", "mask_in0", "mask_in1", "piece_in0", "piece_in1",
                  "piece_scaled", "piece_high", "piece_low"]:
            s[n]
        block = ctx.enter_context(nc.Block())

        def on(n, j):
            return 0 <= n <= LAST if j is None else True

        def steps(eng, step):
            for k in range(-4, 4):
                step(k, k % RING, None)
            with eng.Fori(1, 3) as j:
                for r in range(RING):
                    step(j * RING + r, r, j)
            for k in range(12, 17):
                step(k, k % RING, None)

        def group(k, r, j, ahead):
            return (k + ahead) // RING if j is None else j + (r + ahead) // RING

        def half(k, r, j, ahead):
            return (k + ahead) // 2 if j is None else 2 * j + (r + ahead) // 2

        def head(u):
            return (u % 4) * 4 + u // 4

        def cut_count(i, c):
            return i + c + 1 + (2 if isinstance(i, int) and i == 9 else 0)

        @block.sync
        def _(sp):
            def step(k, r, j):
                piece = weight_piece(dram, w, stage, k, r, j)
                if piece is not None:
                    i, moves, _ = piece
                    wait_alone(sp, s["piece_low"], i + 1, s["seen"])
                    for dst, src in moves:
                        sp.dma_start(dst, src).then_inc(s[f"piece_in{r % 2}"], 16)
                n = k
                if on(n, j):
                    wait_alone(sp, s["masked"], n - 1, s["seen"])
                    sp.dma_start(mask_t[:, r % 2, :], dram["mask_Bx1x2048_fk1"][ds(n, 1)].rearrange("b o t -> (b o) t")
                                 .partition_broadcast(P)).then_inc(s[f"mask_in{r % 2}"], 16)
                n = k + 4
                if on(n, j):
                    if j is not None or k >= 0:
                        wait_alone(sp, s["v_mm"], k + 1, s["seen"])
                        wait_alone(sp, s["qk_mm"], k + 1, s["seen"])
                    sp.dma_start(context[:, r, :], dram["ctx_2048"][ds(n, 1)].rearrange("b c s -> (b c) s")).then_inc(s[f"ctx_in{r}"], 16)
                n = k + 1
                if on(n, j):
                    slot = (r + 1) % RING
                    wait_alone(sp, s["max_cut"], 4 * n + 4, s["seen"])
                    sp.dma_start(scratch["maxima"].rearrange("a h s t -> h s a t")[:, 0], max_part[0:HEADS]).then_inc(s["max_out"], 16)
                    sp.dma_start(scratch["maxima"].rearrange("a h s t -> h s a t")[:, 1], max_part[HEADS:2 * HEADS]).then_inc(s["max_out"], 16)
                    wait_alone(sp, s["max_out"], 32 * (n + 1), s["seen"])
                    sp.dma_start(stack[MAX_ROW:MAX_ROW + 3, slot, 0],
                                 scratch["maxima"].rearrange("a h s t -> a h (s t)")).then_inc(s["max_in"], 16)
                    wait_alone(sp, s["max_in"], 16 * (n + 1), s["seen"])

                n = k + 3
                if on(n, j):
                    slot = (r + 3) % RING
                    wait_alone(sp, s["part2"], n + 1, s["seen"])
                    wait_alone(sp, s["stack_in"], STACK_DMAS * 16 * n, s["seen"])
                    sp.dma_start(scratch["parts"].rearrange("e a d h t -> (d h) (e a) t"), part[:].rearrange("p e a t -> p (e a) t")).then_inc(s["parts_out"], 16)
                    wait_alone(sp, s["parts_out"], 16 * n + 16, s["seen"])
                    if j is not None or n >= RING:
                        wait_alone(sp, s["prob_mm"], 16 * (n - RING) + 16, s["seen"])
                    for i, m, a in SAME:
                        sp.dma_start(stack[i * HD:(i + m) * HD, slot, 0].rearrange("r h t -> r (h t)"),
                                     scratch["parts"][0, a].rearrange("d h t -> d (h t)").unsqueeze(0)
                                     .broadcast_to([m, HD, HEADS * D])).then_inc(s["stack_in"], 16)
                        sp.dma_start(stack[i * HD:(i + m) * HD, slot, 1].rearrange("r h t -> r (h t)"),
                                     scratch["parts"][1, 0:m].rearrange("a d h t -> (a d) (h t)")).then_inc(s["stack_in"], 16)
                    sp.dma_start(stack[MASK_ROW:MASK_ROW + 1, slot, 1],
                                 scratch["penalty"][ds(n, 1)].unsqueeze(1).broadcast_to([1, HEADS, D])).then_inc(s["stack_in"], 16)

            steps(sp, step)

        @block.tensor
        def _(pe):
            def values(g, piece, n, r):
                which, st = divmod(piece, ST)
                if piece == 0:
                    wait(pe, s["exp"], 16 * n + 4 * g + 4)
                    if g == 0:
                        wait(pe, s["sums_evac"], n - 1)
                        wait(pe, s["v_done"], n + 1)
                for q in range(4):
                    at = 32 + 32 * (4 * q + g) - HD * g
                    w = v_wide[:, r % 2, st, at:at + 32] if which == 0 else t["ones_wide"][:, g, :]
                    mm = pe.matmul(sums[32 * q:32 * q + 32, r % 2, which, :], w, probs[:, g % 2, q, st, :],
                                   start=(g == 0 and piece == 0), stop=(g == 3 and st == ST - 1), skip_group_check=True)
                if piece == 3:
                    mm.then_inc(s["av_done"], 1)

            def step(k, r, j):
                n = k + 3
                if on(n, j):
                    wait(pe, s["xn"], n + 1)
                    slot = (r + 3) % RING
                    wait(pe, s[f"ctx_in{slot}"], 16 * (group(k, r, j, 3) + 1))
                    wait(pe, s["qk_evac"], n)
                    pe.matmul(ps_qk[:, 0, :], t["w_qkv"][:, 0, :], xn[:, (r + 3) % 2, :], start=True, stop=True)
                    pe.matmul(ps_qk[:, 1, :], t["w_qkv"][:, 1, :], context[:, slot, :], start=True, stop=True).then_inc(s["qk_mm"], 1)
                for u in range(HEADS):
                    h = head(u)
                    if u >= 5 and on(k, j):
                        values((u - 5) // 4, (u - 5) % 4, k, r)
                    elif u < 5 and on(k - 1, j):
                        values(*((3, u - 1) if u else (2, 3)), k - 1, r + 3)
                    n = k + 2
                    if on(n, j):
                        if u == 0:
                            wait(pe, s["stack_in"], STACK_DMAS * 16 * (n + 1))
                        wait(pe, s["max_done"], 16 * n + u - 1)
                        slot = (r + 2) % RING
                        for tt in range(ST):
                            mm = pe.matmul(scores[:, u % 2, tt * D:(tt + 1) * D],
                                           stack[0:MASK_ROW + 1, slot, 0, h, tt * P:(tt + 1) * P],
                                           stack[0:MASK_ROW + 1, slot, 1, h, :], start=True, stop=True)
                        mm.then_inc(s["score_mm"], 1)
                    n = k
                    if on(n, j):
                        if u == 0:
                            wait(pe, s["max_in"], 16 * (n + 1))
                        wait(pe, s["exp"], 16 * n + u - 1)
                        for st in range(ST):
                            mm = pe.matmul(scores_t[:, u % 2, st * D:(st + 1) * D],
                                           stack[0:ROWS, r, 1, h, st * P:(st + 1) * P],
                                           stack[0:ROWS, r, 0, h, :], start=True, stop=True)
                        mm.then_inc(s["prob_mm"], 1)
                    n = k + 1
                    if on(n, j) and u == 1:
                        wait(pe, s["max_done"], 16 * (n + 1))
                        wait(pe, s["v_done"], n)
                        pe.transpose(ps_v[0:ST * HEADS, 256:256 + P], neg_max[:, (r + 1) % 2, :], t["ident"][:]).then_inc(s["max_turned"], 1)
                    if on(n, j) and u == 5:
                        wait(pe, s["max_cut"], 4 * n + 2)
                        for st in range(ST):
                            mm = pe.matmul(ps_v[:, st * P:(st + 1) * P], context[:, (r + 1) % RING, st * P:(st + 1) * P],
                                           t["w_qkv"][:, 2, :], start=True, stop=True)
                        mm.then_inc(s["v_mm"], 1)

            steps(pe, step)

        @block.scalar
        def _(act):
            def step(k, r, j):
                for u in range(HEADS):
                    n = k + 3
                    if u == 1 and on(n, j):
                        wait(act, s["qk_mm"], n + 1)
                        wait(act, s["parts_out"], 16 * n)
                        wait(act, s["rest1"], n)
                        for e in range(2):
                            act.activation(qk[:, e, :], ps_qk[:, e, :], ACT.Identity, bias=t["b_qk"][:, e:e + 1])
                            mm = act.activation(part[:, e, 0, :], ps_qk[:, e, :], ACT.Identity, bias=t["b_qk"][:, e:e + 1])
                        mm.then_inc(s["qk_evac"], 1)
                    n = k
                    if on(n, j):
                        wait(act, s["prob_mm"], 16 * n + u + 1)
                        if u % 4 == 0:
                            wait(act, s["av_done"], 4 * n + u // 4 - 1)
                        act.activation(probs[:, (u // 4) % 2, u % 4], scores_t[:, u % 2, :].rearrange("p (s t) -> p s t", s=ST),
                                       ACT.Exp, scale=HD ** -0.5).then_inc(s["exp"], 1)
                    n = k + 4
                    if u == 10 and on(n, j):
                        wait(act, s["qk_mm"], n - 1)
                        act.activation(xn[:, r % 2, :], t["x"][:, ds(n, 1), :].rearrange("p o d -> p (o d)"), ACT.Identity,
                                       scale=t["rstd"][:, ds(n, 1)], bias=t["shift"][:, ds(n, 1)]).then_inc(s["xn"], 1)
                    n = k - 1
                    if u == 5 and on(n, j):
                        wait(act, s["av_done"], 4 * n + 4)
                        wait(act, s["ratio"], n)
                        act.activation(out_sums[:], sums[:, (r + 3) % 2], ACT.Copy).then_inc(s["sums_evac"], 1)

                piece = weight_piece(dram, w, stage, k, r, j)
                if piece is not None:
                    i, moves, cuts = piece
                    turns = 2 * (j - 1) + r // 2 + 1 if j is not None else 4 + len(moves)
                    act.wait_ge(s[f"piece_in{r % 2}"], 16 * turns)
                    for src, dst, scale in cuts:
                        act.activation(src, src, ACT.Copy, scale=scale).then_inc(s["piece_scaled"], 1)
                    for c, (src, dst, scale) in enumerate(cuts):
                        act.wait_ge(s["piece_scaled"], cut_count(i, c))
                        act.activation(dst[0], src, ACT.Copy).then_inc(s["piece_high"], 1)

            steps(act, step)

        @block.vector
        def _(dve):
            def step(k, r, j):
                for u in range(HEADS):
                    n = k + 2
                    if on(n, j):
                        wait(dve, s["score_mm"], 16 * n + u + 1)
                        if u == 0:
                            wait(dve, s["max_turned"], n - 1)
                        h = head(u)
                        dve.tensor_reduce(neg_max[:, r % 2, h::HEADS],
                                          scores[:, u % 2, :].rearrange("p (s t) -> p s t", s=ST),
                                          AX.X, ALU.max, negate=True).then_inc(s["max_done"], 1)
                    n = k + 1
                    if on(n, j) and u == 2:
                        turned = ps_v[0:ST * HEADS, 256:256 + P]
                        wait(dve, s["max_turned"], n + 1)
                        wait(dve, s["max_out"], 32 * n)
                        dve.tensor_copy(max_part[:, 0, :], turned).then_inc(s["max_cut"], 1)
                        wait(dve, s["max_cut"], 4 * n + 1)
                        dve.tensor_tensor(max_rest[:, 0, :], turned, max_part[:, 0, :], ALU.subtract).then_inc(s["max_cut"], 1)
                        wait(dve, s["max_cut"], 4 * n + 2)
                        dve.tensor_copy(max_part[:, 1, :], max_rest[:, 0, :]).then_inc(s["max_cut"], 1)
                        wait(dve, s["max_cut"], 4 * n + 3)
                        dve.tensor_tensor(max_part[:, 2, :], max_rest[:, 0, :], max_part[:, 1, :], ALU.subtract).then_inc(s["max_cut"], 1)
                    n = k + 3
                    if on(n, j) and u == 3:
                        wait(dve, s["qk_evac"], n + 1)
                        wait(dve, s["part2"], n)
                        dve.tensor_tensor(rest1[:], qk[:], part[:, :, 0], ALU.subtract).then_inc(s["rest1"], 1)
                        wait(dve, s["rest1"], n + 1)
                        wait(dve, s["parts_out"], 16 * n)
                        dve.tensor_copy(part[:, :, 1], rest1[:]).then_inc(s["part1"], 1)
                    n = k + 1
                    if on(n, j) and u == 8:
                        slot = (r + 1) % 2
                        wait(dve, s["v_mm"], n + 1)
                        wait(dve, s["v_done"], n)
                        dve.tensor_tensor(v_rows[:], ps_v[:, 0:2 * P].rearrange("p (s c) -> p s c", s=ST),
                                          t["bv_rows"][:].unsqueeze(1).broadcast_to([P, ST, P]), ALU.add).then_inc(s["v_bias"], 1)
                        wait(dve, s["v_bias"], n + 1)
                        wait(dve, s["av_done"], 4 * (n - 2) + 4)
                        for st in range(ST):
                            dst = v_wide[:, slot, st, 32:].rearrange("p (h c) -> p h c", c=32)[:, :, 0:HD]
                            mm = dve.tensor_scalar(dst, v_rows[:, st, :].rearrange("p (h d) -> p h d", d=HD),
                                                   t["mask_cols"][:, st, ds(n, 1)], None, ALU.mult)
                        mm.then_inc(s["v_done"], 1)
                    n = k - 1
                    if on(n, j) and u == 12:
                        wait(dve, s["sums_evac"], n + 1)
                        wait(dve, s["ratio"], n)
                        dve.reciprocal(inverse[:], out_sums[:, 1, :]).then_inc(s["inverse"], 1)

            steps(dve, step)

        @block.gpsimd
        def _(pool):
            pool.sem_inc(s["piece_low"], 2)

            def step(k, r, j):
                n = k + 3
                if on(n, j):
                    wait(pool, s["part1"], n + 1)
                    wait(pool, s["parts_out"], 16 * n)
                    pool.tensor_tensor(part[:, :, 2], rest1[:], part[:, :, 1], ALU.subtract).then_inc(s["part2"], 1)
                n = k - 1
                if on(n, j):
                    wait(pool, s["inverse"], n + 1)
                    wait(pool, s["x1"], n)
                    pool.tensor_tensor(ratio[:], out_sums[:, 0, :], inverse[:], ALU.mult).then_inc(s["ratio"], 1)
                    wait(pool, s["ratio"], n + 1)
                    wait(pool, s[f"mask_in{(r + 3) % 2}"], 16 * (half(k, r, j, -1) + 1))
                    pool.tensor_tensor(masked[:], ratio[:], mask_t[:, (r + 3) % 2, :], ALU.mult).then_inc(s["masked"], 1)
                    wait(pool, s["masked"], n + 1)
                    x = t["x"][:, ds(n, 1), :].rearrange("p o d -> p (o d)")
                    pool.tensor_tensor(x, x, masked[:], ALU.add).then_inc(s["x1"], 1)

                piece = weight_piece(dram, w, stage, k, r, j)
                if piece is not None:
                    i, _, cuts = piece
                    for c, (src, dst, scale) in enumerate(cuts):
                        pool.wait_ge(s["piece_high"], cut_count(i, c))
                        pool.tensor_tensor(dst[1], src, dst[0], ALU.subtract).then_inc(s["piece_low"], 1)

            steps(pool, step)


def lasting_tensors(ctx, nc):
    def sb(name, shape, dt=F32):
        return ctx.enter_context(nc.sbuf_tensor(name, shape, dt))

    return {
        "x": sb("x", [P, NB, D]),
        "ident": sb("ident", [P, P]),
        "moments": sb("moments", [P, NB, 2]),
        "rstd": sb("rstd", [P, NB]),
    }


def attention_tensors(ctx, nc):
    def sb(name, shape, dt=F32):
        return ctx.enter_context(nc.sbuf_tensor(name, shape, dt))

    return {
        "b_qk": sb("b_qk", [P, 2]),
        "bv_rows": sb("bv_rows", [P, P]),
        "mask_cols": sb("mask_cols", [P, ST, NB]),
        "w_qkv": sb("w_qkv", [P, 3, P]),
        "stack": sb("stack", [ROWS, RING, 2, HEADS, D], BF16),
        "v_wide": sb("v_wide", [P, 2, ST, (HEADS + 1) * 32]),
        "ones_wide": sb("ones_wide", [P, 4, 32]),
        "shift": sb("shift", [P, NB]),
    }


def scratch_tensors(nc):
    def room(name, shape, dt):
        return nc.dram_tensor(name, shape, dt, kind="Internal").ap()

    return {
        "penalty": room("penalty_rows", [NB, D], BF16),
        "parts": room("parts_room", [2, 3, HD, HEADS, D], BF16),
        "maxima": room("maxima_room", [3, HEADS, ST, P], BF16),
        "summary": room("summary_room", [NB, D], F32),
    }


def weight_tensors(ctx, nc):
    def sb(name, shape, dt=F16):
        return ctx.enter_context(nc.sbuf_tensor(name, shape, dt))

    return {
        "w1": sb("w1", [P, 2, C, ROUTED_K * P]),
        "w2": sb("w2", [P, 2, ROUTED_K * D]),
        "ws1": sb("ws1", [P, 2, C, SHARED_F]),
        "ws2": sb("ws2", [P, 2, 3, D]),
        "table_down": sb("table_down", [P, 2, C, TABLE]),
        "centroids": sb("centroids", [P, 2, C, EXPERTS]),
        "query": sb("query", [P, 2, C, 2, P]),
        "keys": sb("keys", [P, 2, 2, KEYS]),
        "b2": sb("b2", [P, 2, D]),
        "b1": sb("b1", [P, ROUTED_K], F32),
        "bs1": sb("bs1", [P, 3], F32),
        "bs2": sb("bs2", [P, 2, D], F32),
        "router_bias": sb("router_bias", [P, EXPERTS], F32),
    }


STAGE = C * SHARED_F + 3 * D


def weight_piece(dram, w, stage, k, r, j):
    if j is not None:
        i = 4 * (j - 1) + r
        half = EXPERTS // 2 * FF
        v = stage[:, r % 2, 0:half]
        if r % 2 == 0:
            h, rows = r // 2, half // ROUTED_K
            src = dram["L0_ffn_routed_w1"].rearrange("e (p c) f -> c p e f", c=C)[ds(j - 1, 1)][:, :, h * EXPERTS // 2:(h + 1) * EXPERTS // 2]
            dst = [w["w1"][:, a, ds(j - 1, 1)].rearrange("p o (i q) -> p (o q) i", i=ROUTED_K)[:, h * rows:(h + 1) * rows] for a in range(2)]
            return i, [(v.rearrange("p (e f) -> p e f", f=FF), src.rearrange("o p e f -> (o p) e f"))], [(v.rearrange("p (q i) -> p q i", i=ROUTED_K), dst, UP)]
        part = ds((2 * (j - 1) + r // 2) * half, half)
        src = dram["L0_ffn_routed_w2"].rearrange("e f d -> (e f) d").rearrange("(p i) d -> p (i d)", p=P)
        return i, [(v, src[:, part])], [(v, [w["w2"][:, a, part] for a in range(2)], UP)]
    if k == 12:
        v = stage[:, 0, 0:C * SHARED_F]
        v4 = v.rearrange("p (c n f) -> p c n f", c=C, n=SHARED)
        src = dram["L0_ffn_shared_w1"].rearrange("n (p c) f -> c p n f", c=C)
        v2 = stage[:, 0, C * SHARED_F:].rearrange("p (k d) -> p k d", k=3)
        s2 = dram["L0_ffn_shared_w2"].rearrange("n f d -> (n f) d")
        m = SHARED_M[2]
        return 8, ([(v4[:, c], src[c]) for c in range(C)]
                   + [(v2[:, 0:2], s2[0:2 * P].rearrange("(k p) d -> p k d", p=P)), (v2[0:m, 2], s2[2 * P:SHARED_F])]), \
            [(v, [w["ws1"][:, a].rearrange("p c f -> p (c f)") for a in range(2)], UP),
             (v2[:, 0:2], [w["ws2"][:, a, 0:2] for a in range(2)], UP),
             (v2[0:m, 2], [w["ws2"][0:m, a, 2] for a in range(2)], UP)]
    if k == 13:
        small = stage[:, 1, 0:C * 2 * P + 2 * KEYS + D]
        q = small[:, 0:C * 2 * P]
        q4 = q.rearrange("p (c r m) -> p c r m", c=C, r=2)
        ky = small[:, C * 2 * P:C * 2 * P + 2 * KEYS].rearrange("p (s k) -> p s k", s=2)
        b2 = small[:, C * 2 * P + 2 * KEYS:]
        moves = []
        for half in range(2):
            for c in range(C):
                moves.append((q4[:, c, :, half * KDIM:(half + 1) * KDIM],
                              dram["L1_ffn_W_q"].rearrange("(p c) (r m) -> c p r m", c=C, r=2)[c]))
            moves.append((ky[half * KDIM:(half + 1) * KDIM], dram["L1_ffn_keys"].rearrange("s k n -> k s n")))
        moves.append((b2, dram["L0_ffn_routed_b2"].unsqueeze(1).broadcast_to([EXPERTS, P // EXPERTS, D])))
        return 9, moves, [(q, [w["query"][:, a].rearrange("p c r m -> p (c r m)") for a in range(2)], UP),
                          (ky, [w["keys"][:, a] for a in range(2)], UP),
                          (b2, [w["b2"][:, a] for a in range(2)], UP * EXPERTS / P)]
    return None


def mlp_tensors(ctx, nc):
    def sb(name, shape, dt=F16):
        return ctx.enter_context(nc.sbuf_tensor(name, shape, dt))

    return {
        "gate": sb("gate", [P, 2, C, INTER]),
        "up": sb("up", [P, 2, C, INTER]),
        "down": sb("down", [P, 2, INTER_K * D]),
        "table_up": sb("table_up", [P, 2, TABLE_K, D]),
        "gamma": sb("gamma", [P, D], F32),
        "beta": sb("beta", [P, D], F32),
    }


def norm_phase(nc, t, s, call):
    done = call * NB
    with ExitStack() as ctx:
        stats = ctx.enter_context(nc.sbuf_tensor(f"stats{call}", [P, NB, 6], F32))
        base = ctx.enter_context(nc.sbuf_tensor(f"base{call}", [P, NB], F32))
        power = ctx.enter_context(nc.sbuf_tensor(f"power{call}", [P, NB], F32))
        block = ctx.enter_context(nc.Block())

        @block.gpsimd
        def _(pool):
            pool.memset(power[:], -0.5).then_inc(s["power"], 1)
            pool.wait_ge(s["power"], call + 1)
            pool.wait_ge(s["base"], call + 1)
            pool.tensor_tensor(t["rstd"][:], base[:], power[:], ALU.pow).then_inc(s["rstd"], 1)

        @block.vector
        def _(dve):
            for b in range(NB):
                dve.bn_stats(stats[:, b, :], t["x"][:, b, :]).then_inc(s["stats"], 1)
            for b in range(NB):
                dve.wait_ge(s["stats"], done + b + 1)
                dve.bn_aggr(t["moments"][:, b, :], stats[:, b, :]).then_inc(s["moments"], 1)
            dve.wait_ge(s["moments"], done + NB)
            dve.tensor_scalar(base[:], t["moments"][:, :, 1], EPS, None, ALU.add).then_inc(s["base"], 1)
            dve.wait_ge(s["rstd"], call + 1)


def turn_phase(nc, t, w, x_t, s, call, router=None):
    done = call * NB
    with ExitStack() as ctx:
        normed = ctx.enter_context(nc.sbuf_tensor(f"normed{call}", [P, 2, D], F32))
        bias = ctx.enter_context(nc.sbuf_tensor(f"bias{call}", [P, D], F32))
        turned = ctx.enter_context(nc.psum_tensor(f"turned{call}", [P, 2, C, D], F32))
        block = ctx.enter_context(nc.Block())

        @block.vector
        def _(dve):
            if router is not None:
                dve.tensor_tensor(bias[:], w["bs2"][:, 0], w["bs2"][:, 1], ALU.add).then_inc(s["bias"], 1)
            for b in range(NB + 1):
                if b < NB:
                    if b >= 2:
                        dve.wait_ge(s["turned"], done + b - 1)
                    if router is not None:
                        wait(dve, s["based"], b - 1)
                    dve.tensor_scalar(normed[:, b % 2], t["x"][:, b, :], t["moments"][:, b, 0:1], t["rstd"][:, b:b + 1],
                                      ALU.subtract, ALU.mult).then_inc(s["normed"], 1)
                if b > 0:
                    n = b - 1
                    dve.wait_ge(s["high"], done + n + 1)
                    dve.tensor_tensor(x_t[:, 1, :, n * P:(n + 1) * P], turned[:, n % 2, :, 0:P],
                                      x_t[:, 0, :, n * P:(n + 1) * P], ALU.subtract).then_inc(s["low"], 1)
            dve.wait_ge(s["low"], done + NB)

        @block.scalar
        def _(act):
            for b in range(NB):
                act.wait_ge(s["turned"], done + b + 1)
                act.activation(x_t[:, 0, :, b * P:(b + 1) * P], turned[:, b % 2, :, 0:P], ACT.Copy).then_inc(s["high"], 1)

        @block.gpsimd
        def _(pool):
            if router is not None:
                pool.wait_ge(s["bias"], 1)
                for b in range(NB):
                    pool.wait_ge(s["normed"], b + 1)
                    pool.tensor_tensor(t["x"][:, b, :], t["x"][:, b, :], bias[:], ALU.add).then_inc(s["biased"], 1)
                    pool.wait_ge(s["biased"], b + 1)
                    pool.tensor_tensor(t["x"][:, b, :], t["x"][:, b, :], normed[:, b % 2, :], ALU.add).then_inc(s["based"], 1)
                pool.wait_ge(s["based"], NB)

        @block.tensor
        def _(pe):
            for b in range(NB + 1):
                if b < NB:
                    if b >= 2:
                        pe.wait_ge(s["low"], done + b - 1)
                    pe.wait_ge(s["normed"], done + b + 1)
                    for c in range(C):
                        turn = pe.transpose(turned[:, b % 2, c, 0:P], normed[:, b % 2, c::C], t["ident"][:])
                    turn.then_inc(s["turned"], 1)
                if b > 0 and router is not None:
                    n = b - 1
                    pe.wait_ge(s["low"], n + 1)
                    products = [(a, b2, c) for a, b2 in HIGH_LOW for c in range(C)]
                    for i, (a, b2, c) in enumerate(products):
                        mm = pe.matmul(router[:, n, :], x_t[:, a, c, n * P:(n + 1) * P], w["centroids"][:, b2, c, :],
                                       start=(i == 0), stop=(i == len(products) - 1))
                    mm.then_inc(s["router"], 1)
            if router is not None:
                pe.wait_ge(s["router"], NB)


def gating_phase(nc, t, w, router, gates):
    with ExitStack() as ctx:
        s = Sems(ctx, nc, "gating")

        def sb(name, shape, dt=F32):
            return ctx.enter_context(nc.sbuf_tensor(name, shape, dt))

        sig = sb("sig", [P, NB, EXPERTS])
        score = sb("score", [P, NB, EXPERTS])
        best = sb("best", [P, NB, 8])
        place = sb("place", [P, NB, 8], U32)
        place_f = sb("place_f", [P, NB, TOP])
        number = sb("number", [P, EXPERTS])
        hit = sb("hit", [P, NB, TOP, EXPERTS])
        member = sb("member", [P, NB, EXPERTS])
        kept = sb("kept", [P, NB, EXPERTS])
        total = sb("total2", [P, NB])
        floor = sb("floor", [P, NB])
        inverse = sb("inverse2", [P, NB])
        gate = sb("gate_rows", [P, NB, EXPERTS, P // EXPERTS])
        turned = ctx.enter_context(nc.psum_tensor("turned_gates", [P, 4, 4, P], F32))
        for n in ["sig", "score", "best", "place", "number", "step", "gate", "turned", "out"]:
            s[n]
        block = ctx.enter_context(nc.Block())

        @block.gpsimd
        def _(pool):
            pool.iota(number[:], [[1, EXPERTS]], base=0, channel_multiplier=0, allow_small_or_imprecise_dtypes=True).then_inc(s["number"], 1)
            pool.wait_ge(s["number"], 1)

        @block.scalar
        def _(act):
            act.activation(sig[:], router[:], ACT.Sigmoid, scale=DOWN).then_inc(s["sig"], 1)
            for i in range(4):
                act.wait_ge(s["turned"], i + 1)
                act.activation(gates[:, i * CHUNK:(i + 1) * CHUNK], turned[:, i].rearrange("p b m -> p (b m)"), ACT.Copy).then_inc(s["out"], 1)
            act.wait_ge(s["out"], 4)

        @block.vector
        def _(dve):
            dve.wait_ge(s["sig"], 1)
            dve.tensor_tensor(score[:], sig[:], w["router_bias"][:].unsqueeze(1).broadcast_to([P, NB, EXPERTS]), ALU.add).then_inc(s["score"], 1)
            dve.wait_ge(s["score"], 1)
            for b in range(NB):
                dve.max(best[:, b, :], score[:, b, :]).then_inc(s["best"], 1)
            for b in range(NB):
                dve.wait_ge(s["best"], b + 1)
                dve.max_index(place[:, b, :], best[:, b, :], score[:, b, :]).then_inc(s["place"], 1)
            dve.wait_ge(s["place"], NB)
            dve.tensor_copy(place_f[:], place[:, :, 0:TOP]).then_inc(s["step"], 1)
            dve.wait_ge(s["step"], 1)
            dve.wait_ge(s["number"], 1)
            for j in range(TOP):
                dve.tensor_tensor(hit[:, :, j, :], number[:].unsqueeze(1).broadcast_to([P, NB, EXPERTS]),
                                  place_f[:, :, j:j + 1].broadcast_to([P, NB, EXPERTS]), ALU.is_equal).then_inc(s["step"], 1)
            dve.wait_ge(s["step"], TOP + 1)
            dve.tensor_reduce(member[:], hit[:].rearrange("p b j e -> p b e j"), AX.X, ALU.add).then_inc(s["step"], 1)
            dve.wait_ge(s["step"], TOP + 2)
            dve.tensor_tensor(kept[:], score[:], member[:], ALU.mult).then_inc(s["step"], 1)
            dve.wait_ge(s["step"], TOP + 3)
            dve.tensor_reduce(total[:], kept[:], AX.X, ALU.add).then_inc(s["step"], 1)
            dve.wait_ge(s["step"], TOP + 4)
            dve.tensor_scalar(floor[:], total[:], 1e-8, None, ALU.max).then_inc(s["step"], 1)
            dve.wait_ge(s["step"], TOP + 5)
            dve.reciprocal(inverse[:], floor[:]).then_inc(s["step"], 1)
            dve.wait_ge(s["step"], TOP + 6)
            for b in range(NB):
                dve.tensor_scalar(gate[:, b], kept[:, b, :].unsqueeze(2).broadcast_to([P, EXPERTS, P // EXPERTS]),
                                  inverse[:, b:b + 1], None, ALU.mult).then_inc(s["gate"], 1)

        @block.tensor
        def _(pe):
            for b in range(NB):
                pe.wait_ge(s["gate"], b + 1)
                turn = pe.transpose(turned[:, b // 4, b % 4, :], gate[:, b].rearrange("p e r -> p (e r)"), t["ident"][:])
                if b % 4 == 3:
                    turn.then_inc(s["turned"], 1)


def experts_phase(nc, dram, t, w, x_t, gates, scratch):
    UNITS = 3 + ROUTED_K
    AHEAD = 3
    with ExitStack() as ctx:
        s = Sems(ctx, nc, "moe")

        def sb(name, shape, dt=F32):
            return ctx.enter_context(nc.sbuf_tensor(name, shape, dt))

        relu = sb("relu", [P, 4, CHUNK])
        gated = sb("gated", [P, 3, CHUNK])
        hidden = sb("hidden", [P, 4, 2, CHUNK], F16)
        gate_part = sb("gate_part", [P, 2, TOKENS], F16)
        sums = sb("sums_all", [P, NB, D])
        y = sb("y", [P, TILES, D])
        stats = sb("mix_stats", [P, 3, TILES, 6])
        moments = sb("mix_moments", [P, 3, TILES, 2])
        base = sb("mix_base", [P, 3, TILES])
        rstd = sb("mix_rstd", [P, 2, TILES])
        power = sb("mix_power", [P, 1])
        QUARTER = INTER // 4
        stage = sb("stage2", [P, 2 * C * QUARTER + INTER_K * D // 4 + D])
        ps_h = ctx.enter_context(nc.psum_tensor("ps_h", [P, 4, CHUNK], F32))
        ps_o = ctx.enter_context(nc.psum_tensor("ps_o", [P, TILES, 2 * D], F32))
        for n in ["gate_high", "gate_low", "up_mm", "relu", "gated", "high", "low", "down_mm", "added",
                  "rows_in", "power", "stats", "moments", "base", "rstd", "y", "beta", "mixed", "kept",
                  "mlp_in", "mlp_high", "mlp_low", "seen", "dve_seen"]:
            s[n]
        block = ctx.enter_context(nc.Block())

        def mlp_quarter(j):
            moves, cuts = [], []
            for k, name in enumerate(("gate", "up")):
                v = stage[:, k * C * QUARTER:(k + 1) * C * QUARTER].rearrange("p (c f) -> p c f", c=C)
                moves.append((v, dram[f"L1_ffn_{name}_w"].rearrange("(p c) f -> p c f", c=C)[:, :, ds(j * QUARTER, QUARTER)]))
                for c in range(C):
                    dst = [w[name][:, a, c].rearrange("p (i h q) -> p h q i", i=INTER_K, h=4)[:, ds(j, 1)]
                           .rearrange("p h q i -> p (h q) i") for a in range(2)]
                    cuts.append((v[:, c].rearrange("p (q i) -> p q i", i=INTER_K), dst))
            at, n = 2 * C * QUARTER, INTER_K * D // 4
            v = stage[:, at:at + n]
            moves.append((v, dram["L1_ffn_down_w"].rearrange("(p i) d -> p (i d)", p=P)[:, ds(j * n, n)]))
            cuts.append((v, [w["down"][:, a, ds(j * n, n)] for a in range(2)]))
            v = stage[:, at + n:at + n + D]
            moves.append((v, dram["L1_ffn_up_embed"].rearrange("(k p) d -> k p d", p=P)[ds(j, 1)].rearrange("k p d -> (k p) d")))
            cuts.append((v, [w["table_up"][:, a, ds(j, 1)].rearrange("p k d -> p (k d)") for a in range(2)]))
            return moves, cuts

        MLP_CUTS = 2 * C + 2
        CUTS_AT = {21: range(0, C), 22: range(C, 2 * C), 23: range(2 * C, 2 * C + 1), 24: range(2 * C + 1, MLP_CUTS)}

        def stage_order(i, b):
            if isinstance(b, int) and b >= NB - TILES:
                return 3 * (NB - TILES) + i * TILES + b - (NB - TILES)
            return 3 * b + i

        def y_order(b, i):
            if isinstance(b, int) and b >= NB - TILES:
                q = b - (NB - TILES)
                return 3 * (NB - TILES) + (2 * q + i if i < 2 else 2 * TILES + q)
            return 3 * b + i

        def row(x, b):
            return x[:, b, :] if isinstance(b, int) else x[:, ds(b, 1), :].rearrange("p o d -> p (o d)")

        class Tile:

            def __init__(self, j, base, v):
                self.n = j * UNITS + v * 3 + base
                self.buf = (base - 1) % 3 if base else 3
                self.rows = P if base >= 3 else SHARED_M[base]
                self.shared = base if base < 3 else None
                self.routed = v * 3 + (base - 3) if base >= 3 else None

        def tiles(eng, j, body, mix=None):
            for base in range(3):
                body(base, 0)
            if mix is not None:
                with eng.Fori(0, TILES) as v:
                    for base in range(3, 6):
                        body(base, v)
                        mix(base - 3, (j - 1) * TILES + v, 0)
            with eng.Fori(TILES if mix is not None else 0, 6) as v:
                for base in range(3, 6):
                    body(base, v)
            for base in range(21, UNITS):
                body(base, 0)

        @block.sync
        def _(sp):
            sp.dma_start(sums[:], scratch["summary"].partition_broadcast(P)).then_inc(s["rows_in"], 16)
            for name in ("gamma", "beta"):
                sp.dma_start(w[name][:], dram["L1_xattn_" + name].partition_broadcast(P)).then_inc(s["rows_in"], 16)
            with sp.Fori(0, CHUNKS) as j:
                wait_alone(sp, s["mlp_low"], (j + 1) * MLP_CUTS, s["seen"])
                for dst, src in mlp_quarter(j)[0]:
                    sp.dma_start(dst, src).then_inc(s["mlp_in"], 16)

        @block.tensor
        def _(pe):
            pe.wait_ge(s["gate_low"], 1)
            pe.sem_inc(s["down_mm"], AHEAD)

            def up(i, j):
                pe.wait_ge(s["relu"], i.n + 1)
                m = i.rows
                for k, (a, b) in enumerate(HIGH_LOW):
                    for c in range(C):
                        if i.shared is None:
                            lhs = w["w1"][:, a, c, ds(i.routed * P, P)]
                        else:
                            lhs = w["ws1"][:, a, c, i.shared * P:i.shared * P + m]
                        mm = pe.matmul(ps_h[0:m, i.buf, :], lhs, x_t[:, b, c, ds(j * CHUNK, CHUNK)],
                                       start=(k == 0 and c == 0), stop=(k == 2 and c == C - 1))
                mm.then_inc(s["up_mm"], 1)

            def down(i, j, first=False, last=False):
                pe.wait_ge(s["low"], i.n + 1 + AHEAD)
                m = i.rows
                for q in range(TILES):
                    if first:
                        for k, (a, b) in enumerate(HIGH_LOW):
                            pe.matmul(ps_o[:, q, 0:D], gate_part[:, a, ds(j * CHUNK + q * P, P)], w["b2"][:, b, :],
                                      start=(k == 0), stop=False, skip_group_check=True)
                    for k, (a, b) in enumerate(HIGH_LOW):
                        rhs = w["w2"][:, b, ds(i.routed * D, D)] if i.shared is None else w["ws2"][0:m, b, i.shared, :]
                        mm = pe.matmul(ps_o[:, q, 0:D], hidden[0:m, i.buf, a, q * P:(q + 1) * P], rhs,
                                       start=False, stop=(last and k == 2), skip_group_check=True)
                mm.then_inc(s["down_mm"], 1)

            with pe.Fori(0, CHUNKS) as j:
                up(Tile(j, 0, 0), j)
                up(Tile(j, 1, 0), j)

                def body(base, v):
                    if base + 2 < UNITS:
                        up(Tile(j, base + 2, v), j)
                    if base == 0:
                        pe.wait_ge(s["added"], j * TILES + 1)
                    down(Tile(j, base, v), j, first=(base == 0), last=(base == UNITS - 1))

                tiles(pe, j, body)

        @block.scalar
        def _(act):
            act.activation(gate_part[:, 0, :], gates[:], ACT.Copy).then_inc(s["gate_high"], 1)
            act.sem_inc(s["relu"], AHEAD)

            def relu_of(i):
                act.wait_ge(s["up_mm"], i.n + 1)
                act.wait_ge(s["low"], i.n + 1)
                m = i.rows
                bias = w["bs1"][0:m, i.shared:i.shared + 1] if i.shared is not None else w["b1"][:, ds(i.routed, 1)]
                act.activation(relu[0:m, i.buf, :], ps_h[0:m, i.buf, :], ACT.Relu, bias=bias, scale=DOWN).then_inc(s["relu"], 1)

            def high(i, j):
                m = i.rows
                act.wait_ge(s["down_mm"], i.n + 1)
                if i.shared is None:
                    act.wait_ge(s["gated"], j * ROUTED_K + i.routed + 1)
                else:
                    act.wait_ge(s["relu"], i.n + 1 + AHEAD)
                src = gated if i.shared is None else relu
                act.activation(hidden[0:m, i.buf, 0, :], src[0:m, i.buf, :], ACT.Copy).then_inc(s["high"], 1)

            with act.Fori(0, CHUNKS) as j:
                relu_of(Tile(j, 0, 0))

                def body(base, v):
                    if base + 1 < UNITS:
                        relu_of(Tile(j, base + 1, v))
                    high(Tile(j, base, v), j)
                    for c in CUTS_AT.get(base, ()):
                        act.wait_ge(s["mlp_in"], 64 * (j + 1))
                        src, dst = mlp_quarter(j)[1][c]
                        act.activation(dst[0], src, ACT.Copy, scale=UP).then_inc(s["mlp_high"], 1)

                tiles(act, j, body)

        @block.vector
        def _(dve):
            dve.wait_ge(s["gate_high"], 1)
            dve.tensor_tensor(gate_part[:, 1, :], gates[:], gate_part[:, 0, :], ALU.subtract).then_inc(s["gate_low"], 1)

            def mix(stage, b, q):
                def take_moments(i, rows):
                    dve.bn_stats(stats[:, i, q, :], rows).then_inc(s["stats"], 1)
                    wait_alone(dve, s["stats"], order(i) + 1, s["dve_seen"])
                    dve.bn_aggr(moments[:, i, q, :], stats[:, i, q, :]).then_inc(s["moments"], 1)
                    dve.wait_ge(s["moments"], order(i) + 1)
                    dve.tensor_scalar(base[:, i, q:q + 1], moments[:, i, q, 1:2], EPS, None, ALU.add).then_inc(s["base"], 1)

                def order(i):
                    return stage_order(i, b)

                x, yq = row(t["x"], b), y[:, q, :]
                if stage == 0:
                    wait_alone(dve, s["added"], b + 2, s["dve_seen"])
                    take_moments(0, x)
                elif stage == 1:
                    dve.wait_ge(s["rstd"], order(0) + 1)
                    dve.tensor_scalar(yq, x, moments[:, 0, q, 0:1], rstd[:, 0, q:q + 1], ALU.subtract, ALU.mult).then_inc(s["y"], 1)
                    dve.wait_ge(s["y"], y_order(b, 0) + 1)
                    dve.tensor_tensor(yq, yq, row(sums, b), ALU.add).then_inc(s["y"], 1)
                    dve.wait_ge(s["y"], y_order(b, 1) + 1)
                    take_moments(1, yq)
                else:
                    dve.wait_ge(s["rstd"], order(1) + 1)
                    dve.scalar_tensor_tensor(out=yq, in0=yq, scalar=moments[:, 1, q, 0:1], in1=w["gamma"][:],
                                             op0=ALU.subtract, op1=ALU.mult).then_inc(s["y"], 1)
                    dve.wait_ge(s["y"], y_order(b, 2) + 1)
                    dve.wait_ge(s["beta"], b + 1)
                    dve.scalar_tensor_tensor(out=x, in0=yq, scalar=rstd[:, 1, q:q + 1], in1=x,
                                             op0=ALU.mult, op1=ALU.add).then_inc(s["mixed"], 1)
                    wait_alone(dve, s["mixed"], b + 1, s["dve_seen"])
                    take_moments(2, x)
                    dve.tensor_copy(row(t["moments"], b), moments[:, 2, q, :]).then_inc(s["kept"], 1)

            def chunk(j, mixes):
                def body(base, v):
                    i = Tile(j, base, v)
                    if i.shared is None:
                        dve.wait_ge(s["relu"], i.n + 1 + AHEAD)
                        dve.wait_ge(s["low"], i.n + 1)
                        dve.tensor_tensor(gated[:, i.buf, :], relu[:, i.buf, :], gates[:, ds(j * CHUNK, CHUNK)],
                                          ALU.mult).then_inc(s["gated"], 1)
                    for c in CUTS_AT.get(base, ()):
                        dve.wait_ge(s["mlp_high"], MLP_CUTS * j + c + 1)
                        src, dst = mlp_quarter(j)[1][c]
                        dve.scalar_tensor_tensor(out=dst[1], in0=src, scalar=UP, in1=dst[0],
                                                 op0=ALU.mult, op1=ALU.subtract).then_inc(s["mlp_low"], 1)

                tiles(dve, j, body, mixes)
                dve.wait_ge(s["down_mm"], j * UNITS + (UNITS + AHEAD))
                for q in range(TILES):
                    x = row(t["x"], j * TILES + q)
                    dve.scalar_tensor_tensor(out=x, in0=ps_o[:, q, 0:D], scalar=DOWN, in1=x,
                                             op0=ALU.mult, op1=ALU.add).then_inc(s["added"], 1)

            dve.wait_ge(s["rows_in"], 48)
            chunk(0, None)
            with dve.Fori(1, CHUNKS) as j:
                chunk(j, mix)
            for stage_ in range(3):
                for q in range(TILES):
                    mix(stage_, NB - TILES + q, q)
            dve.wait_ge(s["kept"], NB)
            dve.wait_ge(s["rstd"], 3 * NB)
            dve.wait_ge(s["mlp_low"], MLP_CUTS * (CHUNKS + 1))

        @block.gpsimd
        def _(pool):
            pool.sem_inc(s["low"], AHEAD)
            pool.sem_inc(s["added"], 1)

            pool.sem_inc(s["mlp_low"], MLP_CUTS)
            pool.memset(power[:], -0.5).then_inc(s["power"], 1)
            pool.wait_ge(s["power"], 1)
            pool.wait_ge(s["rows_in"], 48)

            def mix(stage, b, q):
                if stage == 1:
                    x = row(t["x"], b)
                    pool.wait_ge(s["y"], y_order(b, 0) + 1)
                    pool.tensor_tensor(x, x, w["beta"][:], ALU.add).then_inc(s["beta"], 1)
                out = rstd[:, stage, q:q + 1] if stage < 2 else t["rstd"][:, ds(b, 1)]
                pool.wait_ge(s["base"], stage_order(stage, b) + 1)
                pool.tensor_tensor(out, base[:, stage, q:q + 1], power[:], ALU.pow).then_inc(s["rstd"], 1)

            def chunk(j, mixes):
                def body(base, v):
                    i = Tile(j, base, v)
                    pool.wait_ge(s["high"], i.n + 1)
                    src = gated if i.shared is None else relu
                    pool.tensor_tensor(hidden[0:i.rows, i.buf, 1, :], src[0:i.rows, i.buf, :], hidden[0:i.rows, i.buf, 0, :],
                                       ALU.subtract).then_inc(s["low"], 1)

                tiles(pool, j, body, mixes)

            chunk(0, None)
            with pool.Fori(1, CHUNKS) as j:
                chunk(j, mix)
            for stage_ in range(3):
                for q in range(TILES):
                    mix(stage_, NB - TILES + q, q)


def query_phase(nc, t, w, x_t, routing):
    SETS = 2 * TOKENS // P
    with ExitStack() as ctx:
        s = Sems(ctx, nc, "query")
        q = ctx.enter_context(nc.sbuf_tensor("q_line", [P, 2 * TOKENS], F16))
        ps_q = ctx.enter_context(nc.psum_tensor("ps_q", [P, 2, CHUNK], F32))
        ps_r = ctx.enter_context(nc.psum_tensor("ps_r", [P, 4, CHUNK], F32))
        for n in ["query_mm", "high", "low", "key_mm", "out"]:
            s[n]
        block = ctx.enter_context(nc.Block())
        line = q[:].rearrange("p (n r) -> p r n", r=2)

        @block.tensor
        def _(pe):
            for n in range(2 * CHUNKS):
                j, r = n // 2, n % 2
                wait(pe, s["low"], n - 1)
                for k, (a, b) in enumerate(HIGH_LOW):
                    for c in range(C):
                        mm = pe.matmul(ps_q[:, n % 2, :], w["query"][:, a, c, r, :], x_t[:, b, c, j * CHUNK:(j + 1) * CHUNK],
                                       start=(k == 0 and c == 0), stop=(k == 2 and c == C - 1))
                mm.then_inc(s["query_mm"], 1)
            pe.wait_ge(s["low"], 2 * CHUNKS)
            for n in range(SETS):
                for a in range(2):
                    mm = pe.matmul(ps_r[:, n // 8, (n % 8) * KEYS:(n % 8 + 1) * KEYS], q[:, n * P:(n + 1) * P],
                                   w["keys"][:, a, n // NB, :], start=(a == 0), stop=(a == 1))
                if n % 8 == 7:
                    mm.then_inc(s["key_mm"], 1)

        @block.scalar
        def _(act):
            for n in range(2 * CHUNKS):
                j, r = n // 2, n % 2
                act.wait_ge(s["query_mm"], n + 1)
                act.activation(line[:, r, j * CHUNK:(j + 1) * CHUNK], ps_q[:, n % 2, :], ACT.Copy, scale=DOWN).then_inc(s["high"], 1)
            act.wait_ge(s["high"], 2 * CHUNKS)
            for n in range(4):
                act.wait_ge(s["key_mm"], n + 1)
                act.activation(routing[:, n * 8:(n + 1) * 8, :], ps_r[:, n, :].rearrange("p (g k) -> p g k", g=8),
                               ACT.Copy, scale=DOWN).then_inc(s["out"], 1)
            act.wait_ge(s["out"], 4)

        @block.vector
        def _(dve):
            for n in range(2 * CHUNKS):
                j, r = n // 2, n % 2
                dve.wait_ge(s["high"], n + 1)
                part = line[KDIM:P, r, j * CHUNK:(j + 1) * CHUNK]
                dve.scalar_tensor_tensor(out=part, in0=ps_q[KDIM:P, n % 2, :], scalar=DOWN, in1=part,
                                         op0=ALU.mult, op1=ALU.subtract).then_inc(s["low"], 1)
            dve.wait_ge(s["low"], 2 * CHUNKS)


def retrieval_phase(nc, t, w, routing, picks, inverse):
    with ExitStack() as ctx:
        s = Sems(ctx, nc, "retrieve")

        def sb(name, shape, dt=F32):
            return ctx.enter_context(nc.sbuf_tensor(name, shape, dt))

        best = sb("best_keys", [P, 2 * NB, 8])
        pairs = sb("pairs", [P, NB, 8, 8])
        top = sb("top", [P, NB, 8])
        lowered = sb("lowered", [P, NB, 8])
        exps = sb("exps", [P, NB, 8])
        neg = sb("neg", [P, NB])
        total = sb("total3", [P, NB])
        listed = sb("listed", [P, NB])
        dense = sb("dense", [P, 2, 8, KEYS])
        dense_exp = sb("dense_exp", [P, 2, TABLE])
        for n in ["best", "pairs", "top", "neg", "lowered", "exps", "total", "inverse", "dense", "dense_exp", "picks", "last"]:
            s[n]
        block = ctx.enter_context(nc.Block())

        @block.vector
        def _(dve):
            for n in range(2 * NB):
                dve.max(best[:, n, :], routing[:, n, :]).then_inc(s["best"], 1)
            dve.wait_ge(s["best"], 2 * NB)
            for i in range(8):
                dve.tensor_tensor(pairs[:, :, i, :], best[:, NB:2 * NB, :], best[:, 0:NB, i:i + 1].broadcast_to([P, NB, 8]),
                                  ALU.add).then_inc(s["pairs"], 1)
            dve.wait_ge(s["pairs"], 8)
            for b in range(NB):
                dve.max(top[:, b, :], pairs[:, b]).then_inc(s["top"], 1)
            dve.wait_ge(s["top"], NB)
            dve.tensor_scalar(neg[:], top[:, :, 0], -1.0, None, ALU.mult).then_inc(s["neg"], 1)
            dve.tensor_tensor(lowered[:], top[:], top[:, :, 0:1].broadcast_to([P, NB, 8]), ALU.subtract).then_inc(s["lowered"], 1)
            dve.wait_ge(s["exps"], 1)
            dve.tensor_reduce(total[:], exps[:], AX.X, ALU.add).then_inc(s["total"], 1)
            dve.wait_ge(s["total"], 1)
            dve.reciprocal(inverse[:], total[:]).then_inc(s["inverse"], 1)
            for b in range(NB + 1):
                if b < NB:
                    wait(dve, s["picks"], b - 1)
                    dve.tensor_tensor(dense[:, b % 2], routing[:, b, 0:8].unsqueeze(2).broadcast_to([P, 8, KEYS]),
                                      routing[:, NB + b, :].unsqueeze(1).broadcast_to([P, 8, KEYS]), ALU.add).then_inc(s["dense"], 1)
                if b > 0:
                    n = b - 1
                    dve.wait_ge(s["dense_exp"], n + 1)
                    flat = dense[:, n % 2].rearrange("p i j -> p (i j)")
                    dve.scalar_tensor_tensor(out=picks[:, n, 0:TABLE - 1], in0=flat[:, 0:TABLE - 1], scalar=top[:, n, 7:8],
                                             in1=dense_exp[:, n % 2, 0:TABLE - 1], op0=ALU.is_ge, op1=ALU.mult,
                                             accum_out=listed[:, n:n + 1]).then_inc(s["picks"], 1)
            dve.wait_ge(s["picks"], NB)
            dve.tensor_tensor(picks[:, :, TABLE - 1], total[:], listed[:], ALU.subtract).then_inc(s["last"], 1)
            dve.wait_ge(s["last"], 1)
            dve.wait_ge(s["inverse"], 1)

        @block.scalar
        def _(act):
            act.wait_ge(s["lowered"], 1)
            act.activation(exps[:], lowered[:], ACT.Exp).then_inc(s["exps"], 1)
            for b in range(NB):
                act.wait_ge(s["dense"], b + 1)
                wait(act, s["picks"], b - 1)
                act.activation(dense_exp[:, b % 2, :], dense[:, b % 2].rearrange("p i j -> p (i j)"), ACT.Exp,
                               bias=neg[:, b:b + 1]).then_inc(s["dense_exp"], 1)


def ffn_phase(nc, dram, t, w, x_t, picks, inverse):
    with ExitStack() as ctx:
        s = Sems(ctx, nc, "ffn")

        def sb(name, shape, dt=F32):
            return ctx.enter_context(nc.sbuf_tensor(name, shape, dt))

        act_g = sb("act_g", [P, 2, CHUNK])
        prod = sb("prod", [P, 2, CHUNK])
        hidden = sb("hidden2", [P, 2, 2, CHUNK], F16)
        act_e = sb("act_e", [P, 2, TABLE])
        weight = sb("weight2", [P, 2, TABLE])
        weight_t = sb("weight_t", [P, 2, 2, TABLE_K, P], F16)
        ps_g = ctx.enter_context(nc.psum_tensor("ps_g", [P, 2, 2, CHUNK], F32))
        ps_e = ctx.enter_context(nc.psum_tensor("ps_e", [P, 2, TABLE], F32))
        ps_o = ctx.enter_context(nc.psum_tensor("ps_out", [P, TILES // 2, 2, D], F32))
        for n in ["gate_mm", "up_mm", "act_g", "prod", "high", "low", "down_mm", "table_mm", "act_e", "weight",
                  "turned", "wt_high", "wt_low", "row_mm", "added", "stored"]:
            s[n]
        block = ctx.enter_context(nc.Block())
        K = INTER_K

        @block.tensor
        def _(pe):
            def product(out, lhs, rhs, start, stop):
                for k, (a, b) in enumerate(HIGH_LOW):
                    for c in range(C):
                        mm = pe.matmul(out, lhs(a, c), rhs(b, c), start=(start and k == 0 and c == 0), stop=(stop and k == 2 and c == C - 1))
                return mm

            def up(i, j):
                n = j * K + i
                pe.wait_ge(s["prod"], n + 1)
                for which, name in ((0, "gate"), (1, "up")):
                    product(ps_g[:, i % 2, which, :], lambda a, c: w[name][:, a, c, i * P:(i + 1) * P],
                            lambda b, c: x_t[:, b, c, ds(j * CHUNK, CHUNK)], True, True).then_inc(s[name + "_mm"], 1)

            def down(i, j):
                n = j * K + i
                pe.wait_ge(s["low"], n + 2)
                if i == 0:
                    pe.wait_ge(s["added"], j * TILES + 1)
                for q in range(TILES):
                    for k, (a, b) in enumerate(HIGH_LOW):
                        mm = pe.matmul(ps_o[:, q // 2, q % 2, :], hidden[:, i % 2, a, q * P:(q + 1) * P],
                                       w["down"][:, b, i * D:(i + 1) * D], start=(i == 0 and k == 0 and q % 2 == 0),
                                       stop=False, skip_group_check=True)
                mm.then_inc(s["down_mm"], 1)

            def table(q, j):
                n = j * TILES + q
                pe.wait_ge(s["wt_low"], n + 1)
                product(ps_e[:, q % 2, :], lambda a, c: x_t[:, a, c, ds(j * CHUNK + q * P, P)],
                        lambda b, c: w["table_down"][:, b, c, :], True, True).then_inc(s["table_mm"], 1)

            def turn(q, j):
                pe.wait_ge(s["weight"], j * TILES + q + 2)
                for k in range(TABLE_K):
                    mm = pe.transpose(ps_e[:, q % 2, k * P:(k + 1) * P], weight[:, q % 2, k * P:(k + 1) * P], t["ident"][:])
                mm.then_inc(s["turned"], 1)

            def rows(q, j):
                pe.wait_ge(s["wt_low"], j * TILES + q + 3)
                for k, (a, b) in enumerate(HIGH_LOW):
                    for i in range(TABLE_K):
                        mm = pe.matmul(ps_o[:, q // 2, q % 2, :], weight_t[:, q % 2, a, i, :], w["table_up"][:, b, i, :],
                                       start=False, stop=(q % 2 == 1 and k == 2 and i == TABLE_K - 1), skip_group_check=True)
                mm.then_inc(s["row_mm"], 1)

            with pe.Fori(0, CHUNKS) as j:
                up(0, j)
                for i in range(K):
                    if i % 2 == 0:
                        table(i // 2, j)
                    if i + 1 < K:
                        up(i + 1, j)
                    if i % 2 == 1:
                        turn(i // 2, j)
                    down(i, j)
                    if i % 2 == 0 and i > 0:
                        rows(i // 2 - 1, j)
                rows(TILES - 1, j)

        @block.scalar
        def _(act):
            with act.Fori(0, CHUNKS) as j:
                for i in range(K):
                    n = j * K + i
                    act.wait_ge(s["gate_mm"], n + 1)
                    act.wait_ge(s["prod"], n + 1)
                    act.activation(act_g[:, i % 2, :], ps_g[:, i % 2, 0, :], ACT.Silu, scale=DOWN).then_inc(s["act_g"], 1)
                    if i % 2 == 0:
                        q = i // 2
                        m = j * TILES + q
                        act.wait_ge(s["table_mm"], m + 1)
                        act.wait_ge(s["weight"], m + 1)
                        act.activation(act_e[:, q % 2, :], ps_e[:, q % 2, :], ACT.Silu, scale=DOWN).then_inc(s["act_e"], 1)
                    act.wait_ge(s["prod"], n + 3)
                    act.wait_ge(s["down_mm"], n + 1)
                    act.activation(hidden[:, i % 2, 0, :], prod[:, i % 2, :], ACT.Copy).then_inc(s["high"], 1)
                    if i % 2 == 1:
                        q = i // 2
                        m = j * TILES + q
                        act.wait_ge(s["turned"], m + 2)
                        act.wait_ge(s["row_mm"], m + 1)
                        act.activation(weight_t[:, q % 2, 0].rearrange("p k n -> p (k n)"), ps_e[:, q % 2, :], ACT.Copy).then_inc(s["wt_high"], 1)

        @block.vector
        def _(dve):
            dve.sem_inc(s["prod"], 2)
            dve.sem_inc(s["down_mm"], 2)
            dve.sem_inc(s["row_mm"], 2)
            dve.sem_inc(s["wt_low"], 2)
            dve.sem_inc(s["added"], 1)
            dve.sem_inc(s["weight"], 1)
            dve.sem_inc(s["turned"], 1)
            dve.sem_inc(s["low"], 1)
            with dve.Fori(0, CHUNKS) as j:
                for i in range(K):
                    n = j * K + i
                    if i % 2 == 0:
                        q = i // 2
                        m = j * TILES + q
                        dve.wait_ge(s["act_e"], m + 1)
                        dve.wait_ge(s["turned"], m + 1)
                        dve.scalar_tensor_tensor(out=weight[:, q % 2, :], in0=picks[:, ds(m, 1), :].rearrange("p o e -> p (o e)"),
                                                 scalar=inverse[:, ds(m, 1)], in1=act_e[:, q % 2, :],
                                                 op0=ALU.mult, op1=ALU.mult).then_inc(s["weight"], 1)
                    dve.wait_ge(s["act_g"], n + 1)
                    dve.wait_ge(s["up_mm"], n + 1)
                    dve.wait_ge(s["low"], n + 1)
                    dve.scalar_tensor_tensor(out=prod[:, i % 2, :], in0=ps_g[:, i % 2, 1, :], scalar=DOWN, in1=act_g[:, i % 2, :],
                                             op0=ALU.mult, op1=ALU.mult).then_inc(s["prod"], 1)
                    if i % 2 == 1:
                        q = i // 2
                        m = j * TILES + q
                        dve.wait_ge(s["wt_high"], m + 1)
                        dve.tensor_tensor(weight_t[:, q % 2, 1].rearrange("p k n -> p (k n)"), ps_e[:, q % 2, :],
                                          weight_t[:, q % 2, 0].rearrange("p k n -> p (k n)"), ALU.subtract).then_inc(s["wt_low"], 1)
                dve.wait_ge(s["row_mm"], j * TILES + TILES + 2)
                for q in range(TILES):
                    x = t["x"][:, ds(j * TILES + q, 1), :].rearrange("p o d -> p (o d)")
                    dve.scalar_tensor_tensor(out=x, in0=ps_o[:, q // 2, q % 2, :], scalar=DOWN, in1=x,
                                             op0=ALU.mult, op1=ALU.add).then_inc(s["added"], 1)

        @block.gpsimd
        def _(pool):
            with pool.Fori(0, CHUNKS) as j:
                for i in range(K):
                    n = j * K + i
                    pool.wait_ge(s["high"], n + 1)
                    pool.tensor_tensor(hidden[:, i % 2, 1, :], prod[:, i % 2, :], hidden[:, i % 2, 0, :], ALU.subtract).then_inc(s["low"], 1)

        @block.sync
        def _(sp):
            with sp.Fori(0, CHUNKS) as j:
                wait_alone(sp, s["added"], j * TILES + (TILES + 1), s["seen"])
                sp.dma_start(dram["out"][ds(j * TILES, TILES)].rearrange("b p d -> p b d"), t["x"][:, ds(j * TILES, TILES), :]).then_inc(s["stored"], 16)
            sp.wait_ge(s["stored"], 16 * CHUNKS)


def two_layers(nc, dram):
    scratch = scratch_tensors(nc)
    with ExitStack() as ctx:
        t = lasting_tensors(ctx, nc)
        w = weight_tensors(ctx, nc)
        norm = Sems(ctx, nc, "norm")
        for n in ["power", "base", "rstd", "stats", "moments"]:
            norm[n]
        turn = Sems(ctx, nc, "turn")
        for n in ["normed", "turned", "high", "low", "router", "bias", "biased", "based"]:
            turn[n]
        with ExitStack() as inner:
            attention = dict(t, **attention_tensors(inner, nc))
            setup_phase(nc, dram, attention, scratch, w)
            sems = Sems(inner, nc, "att")
            attention_phase(nc, dram, attention, scratch, w, sems)
            sems.clear()
        w.update(mlp_tensors(ctx, nc))
        x_t = ctx.enter_context(nc.sbuf_tensor("x_t", [P, 2, C, TOKENS], F16))
        with nc.sbuf_tensor("gates", [P, TOKENS], F32) as gates:
            norm_phase(nc, t, norm, 0)
            with nc.psum_tensor("router", [P, NB, EXPERTS], F32) as router:
                turn_phase(nc, t, w, x_t, turn, 0, router)
                gating_phase(nc, t, w, router, gates)
            experts_phase(nc, dram, t, w, x_t, gates, scratch)
        turn_phase(nc, t, w, x_t, turn, 1)
        with ExitStack() as inner:
            picks = inner.enter_context(nc.sbuf_tensor("picks", [P, NB, TABLE], F32))
            inverse = inner.enter_context(nc.sbuf_tensor("inverse3", [P, NB], F32))
            with nc.sbuf_tensor("routing", [P, 2 * NB, KEYS], F32) as routing:
                query_phase(nc, t, w, x_t, routing)
                retrieval_phase(nc, t, w, routing, picks, inverse)
            ffn_phase(nc, dram, t, w, x_t, picks, inverse)


INPUTS = [
    "x", "ctx_2048", "mask_Bx1x2048_fk1", "L0_xattn_Wq", "L0_xattn_bq", "L0_xattn_Wk",
    "L0_xattn_bk", "L0_xattn_Wv", "L0_xattn_bv", "L0_ffn_shared_w1", "L0_ffn_shared_b1",
    "L0_ffn_shared_w2", "L0_ffn_shared_b2", "L0_ffn_routed_w1", "L0_ffn_routed_b1",
    "L0_ffn_routed_w2", "L0_ffn_routed_b2", "L0_ffn_centroids", "L0_ffn_bias", "L1_xattn_decay",
    "L1_xattn_W_in", "L1_xattn_b_in", "L1_xattn_W_out", "L1_xattn_b_out", "L1_xattn_gamma",
    "L1_xattn_beta", "L1_ffn_W_q", "L1_ffn_keys", "L1_ffn_down_embed", "L1_ffn_up_embed",
    "L1_ffn_gate_w", "L1_ffn_up_w", "L1_ffn_down_w"]


def kernel(**inputs):
    import numpy as np
    import concourse.bacc as bacc
    from concourse.bass_utils import run_bass_kernel_spmd

    nc = bacc.Bacc("TRN2", target_bir_lowering=False, num_devices=1)
    arrays, dram = {}, {}
    for name in INPUTS:
        a = np.ascontiguousarray(inputs[name])
        if a.ndim == 0:
            a = a.reshape(1)
        arrays[f"in_{name}_dram"] = a
        dram[name] = nc.dram_tensor(f"in_{name}_dram", a.shape, mybir.dt.from_np(a.dtype), kind="ExternalInput").ap()
    dram["out"] = nc.dram_tensor("out_0_dram", (NB, P, D), F32, kind="ExternalOutput").ap()
    two_layers(nc, dram)
    return run_bass_kernel_spmd(nc, [arrays], core_ids=[0]).results[0]["out_0_dram"]
```

```python
from contextlib import ExitStack

from concourse import mybir
from concourse.bass import ds

F32 = mybir.dt.float32
F16 = mybir.dt.float16
BF16 = mybir.dt.bfloat16
U32 = mybir.dt.uint32
ALU = mybir.AluOpType
ACT = mybir.ActivationFunctionType
AX = mybir.AxisListType

P = 128
NB = 16
D = 256
HEADS = 16
HD = P // HEADS
ST = D // P
EPS = 1e-5
NEG = 1e6 * HD ** 0.5

SAME = ((0, 3, 0), (3, 2, 1), (5, 1, 2))
MASK_ROW = 64
MAX_ROW = 65
ROWS = 68
STACK_DMAS = 2 * len(SAME) + 1
RING = 4
PAIR_OF_ONES = 1.0 + 0x3F80 / 2 ** 23


HIGH_LOW = ((0, 0), (0, 1), (1, 0))
UP = 64.0
DOWN = 1.0 / UP
C = D // P
CHUNK = 512
TOKENS = NB * P
CHUNKS = TOKENS // CHUNK
TILES = CHUNK // P
EXPERTS, SHARED, FF = 16, 2, 176
ROUTED_K = EXPERTS * FF // P
SHARED_F = SHARED * FF
SHARED_M = (P, P, SHARED_F - 2 * P)
TOP = 4
INTER = 1024
INTER_K = INTER // P
TABLE = 512
TABLE_K = TABLE // P
KEYS = 64
KDIM = 64


def wait(eng, sem, value):
    if not (isinstance(value, int) and value <= 0):
        eng.wait_ge(sem, value)


def wait_alone(eng, sem, value, seen):
    wait(eng, sem, value)
    if not isinstance(value, int):
        eng.sem_inc(seen, 1)


class Sems:

    def __init__(self, nc, prefix):
        self._nc, self._prefix, self._made = nc, prefix, {}

    def __getitem__(self, name):
        if name not in self._made:
            self._made[name] = self._nc.alloc_semaphore(f"{self._prefix}_{name}")
        return self._made[name]

    def clear(self):
        self._nc.clear_and_free_semaphores(list(self._made.values()))
        self._nc.all_engine_barrier()


def setup_phase(nc, dram, t, scratch, w):
    with ExitStack() as ctx:
        s = Sems(nc, "setup")

        def sb(name, shape, dt=F32):
            return ctx.enter_context(nc.sbuf_tensor(name, shape, dt))

        w_rows = sb("w_rows", [P, 3, P])
        mask_rows = sb("mask_rows", [NB, D])
        penalty = sb("penalty", [NB, D], BF16)
        stats = sb("stats", [P, NB, 6])
        base = sb("base", [P, NB])
        power = sb("power", [P, NB])
        rows = sb("rows", [P, TABLE_K + 1, D])
        context = sb("context2", [P, NB, D])
        decay = sb("decay", [P, 1])
        keep = sb("keep", [P, 8])
        runs = sb("runs", [P, P])
        anti = sb("anti", [P, P])
        picked = sb("picked", [P, P])
        weight = sb("weight", [P, 1])
        total = sb("total", [1, 2])
        spread = sb("spread", [P, NB, NB])
        proj_rows = sb("proj_rows", [P, 2, C, D])
        proj_cols = sb("proj_cols", [P, 2, C, D])
        biases = sb("biases", [1, 2, D])
        factors = sb("factors", [1, 2, NB])
        mean = sb("mean", [NB, 3, D])
        mean_t = sb("mean_t", [P, 2, C, NB])
        turned = ctx.enter_context(nc.psum_tensor("turned", [P, 2 * D], F32))
        turned_small = ctx.enter_context(nc.psum_tensor("turned_small", [P, 4, P], F32))
        turned_proj = ctx.enter_context(nc.psum_tensor("turned_proj", [P, 2, C, D], F32))
        ps_mean = ctx.enter_context(nc.psum_tensor("ps_mean", [NB, 4, D], F32))
        turned_table = ctx.enter_context(nc.psum_tensor("turned_table", [P, C, TABLE], F32))
        turned_mask = turned_small[:, 0, 0:ST * NB].rearrange("p (s b) -> p s b", s=ST)
        turned_c = turned_small[:, 1, 0:C * EXPERTS].rearrange("p (c e) -> p c e", c=C)
        for n in ["x_in", "w_in", "mask_in", "other_in", "ident", "w_turned", "w_copied",
                  "mask_turned", "mask_copied", "stats", "moments", "base", "rstd", "shift", "penalty", "penalty_out",
                  "clear", "ones", "small_in", "rows_in", "table_turned", "high", "low",
                  "decay_in", "ctx_in", "proj_in", "bias_in", "anti", "keep", "runs", "weight", "spread",
                  "total", "factors", "proj_turned", "proj_cols", "mean_mm", "mean", "mean_turned", "mean_t"]:
            s[n]
        small_moves = [(w["b1"][:], dram["L0_ffn_routed_b1"].rearrange("e f -> (e f)").rearrange("(p i) -> p i", p=P)),
                       (w["bs2"][:], dram["L0_ffn_shared_b2"].partition_broadcast(P)),
                       (w["router_bias"][:], dram["L0_ffn_bias"].partition_broadcast(P))]
        bs1 = dram["L0_ffn_shared_b1"].rearrange("n f -> (n f)")
        for k, m in enumerate(SHARED_M):
            small_moves.append((w["bs1"][0:m, k:k + 1], bs1[k * P:k * P + m].rearrange("(p o) -> p o", o=1)))
        turned_cuts = [(turned_table[:, c], [w["table_down"][:, a, c] for a in range(2)]) for c in range(C)]
        turned_cuts += [(turned_c, [w["centroids"][:, a] for a in range(2)])]
        block = ctx.enter_context(nc.Block())

        @block.sync
        def _(sp):
            for i, name in enumerate(("L0_xattn_Wq", "L0_xattn_Wk", "L0_xattn_Wv")):
                sp.dma_start(w_rows[:, i, :], dram[name]).then_inc(s["w_in"], 16)
            sp.dma_start(mask_rows[:], dram["mask_Bx1x2048_fk1"].rearrange("b o t -> (b o) t")).then_inc(s["mask_in"], 16)
            sp.dma_start(decay[:], dram["L1_xattn_decay"].partition_broadcast(P)).then_inc(s["decay_in"], 16)
            for i, name in enumerate(("L1_xattn_W_in", "L1_xattn_W_out")):
                sp.dma_start(proj_rows[:, i], dram[name].rearrange("(k p) d -> p k d", p=P)).then_inc(s["proj_in"], 16)
            for i, name in enumerate(("L1_xattn_b_in", "L1_xattn_b_out")):
                sp.dma_start(biases[:, i, :], dram[name].rearrange("(o d) -> o d", o=1)).then_inc(s["bias_in"], 16)
            sp.dma_start(rows[:, 0:TABLE_K], dram["L1_ffn_down_embed"].rearrange("(k p) d -> p k d", p=P)).then_inc(s["rows_in"], 16)
            sp.dma_start(rows[0:EXPERTS, TABLE_K], dram["L0_ffn_centroids"]).then_inc(s["rows_in"], 16)
            sp.dma_start(t["x"][:], dram["x"].rearrange("b p d -> p b d")).then_inc(s["x_in"], 16)
            sp.dma_start(context[:], dram["ctx_2048"].rearrange("b p d -> p b d")).then_inc(s["ctx_in"], 16)
            for i, name in enumerate(("L0_xattn_bq", "L0_xattn_bk")):
                sp.dma_start(t["b_qk"][:, i:i + 1], dram[name].rearrange("(h d) -> d h", d=HD),
                             allow_slow_non_contiguous=True).then_inc(s["other_in"], 16)
            sp.dma_start(t["bv_rows"][:], dram["L0_xattn_bv"].partition_broadcast(P)).then_inc(s["other_in"], 16)
            for dst, src in small_moves:
                sp.dma_start(dst, src).then_inc(s["small_in"], 16)
            sp.wait_ge(s["penalty"], 1)
            sp.dma_start(scratch["penalty"], penalty[:]).then_inc(s["penalty_out"], 16)
            sp.wait_ge(s["mean"], 3)
            sp.dma_start(scratch["summary"], mean[:, 2, :]).then_inc(s["penalty_out"], 16)
            sp.wait_ge(s["penalty_out"], 32)
            sp.wait_ge(s["x_in"], 16)
            sp.wait_ge(s["other_in"], 48)
            sp.wait_ge(s["small_in"], 16 * len(small_moves))

        @block.gpsimd
        def _(pool):
            pool.memset(t["ident"][:], 0.0).then_inc(s["ident"], 1)
            pool.memset(anti[:], 0.0).then_inc(s["anti"], 1)
            pool.wait_ge(s["ident"], 1)
            pool.affine_select(out=t["ident"][:], in_=t["ident"][:], compare_op=ALU.not_equal, fill=1.0,
                               base=0, pattern=[[-1, P]], channel_multiplier=1).then_inc(s["ident"], 1)
            pool.wait_ge(s["anti"], 1)
            pool.affine_select(out=anti[:], in_=anti[:], compare_op=ALU.not_equal, fill=1.0 / P,
                               base=-(P - 1), pattern=[[1, P]], channel_multiplier=1).then_inc(s["anti"], 1)
            pool.memset(power[:], -0.5).then_inc(s["clear"], 1)
            pool.wait_ge(s["clear"], 1)
            pool.memset(t["v_wide"][:], 0.0).then_inc(s["clear"], 1)
            pool.wait_ge(s["clear"], 2)
            pool.memset(t["stack"][32:64, 0].bitcast(F32), 0.0).then_inc(s["clear"], 1)
            pool.wait_ge(s["clear"], 3)
            pool.wait_ge(s["base"], 1)
            pool.tensor_tensor(t["rstd"][:], base[:], power[:], ALU.pow).then_inc(s["rstd"], 1)

        @block.tensor
        def _(pe):
            pe.wait_ge(s["ident"], 2)
            pe.wait_ge(s["w_in"], 48)
            for i in range(3):
                turn = pe.transpose(turned[:, i * P:(i + 1) * P], w_rows[:, i, :], t["ident"][:])
            turn.then_inc(s["w_turned"], 1)
            pe.wait_ge(s["mask_in"], 16)
            for h in range(ST):
                turn = pe.transpose(turned_mask[:, h, :], mask_rows[:, h * P:(h + 1) * P], t["ident"][0:NB, 0:NB])
            turn.then_inc(s["mask_turned"], 1)
            pe.wait_ge(s["proj_in"], 32)
            for i in range(2):
                for k in range(C):
                    for c in range(C):
                        turn = pe.transpose(turned_proj[:, i, c, k * P:(k + 1) * P], proj_rows[:, i, k, c * P:(c + 1) * P], t["ident"][:])
            turn.then_inc(s["proj_turned"], 1)
            pe.wait_ge(s["rows_in"], 32)
            for c in range(C):
                for k in range(TABLE_K):
                    pe.transpose(turned_table[:, c, k * P:(k + 1) * P], rows[:, k, c::C], t["ident"][:])
            pe.wait_ge(s["mask_copied"], 1)
            for c in range(C):
                turn = pe.transpose(turned_c[:, c, :], rows[0:EXPERTS, TABLE_K, c::C], t["ident"][0:EXPERTS, 0:EXPERTS])
            turn.then_inc(s["table_turned"], 1)
            pe.wait_ge(s["ctx_in"], 16)
            pe.wait_ge(s["spread"], 1 + NB)
            for b in range(NB):
                mm = pe.matmul(ps_mean[:, 0, :], spread[:, b, :], context[:, b, :], start=(b == 0), stop=(b == NB - 1))
            mm.then_inc(s["mean_mm"], 1)
            pe.wait_ge(s["proj_cols"], 1)
            pe.wait_ge(s["bias_in"], 32)
            pe.wait_ge(s["factors"], 2)
            pe.wait_ge(s["w_copied"], 3)
            for i in range(2):
                pe.wait_ge(s["mean"], i + 1)
                for c in range(C):
                    turn = pe.transpose(turned[:, c * NB:(c + 1) * NB], mean[:, i, c * P:(c + 1) * P], t["ident"][0:NB, 0:NB])
                turn.then_inc(s["mean_turned"], 1)
                pe.wait_ge(s["mean_t"], i + 1)
                for c in range(C):
                    pe.matmul(ps_mean[:, i + 1, :], mean_t[:, i, c, :], proj_cols[:, i, c, :], start=(c == 0), stop=False)
                pe.matmul(ps_mean[:, i + 1, :], factors[:, i, :], biases[:, i, :], start=False, stop=True).then_inc(s["mean_mm"], 1)

        @block.scalar
        def _(act):
            act.wait_ge(s["decay_in"], 16)
            act.activation(keep[:, 0:1], decay[:], ACT.Sigmoid).then_inc(s["keep"], 1)
            act.wait_ge(s["w_turned"], 1)
            for i in range(2):
                act.activation(t["w_qkv"][:, i].rearrange("p (d h) -> p h d", d=HD),
                               turned[:, i * P:(i + 1) * P].rearrange("p (h d) -> p h d", d=HD), ACT.Copy).then_inc(s["w_copied"], 1)
            act.activation(t["w_qkv"][:, 2], turned[:, 2 * P:3 * P], ACT.Copy).then_inc(s["w_copied"], 1)
            act.wait_ge(s["mask_turned"], 1)
            act.activation(t["mask_cols"][:], turned_mask, ACT.Copy).then_inc(s["mask_copied"], 1)
            act.wait_ge(s["proj_turned"], 1)
            act.activation(proj_cols[:], turned_proj[:], ACT.Copy).then_inc(s["proj_cols"], 1)
            act.wait_ge(s["table_turned"], 1)
            for src, dst in turned_cuts:
                act.activation(dst[0], src, ACT.Copy, scale=UP).then_inc(s["high"], 1)
            act.wait_ge(s["mask_copied"], 1)
            act.wait_ge(s["w_copied"], 3)

        @block.vector
        def _(dve):
            dve.memset(spread[:], 0.0).then_inc(s["spread"], 1)
            dve.memset(runs[:, 0:1], 1.0).then_inc(s["runs"], 1)
            dve.memset(factors[:, 1, :], 1.0).then_inc(s["factors"], 1)
            dve.memset(t["ones_wide"][:], 0.0).then_inc(s["ones"], 1)
            dve.wait_ge(s["ones"], 1)
            for g in range(4):
                dve.memset(t["ones_wide"][:, g, g * HD:(g + 1) * HD], 1.0).then_inc(s["ones"], 1)
            dve.memset(t["stack"][64:ROWS, 0].bitcast(F32), PAIR_OF_ONES).then_inc(s["ones"], 1)
            dve.wait_ge(s["mask_in"], 16)
            dve.tensor_scalar(penalty[:], mask_rows[:], -1.0, NEG, ALU.add, ALU.mult).then_inc(s["penalty"], 1)
            n = 1
            for i in range(7):
                dve.wait_ge(s["runs"], i + 1)
                dve.wait_ge(s["keep"], i + 1)
                dve.tensor_scalar(runs[:, n:2 * n], runs[:, 0:n], keep[:, i:i + 1], runs[:, n - 1:n],
                                  ALU.mult, ALU.add).then_inc(s["runs"], 1)
                dve.tensor_tensor(keep[:, i + 1:i + 2], keep[:, i:i + 1], keep[:, i:i + 1], ALU.mult).then_inc(s["keep"], 1)
                n *= 2
            dve.wait_ge(s["runs"], 8)
            dve.wait_ge(s["anti"], 2)
            dve.tensor_tensor(picked[:], runs[:], anti[:], ALU.mult).then_inc(s["weight"], 1)
            dve.wait_ge(s["weight"], 1)
            dve.tensor_reduce(weight[:], picked[:], AX.X, ALU.add).then_inc(s["weight"], 1)
            dve.tensor_reduce(total[:, 0:1], runs[0:1, :], AX.X, ALU.add).then_inc(s["total"], 1)
            dve.wait_ge(s["weight"], 2)
            dve.wait_ge(s["spread"], 1)
            for b in range(NB):
                dve.tensor_copy(spread[:, b, b:b + 1], weight[:]).then_inc(s["spread"], 1)
            dve.wait_ge(s["total"], 1)
            dve.wait_ge(s["factors"], 1)
            dve.tensor_scalar(factors[:, 0, :], factors[:, 1, :], total[:, 0:1], 1.0 / P, ALU.mult, ALU.mult).then_inc(s["factors"], 1)
            dve.wait_ge(s["x_in"], 16)
            for b in range(NB):
                dve.bn_stats(stats[:, b, :], t["x"][:, b, :]).then_inc(s["stats"], 1)
            for b in range(NB):
                dve.wait_ge(s["stats"], b + 1)
                dve.bn_aggr(t["moments"][:, b, :], stats[:, b, :]).then_inc(s["moments"], 1)
            dve.wait_ge(s["moments"], NB)
            dve.tensor_scalar(base[:], t["moments"][:, :, 1], EPS, None, ALU.add).then_inc(s["base"], 1)
            dve.wait_ge(s["rstd"], 1)
            dve.scalar_tensor_tensor(out=t["shift"][:], in0=t["moments"][:, :, 0], scalar=-1.0, in1=t["rstd"][:],
                                     op0=ALU.mult, op1=ALU.mult).then_inc(s["shift"], 1)
            for i in range(3):
                dve.wait_ge(s["mean_mm"], i + 1)
                dve.tensor_copy(mean[:, i, :], ps_mean[:, i, :]).then_inc(s["mean"], 1)
                if i < 2:
                    dve.wait_ge(s["mean_turned"], i + 1)
                    dve.tensor_copy(mean_t[:, i], turned[:, 0:C * NB].rearrange("p (c b) -> p c b", c=C)).then_inc(s["mean_t"], 1)
            for i, (src, dst) in enumerate(turned_cuts):
                dve.wait_ge(s["high"], i + 1)
                dve.scalar_tensor_tensor(out=dst[1], in0=src, scalar=UP, in1=dst[0],
                                         op0=ALU.mult, op1=ALU.subtract).then_inc(s["low"], 1)
            dve.wait_ge(s["shift"], 1)
            dve.wait_ge(s["ones"], 6)
            dve.wait_ge(s["low"], len(turned_cuts))


def attention_phase(nc, dram, t, scratch, w, s):
    LAST = NB - 1
    with ExitStack() as ctx:

        def sb(name, shape, dt):
            return ctx.enter_context(nc.sbuf_tensor(name, shape, dt))

        context = sb("context", [P, RING, D], F32)
        xn = sb("xn", [P, 2, D], F32)
        mask_t = sb("mask_t", [P, 2, D], F32)
        qk = sb("qk", [P, 2, D], F32)
        part = sb("part", [P, 2, 3, D], BF16)
        rest1 = sb("rest1", [P, 2, D], F32)
        v_rows = sb("v_rows", [P, ST, P], F32)
        neg_max = sb("neg_max", [P, 2, ST * HEADS], F32)
        max_part = sb("max_part", [ST * HEADS, 3, P], BF16)
        max_rest = sb("max_rest", [ST * HEADS, 2, P], F32)
        probs = sb("probs", [P, 2, 4, ST, D], F32)
        out_sums = sb("out_sums", [P, 2, D], F32)
        inverse = sb("inverse", [P, D], F32)
        ratio = sb("ratio", [P, D], F32)
        masked = sb("masked", [P, D], F32)
        stats = sb("new_stats", [P, 6], F32)
        moments = sb("new_moments", [P, 2], F32)
        stage = sb("stage", [P, 2, STAGE], F32)
        stack, v_wide = t["stack"], t["v_wide"]

        def ps(name, shape):
            return ctx.enter_context(nc.psum_tensor(name, shape, F32))

        scores = ps("scores", [P, 2, 2 * D])
        scores_t = ps("scores_t", [P, 2, 2 * D])
        sums = ps("sums", [P, 2, 2, D])
        ps_qk = ps("ps_qk", [P, 2, D])
        ps_v = ps("ps_v", [P, 2 * D])
        for n in ["ctx_in0", "ctx_in1", "ctx_in2", "ctx_in3", "xn", "qk_mm", "qk_evac", "rest1", "part1", "part2", "parts_out",
                  "stack_in", "v_mm", "v_bias", "v_done", "max_done", "max_turned", "max_cut",
                  "max_out", "max_in", "score_mm", "prob_mm", "exp", "av_done",
                  "sums_evac", "inverse", "ratio", "masked", "x1", "mask_in0", "mask_in1", "piece_in0", "piece_in1",
                  "piece_scaled", "piece_high", "piece_low",
                  "slot_ones", "slot_zeros", "stats", "moments", "kept", "dve_seen"]:
            s[n]
        block = ctx.enter_context(nc.Block())

        def on(n, j):
            return 0 <= n <= LAST if j is None else True

        def steps(eng, step):
            for k in range(-4, 4):
                step(k, k % RING, None)
            with eng.Fori(1, 3) as j:
                for r in range(RING):
                    step(j * RING + r, r, j)
            for k in range(12, 18):
                step(k, k % RING, None)

        def group(k, r, j, ahead):
            return (k + ahead) // RING if j is None else j + (r + ahead) // RING

        def half(k, r, j, ahead):
            return (k + ahead) // 2 if j is None else 2 * j + (r + ahead) // 2

        def head(u):
            return (u % 4) * 4 + u // 4

        def cut_count(i, c):
            return i + c + 1 + (2 if isinstance(i, int) and i == 9 else 0)

        @block.sync
        def _(sp):
            def step(k, r, j):
                piece = weight_piece(dram, w, stage, k, r, j)
                if piece is not None:
                    i, moves, _ = piece
                    wait_alone(sp, s["piece_low"], i + 1, s["seen"])
                    for dst, src in moves:
                        sp.dma_start(dst, src).then_inc(s[f"piece_in{r % 2}"], 16)
                n = k
                if on(n, j):
                    wait_alone(sp, s["masked"], n - 1, s["seen"])
                    sp.dma_start(mask_t[:, r % 2, :], dram["mask_Bx1x2048_fk1"][ds(n, 1)].rearrange("b o t -> (b o) t")
                                 .partition_broadcast(P)).then_inc(s[f"mask_in{r % 2}"], 16)
                n = k + 4
                if on(n, j):
                    if j is not None or k >= 0:
                        wait_alone(sp, s["v_mm"], k + 1, s["seen"])
                        wait_alone(sp, s["qk_mm"], k + 1, s["seen"])
                    sp.dma_start(context[:, r, :], dram["ctx_2048"][ds(n, 1)].rearrange("b c s -> (b c) s")).then_inc(s[f"ctx_in{r}"], 16)
                m, n = k + 1, k + 3
                if on(m, j):
                    wait_alone(sp, s["max_cut"], 4 * m + 4, s["seen"])
                    wait_alone(sp, s["max_in"], 16 * m, s["seen"])
                    sp.dma_start(scratch["maxima"].rearrange("a h s t -> h s a t")[:, 0], max_part[0:HEADS]).then_inc(s["max_out"], 16)
                    sp.dma_start(scratch["maxima"].rearrange("a h s t -> h s a t")[:, 1], max_part[HEADS:2 * HEADS]).then_inc(s["max_out"], 16)
                if on(n, j):
                    wait_alone(sp, s["part2"], n + 1, s["seen"])
                    wait_alone(sp, s["stack_in"], STACK_DMAS * 16 * n, s["seen"])
                    sp.dma_start(scratch["parts"].rearrange("e a d h t -> (d h) (e a) t"), part[:].rearrange("p e a t -> p (e a) t")).then_inc(s["parts_out"], 16)
                if on(m, j):
                    wait_alone(sp, s["max_out"], 32 * (m + 1), s["seen"])
                    sp.dma_start(stack[MAX_ROW:MAX_ROW + 3, (r + 1) % RING, 0],
                                 scratch["maxima"].rearrange("a h s t -> a h (s t)")).then_inc(s["max_in"], 16)
                if on(n, j):
                    slot = (r + 3) % RING
                    wait_alone(sp, s["parts_out"], 16 * n + 16, s["seen"])
                    if j is None and 0 < n < RING:
                        sp.wait_ge(s["slot_ones"], n)
                        sp.wait_ge(s["slot_zeros"], n)
                    if j is not None or n >= RING:
                        wait_alone(sp, s["prob_mm"], 16 * (n - RING) + 16, s["seen"])
                    for i, count, a in SAME:
                        sp.dma_start(stack[i * HD:(i + count) * HD, slot, 0].rearrange("r h t -> r (h t)"),
                                     scratch["parts"][0, a].rearrange("d h t -> d (h t)").unsqueeze(0)
                                     .broadcast_to([count, HD, HEADS * D])).then_inc(s["stack_in"], 16)
                        sp.dma_start(stack[i * HD:(i + count) * HD, slot, 1].rearrange("r h t -> r (h t)"),
                                     scratch["parts"][1, 0:count].rearrange("a d h t -> (a d) (h t)")).then_inc(s["stack_in"], 16)
                    sp.dma_start(stack[MASK_ROW:MASK_ROW + 1, slot, 1],
                                 scratch["penalty"][ds(n, 1)].unsqueeze(1).broadcast_to([1, HEADS, D])).then_inc(s["stack_in"], 16)

            steps(sp, step)

        @block.tensor
        def _(pe):
            def values(g, piece, n, r):
                which, st = divmod(piece, ST)
                if piece == 0:
                    wait(pe, s["exp"], 16 * n + 4 * g + 4)
                    if g == 0:
                        wait(pe, s["sums_evac"], n - 1)
                        wait(pe, s["v_done"], n + 1)
                for q in range(4):
                    at = 32 + 32 * (4 * q + g) - HD * g
                    w = v_wide[:, r % 2, st, at:at + 32] if which == 0 else t["ones_wide"][:, g, :]
                    mm = pe.matmul(sums[32 * q:32 * q + 32, r % 2, which, :], w, probs[:, g % 2, q, st, :],
                                   start=(g == 0 and piece == 0), stop=(g == 3 and st == ST - 1), skip_group_check=True)
                if piece == 3:
                    mm.then_inc(s["av_done"], 1)

            def step(k, r, j):
                n = k + 3
                if on(n, j):
                    wait(pe, s["xn"], n + 1)
                    slot = (r + 3) % RING
                    wait(pe, s[f"ctx_in{slot}"], 16 * (group(k, r, j, 3) + 1))
                    wait(pe, s["qk_evac"], n)
                    pe.matmul(ps_qk[:, 0, :], t["w_qkv"][:, 0, :], xn[:, (r + 3) % 2, :], start=True, stop=True)
                    pe.matmul(ps_qk[:, 1, :], t["w_qkv"][:, 1, :], context[:, slot, :], start=True, stop=True).then_inc(s["qk_mm"], 1)
                for u in range(HEADS):
                    h = head(u)
                    if u >= 5 and on(k, j):
                        values((u - 5) // 4, (u - 5) % 4, k, r)
                    elif u < 5 and on(k - 1, j):
                        values(*((3, u - 1) if u else (2, 3)), k - 1, r + 3)
                    n = k + 2
                    if on(n, j):
                        if u == 0:
                            wait(pe, s["stack_in"], STACK_DMAS * 16 * (n + 1))
                        wait(pe, s["max_done"], 16 * n + u - 1)
                        slot = (r + 2) % RING
                        for tt in range(ST):
                            mm = pe.matmul(scores[:, u % 2, tt * D:(tt + 1) * D],
                                           stack[0:MASK_ROW + 1, slot, 0, h, tt * P:(tt + 1) * P],
                                           stack[0:MASK_ROW + 1, slot, 1, h, :], start=True, stop=True)
                        mm.then_inc(s["score_mm"], 1)
                    n = k
                    if on(n, j):
                        if u == 0:
                            wait(pe, s["max_in"], 16 * (n + 1))
                        wait(pe, s["exp"], 16 * n + u - 1)
                        for st in range(ST):
                            mm = pe.matmul(scores_t[:, u % 2, st * D:(st + 1) * D],
                                           stack[0:ROWS, r, 1, h, st * P:(st + 1) * P],
                                           stack[0:ROWS, r, 0, h, :], start=True, stop=True)
                        mm.then_inc(s["prob_mm"], 1)
                    n = k + 1
                    if on(n, j) and u == 1:
                        wait(pe, s["max_done"], 16 * (n + 1))
                        wait(pe, s["v_done"], n)
                        pe.transpose(ps_v[0:ST * HEADS, 256:256 + P], neg_max[:, (r + 1) % 2, :], t["ident"][:]).then_inc(s["max_turned"], 1)
                    if on(n, j) and u == 5:
                        wait(pe, s["max_cut"], 4 * n + 2)
                        for st in range(ST):
                            mm = pe.matmul(ps_v[:, st * P:(st + 1) * P], context[:, (r + 1) % RING, st * P:(st + 1) * P],
                                           t["w_qkv"][:, 2, :], start=True, stop=True)
                        mm.then_inc(s["v_mm"], 1)

            steps(pe, step)

        @block.scalar
        def _(act):
            def step(k, r, j):
                piece = weight_piece(dram, w, stage, k, r, j)
                for u in range(HEADS):
                    if piece is not None and u == 8:
                        i, moves, cuts = piece
                        turns = 2 * (j - 1) + r // 2 + 1 if j is not None else 4 + len(moves)
                        act.wait_ge(s[f"piece_in{r % 2}"], 16 * turns)
                        for src, dst, scale in cuts:
                            act.activation(src, src, ACT.Copy, scale=scale).then_inc(s["piece_scaled"], 1)
                    if piece is not None and u == 13:
                        for c, (src, dst, scale) in enumerate(cuts):
                            act.wait_ge(s["piece_scaled"], cut_count(i, c))
                            act.activation(dst[0], src, ACT.Copy).then_inc(s["piece_high"], 1)
                    n = k + 3
                    if u == 1 and on(n, j):
                        wait(act, s["qk_mm"], n + 1)
                        wait(act, s["parts_out"], 16 * n)
                        wait(act, s["rest1"], n)
                        for e in range(2):
                            act.activation(qk[:, e, :], ps_qk[:, e, :], ACT.Identity, bias=t["b_qk"][:, e:e + 1])
                            mm = act.activation(part[:, e, 0, :], ps_qk[:, e, :], ACT.Identity, bias=t["b_qk"][:, e:e + 1])
                        mm.then_inc(s["qk_evac"], 1)
                    n = k
                    if on(n, j):
                        wait(act, s["prob_mm"], 16 * n + u + 1)
                        if u % 4 == 0:
                            wait(act, s["av_done"], 4 * n + u // 4 - 1)
                        act.activation(probs[:, (u // 4) % 2, u % 4], scores_t[:, u % 2, :].rearrange("p (s t) -> p s t", s=ST),
                                       ACT.Exp, scale=HD ** -0.5).then_inc(s["exp"], 1)
                    n = k + 4
                    if u == 10 and on(n, j):
                        wait(act, s["qk_mm"], n - 1)
                        act.activation(xn[:, r % 2, :], t["x"][:, ds(n, 1), :].rearrange("p o d -> p (o d)"), ACT.Identity,
                                       scale=t["rstd"][:, ds(n, 1)], bias=t["shift"][:, ds(n, 1)]).then_inc(s["xn"], 1)
                    n = k - 1
                    if u == 5 and on(n, j):
                        wait(act, s["av_done"], 4 * n + 4)
                        wait(act, s["ratio"], n)
                        act.activation(out_sums[:], sums[:, (r + 3) % 2], ACT.Copy).then_inc(s["sums_evac"], 1)

            steps(act, step)

        @block.vector
        def _(dve):
            def step(k, r, j):
                for u in range(HEADS):
                    n = k + 2
                    if on(n, j):
                        wait(dve, s["score_mm"], 16 * n + u + 1)
                        if u == 0:
                            wait(dve, s["max_turned"], n - 1)
                        h = head(u)
                        dve.tensor_reduce(neg_max[:, r % 2, h::HEADS],
                                          scores[:, u % 2, :].rearrange("p (s t) -> p s t", s=ST),
                                          AX.X, ALU.max, negate=True).then_inc(s["max_done"], 1)
                    n = k + 1
                    if on(n, j) and u == 2:
                        turned = ps_v[0:ST * HEADS, 256:256 + P]
                        wait(dve, s["max_turned"], n + 1)
                        wait(dve, s["max_out"], 32 * n)
                        dve.tensor_copy(max_part[:, 0, :], turned).then_inc(s["max_cut"], 1)
                        wait(dve, s["max_cut"], 4 * n + 1)
                        dve.tensor_tensor(max_rest[:, 0, :], turned, max_part[:, 0, :], ALU.subtract).then_inc(s["max_cut"], 1)
                        wait(dve, s["max_cut"], 4 * n + 2)
                        dve.tensor_copy(max_part[:, 1, :], max_rest[:, 0, :]).then_inc(s["max_cut"], 1)
                        wait(dve, s["max_cut"], 4 * n + 3)
                        dve.tensor_tensor(max_part[:, 2, :], max_rest[:, 0, :], max_part[:, 1, :], ALU.subtract).then_inc(s["max_cut"], 1)
                    n = k + 3
                    if on(n, j) and u == 4:
                        wait(dve, s["qk_evac"], n + 1)
                        wait(dve, s["part2"], n)
                        dve.tensor_tensor(rest1[:], qk[:], part[:, :, 0], ALU.subtract).then_inc(s["rest1"], 1)
                        wait(dve, s["rest1"], n + 1)
                        wait(dve, s["parts_out"], 16 * n)
                        dve.tensor_copy(part[:, :, 1], rest1[:]).then_inc(s["part1"], 1)
                    n = k + 1
                    if on(n, j) and u == 8:
                        slot = (r + 1) % 2
                        wait(dve, s["v_mm"], n + 1)
                        wait(dve, s["v_done"], n)
                        dve.tensor_tensor(v_rows[:], ps_v[:, 0:2 * P].rearrange("p (s c) -> p s c", s=ST),
                                          t["bv_rows"][:].unsqueeze(1).broadcast_to([P, ST, P]), ALU.add).then_inc(s["v_bias"], 1)
                        wait(dve, s["v_bias"], n + 1)
                        wait(dve, s["av_done"], 4 * (n - 2) + 4)
                        for st in range(ST):
                            dst = v_wide[:, slot, st, 32:].rearrange("p (h c) -> p h c", c=32)[:, :, 0:HD]
                            mm = dve.tensor_scalar(dst, v_rows[:, st, :].rearrange("p (h d) -> p h d", d=HD),
                                                   t["mask_cols"][:, st, ds(n, 1)], None, ALU.mult)
                        mm.then_inc(s["v_done"], 1)
                    n = k - 1
                    if on(n, j) and u in (10, 12):
                        if u == 10:
                            wait(dve, s["sums_evac"], n + 1)
                            wait(dve, s["ratio"], n)
                        part_of = slice((u - 10) // 2 * P, (u - 8) // 2 * P)
                        dve.reciprocal(inverse[:, part_of], out_sums[:, 1, part_of]).then_inc(s["inverse"], 1)
                    n = k - 2
                    if on(n, j) and u == 14:
                        wait_alone(dve, s["x1"], n + 1, s["dve_seen"])
                        dve.bn_stats(stats[:], t["x"][:, ds(n, 1), :].rearrange("p o d -> p (o d)")).then_inc(s["stats"], 1)
                        wait_alone(dve, s["stats"], n + 1, s["dve_seen"])
                        dve.bn_aggr(moments[:], stats[:]).then_inc(s["moments"], 1)
                        wait(dve, s["moments"], n + 1)
                        dve.tensor_copy(t["moments"][:, ds(n, 1), :].rearrange("p o m -> p (o m)"), moments[:]).then_inc(s["kept"], 1)
                slot = k + 4
                if j is None and 0 < slot < RING:
                    dve.memset(stack[64:ROWS, slot].bitcast(F32), PAIR_OF_ONES).then_inc(s["slot_ones"], 1)

            steps(dve, step)

        @block.gpsimd
        def _(pool):
            pool.sem_inc(s["piece_low"], 2)

            def step(k, r, j):
                n = k + 3
                if on(n, j):
                    wait(pool, s["part1"], n + 1)
                    wait(pool, s["parts_out"], 16 * n)
                    pool.tensor_tensor(part[:, :, 2], rest1[:], part[:, :, 1], ALU.subtract).then_inc(s["part2"], 1)
                slot = k + 4
                if j is None and 0 < slot < RING:
                    wait(pool, s["slot_zeros"], slot - 1)
                    pool.wait_ge(s["part2"], slot)
                    pool.memset(stack[32:64, slot].bitcast(F32), 0.0).then_inc(s["slot_zeros"], 1)
                    pool.wait_ge(s["slot_zeros"], slot)
                n = k - 1
                if on(n, j):
                    wait(pool, s["inverse"], 2 * n + 2)
                    wait(pool, s["x1"], n)
                    pool.tensor_tensor(ratio[:], out_sums[:, 0, :], inverse[:], ALU.mult).then_inc(s["ratio"], 1)
                    wait(pool, s["ratio"], n + 1)
                    wait(pool, s[f"mask_in{(r + 3) % 2}"], 16 * (half(k, r, j, -1) + 1))
                    pool.tensor_tensor(masked[:], ratio[:], mask_t[:, (r + 3) % 2, :], ALU.mult).then_inc(s["masked"], 1)
                    wait(pool, s["masked"], n + 1)
                    x = t["x"][:, ds(n, 1), :].rearrange("p o d -> p (o d)")
                    pool.tensor_tensor(x, x, masked[:], ALU.add).then_inc(s["x1"], 1)

                piece = weight_piece(dram, w, stage, k, r, j)
                if piece is not None:
                    i, _, cuts = piece
                    for c, (src, dst, scale) in enumerate(cuts):
                        pool.wait_ge(s["piece_high"], cut_count(i, c))
                        pool.tensor_tensor(dst[1], src, dst[0], ALU.subtract).then_inc(s["piece_low"], 1)

            steps(pool, step)


def lasting_tensors(ctx, nc):
    def sb(name, shape, dt=F32):
        return ctx.enter_context(nc.sbuf_tensor(name, shape, dt))

    return {
        "x": sb("x", [P, NB, D]),
        "ident": sb("ident", [P, P]),
        "moments": sb("moments", [P, NB, 2]),
        "rstd": sb("rstd", [P, NB]),
    }


def attention_tensors(ctx, nc):
    def sb(name, shape, dt=F32):
        return ctx.enter_context(nc.sbuf_tensor(name, shape, dt))

    return {
        "b_qk": sb("b_qk", [P, 2]),
        "bv_rows": sb("bv_rows", [P, P]),
        "mask_cols": sb("mask_cols", [P, ST, NB]),
        "w_qkv": sb("w_qkv", [P, 3, P]),
        "stack": sb("stack", [ROWS, RING, 2, HEADS, D], BF16),
        "v_wide": sb("v_wide", [P, 2, ST, (HEADS + 1) * 32]),
        "ones_wide": sb("ones_wide", [P, 4, 32]),
        "shift": sb("shift", [P, NB]),
    }


def scratch_tensors(nc):
    def room(name, shape, dt):
        return nc.dram_tensor(name, shape, dt, kind="Internal").ap()

    return {
        "penalty": room("penalty_rows", [NB, D], BF16),
        "parts": room("parts_room", [2, 3, HD, HEADS, D], BF16),
        "maxima": room("maxima_room", [3, HEADS, ST, P], BF16),
        "summary": room("summary_room", [NB, D], F32),
    }


def weight_tensors(ctx, nc):
    def sb(name, shape, dt=F16):
        return ctx.enter_context(nc.sbuf_tensor(name, shape, dt))

    return {
        "w1": sb("w1", [P, 2, C, ROUTED_K * P]),
        "w2": sb("w2", [P, 2, ROUTED_K * D]),
        "ws1": sb("ws1", [P, 2, C, SHARED_F]),
        "ws2": sb("ws2", [P, 2, 3, D]),
        "table_down": sb("table_down", [P, 2, C, TABLE]),
        "centroids": sb("centroids", [P, 2, C, EXPERTS]),
        "query": sb("query", [P, 2, C, 2, P]),
        "keys": sb("keys", [P, 2, 2, KEYS]),
        "b2": sb("b2", [P, 2, D]),
        "b1": sb("b1", [P, ROUTED_K], F32),
        "bs1": sb("bs1", [P, 3], F32),
        "bs2": sb("bs2", [P, 2, D], F32),
        "router_bias": sb("router_bias", [P, EXPERTS], F32),
    }


STAGE = C * SHARED_F + 3 * D


def weight_piece(dram, w, stage, k, r, j):
    if j is not None:
        i = 4 * (j - 1) + r
        half = EXPERTS // 2 * FF
        v = stage[:, r % 2, 0:half]
        if r % 2 == 0:
            h, rows = r // 2, half // ROUTED_K
            src = dram["L0_ffn_routed_w1"].rearrange("e (p c) f -> c p e f", c=C)[ds(j - 1, 1)][:, :, h * EXPERTS // 2:(h + 1) * EXPERTS // 2]
            dst = [w["w1"][:, a, ds(j - 1, 1)].rearrange("p o (i q) -> p (o q) i", i=ROUTED_K)[:, h * rows:(h + 1) * rows] for a in range(2)]
            return i, [(v.rearrange("p (e f) -> p e f", f=FF), src.rearrange("o p e f -> (o p) e f"))], [(v.rearrange("p (q i) -> p q i", i=ROUTED_K), dst, UP)]
        part = ds((2 * (j - 1) + r // 2) * half, half)
        src = dram["L0_ffn_routed_w2"].rearrange("e f d -> (e f) d").rearrange("(p i) d -> p (i d)", p=P)
        return i, [(v, src[:, part])], [(v, [w["w2"][:, a, part] for a in range(2)], UP)]
    if k == 12:
        v = stage[:, 0, 0:C * SHARED_F]
        v4 = v.rearrange("p (c n f) -> p c n f", c=C, n=SHARED)
        src = dram["L0_ffn_shared_w1"].rearrange("n (p c) f -> c p n f", c=C)
        v2 = stage[:, 0, C * SHARED_F:].rearrange("p (k d) -> p k d", k=3)
        s2 = dram["L0_ffn_shared_w2"].rearrange("n f d -> (n f) d")
        m = SHARED_M[2]
        return 8, ([(v4[:, c], src[c]) for c in range(C)]
                   + [(v2[:, 0:2], s2[0:2 * P].rearrange("(k p) d -> p k d", p=P)), (v2[0:m, 2], s2[2 * P:SHARED_F])]), \
            [(v, [w["ws1"][:, a].rearrange("p c f -> p (c f)") for a in range(2)], UP),
             (v2[:, 0:2], [w["ws2"][:, a, 0:2] for a in range(2)], UP),
             (v2[0:m, 2], [w["ws2"][0:m, a, 2] for a in range(2)], UP)]
    if k == 13:
        small = stage[:, 1, 0:C * 2 * P + 2 * KEYS + D]
        q = small[:, 0:C * 2 * P]
        q4 = q.rearrange("p (c r m) -> p c r m", c=C, r=2)
        ky = small[:, C * 2 * P:C * 2 * P + 2 * KEYS].rearrange("p (s k) -> p s k", s=2)
        b2 = small[:, C * 2 * P + 2 * KEYS:]
        moves = []
        for half in range(2):
            for c in range(C):
                moves.append((q4[:, c, :, half * KDIM:(half + 1) * KDIM],
                              dram["L1_ffn_W_q"].rearrange("(p c) (r m) -> c p r m", c=C, r=2)[c]))
            moves.append((ky[half * KDIM:(half + 1) * KDIM], dram["L1_ffn_keys"].rearrange("s k n -> k s n")))
        moves.append((b2, dram["L0_ffn_routed_b2"].unsqueeze(1).broadcast_to([EXPERTS, P // EXPERTS, D])))
        return 9, moves, [(q, [w["query"][:, a].rearrange("p c r m -> p (c r m)") for a in range(2)], UP),
                          (ky, [w["keys"][:, a] for a in range(2)], UP),
                          (b2, [w["b2"][:, a] for a in range(2)], UP * EXPERTS / P)]
    return None


def mlp_tensors(ctx, nc):
    def sb(name, shape, dt=F16):
        return ctx.enter_context(nc.sbuf_tensor(name, shape, dt))

    return {
        "gate": sb("gate", [P, 2, C, INTER]),
        "up": sb("up", [P, 2, C, INTER]),
        "down": sb("down", [P, 2, INTER_K * D]),
        "table_up": sb("table_up", [P, 2, TABLE_K, D]),
        "gamma": sb("gamma", [P, D], F32),
        "beta": sb("beta", [P, D], F32),
    }


def on_dve(i):
    return i % 2 == 1 and i < NB // 2 + 4


def on_act(i):
    return sum(not on_dve(b) for b in range(i))


def route_phase(nc, t, w, x_t, s, gates):
    HALF = NB // 2
    SLOTS = 3
    STEPS = NB + 3
    with ExitStack() as ctx:
        def sb(name, shape, dt=F32):
            return ctx.enter_context(nc.sbuf_tensor(name, shape, dt))

        normed = sb("normed0", [P, SLOTS, D])
        base = sb("base0", [P, NB])
        power = sb("power0", [P, NB])
        shift = sb("route_shift", [P, NB])
        sig = sb("sig", [P, NB, EXPERTS])
        score = sb("score", [P, NB, EXPERTS])
        best = sb("best", [P, NB, 8])
        place = sb("place", [P, NB, 8], U32)
        place_f = sb("place_f", [P, NB, TOP])
        number = sb("number", [P, EXPERTS])
        hit = sb("hit", [P, NB, TOP, EXPERTS])
        member = sb("member", [P, NB, EXPERTS])
        kept = sb("kept", [P, NB, EXPERTS])
        total = sb("total2", [P, NB])
        floor = sb("floor", [P, NB])
        inverse = sb("inverse2", [P, NB])
        gate = sb("gate_rows", [P, NB, EXPERTS, P // EXPERTS])
        turned = ctx.enter_context(nc.psum_tensor("turned0", [P, SLOTS, C, D], F32))
        router = ctx.enter_context(nc.psum_tensor("router", [P, 2, CHUNK], F32))
        turned_gates = ctx.enter_context(nc.psum_tensor("turned_gates", [P, 3, TILES, P], F32))
        own = Sems(nc, "route")
        for n in ["power", "base", "rstd", "shift", "router", "number", "sig", "score", "best", "place", "step", "gate", "turned", "out", "normed"]:
            own[n]
        block = ctx.enter_context(nc.Block())
        GATE_STAGES = 7
        DVE_STEPS = TOP + 6

        @block.gpsimd
        def _(pool):
            pool.memset(power[:], -0.5).then_inc(own["power"], 1)
            pool.wait_ge(own["power"], 1)
            pool.wait_ge(own["base"], 1)
            for first, last in ((0, TILES), (TILES, NB)):
                pool.tensor_tensor(t["rstd"][:, first:last], base[:, first:last], power[:, first:last], ALU.pow).then_inc(own["rstd"], 1)
            pool.iota(number[:], [[1, EXPERTS]], base=0, channel_multiplier=0, allow_small_or_imprecise_dtypes=True).then_inc(own["number"], 1)
            pool.wait_ge(own["number"], 1)

        @block.tensor
        def _(pe):
            for i in range(STEPS):
                if i < NB:
                    if i >= SLOTS:
                        pe.wait_ge(s["low"], i - SLOTS + 1)
                    if on_dve(i):
                        pe.wait_ge(own["normed"], i // 2 + 1)
                    else:
                        pe.wait_ge(s["normed"], on_act(i + 1))
                    for c in range(C):
                        turn = pe.transpose(turned[:, i % SLOTS, c, 0:P], normed[:, i % SLOTS, c::C], t["ident"][:])
                    turn.then_inc(s["turned"], 1)
                n = i - 3
                if 0 <= n < NB:
                    pe.wait_ge(s["low"], n + 1)
                    products = [(a, b, c) for a, b in HIGH_LOW for c in range(C)]
                    at = n % HALF * EXPERTS
                    for k, (a, b, c) in enumerate(products):
                        mm = pe.matmul(router[:, n // HALF, at:at + EXPERTS], x_t[:, a, c, n * P:(n + 1) * P], w["centroids"][:, b, c, :],
                                       start=(k == 0), stop=(k == len(products) - 1))
                    if n % HALF == HALF - 1:
                        mm.then_inc(own["router"], 1)
            for j in range(CHUNKS):
                if j >= 3:
                    pe.wait_ge(own["out"], j - 2)
                pe.wait_ge(own["gate"], TILES * (j + 1))
                for b in range(TILES):
                    turn = pe.transpose(turned_gates[:, j % 3, b, :], gate[:, j * TILES + b].rearrange("p e r -> p (e r)"), t["ident"][:])
                turn.then_inc(own["turned"], 1)

        @block.scalar
        def _(act):
            for i in range(STEPS):
                if i < NB and not on_dve(i):
                    act.wait_ge(own["shift"], 1 if i < TILES else 2)
                    if i >= SLOTS:
                        act.wait_ge(s["turned"], i - SLOTS + 1)
                    act.activation(normed[:, i % SLOTS], t["x"][:, i, :], ACT.Identity, scale=t["rstd"][:, i:i + 1],
                                   bias=shift[:, i:i + 1]).then_inc(s["normed"], 1)
                n = i - 2
                if 0 <= n < NB:
                    act.wait_ge(s["turned"], n + 1)
                    act.activation(x_t[:, 0, :, n * P:(n + 1) * P], turned[:, n % SLOTS, :, 0:P], ACT.Copy).then_inc(s["high"], 1)
                if i in (HALF + 3, NB + 2):
                    h = i // NB
                    act.wait_ge(own["router"], h + 1)
                    act.activation(sig[:, h * HALF:(h + 1) * HALF], router[:, h, 0:HALF * EXPERTS].rearrange("p (b e) -> p b e", b=HALF),
                                   ACT.Sigmoid, scale=DOWN).then_inc(own["sig"], 1)
            for j in range(CHUNKS):
                act.wait_ge(own["turned"], j + 1)
                act.activation(gates[:, j * CHUNK:(j + 1) * CHUNK], turned_gates[:, j % 3].rearrange("p b m -> p (b m)"),
                               ACT.Copy).then_inc(own["out"], 1)
            act.wait_ge(own["out"], CHUNKS)

        @block.vector
        def _(dve):
            def gate_stage(h, stage):
                batches = range(h * HALF, (h + 1) * HALF)
                bs = slice(h * HALF, (h + 1) * HALF)
                step = h * DVE_STEPS
                if stage == 0:
                    dve.wait_ge(own["sig"], h + 1)
                    dve.tensor_tensor(score[:, bs], sig[:, bs], w["router_bias"][:].unsqueeze(1).broadcast_to([P, HALF, EXPERTS]), ALU.add).then_inc(own["score"], 1)
                    dve.wait_ge(own["score"], h + 1)
                    for b in batches:
                        dve.max(best[:, b, :], score[:, b, :]).then_inc(own["best"], 1)
                elif stage == 1:
                    for b in batches:
                        dve.wait_ge(own["best"], b + 1)
                        dve.max_index(place[:, b, :], best[:, b, :], score[:, b, :]).then_inc(own["place"], 1)
                elif stage == 2:
                    dve.wait_ge(own["place"], (h + 1) * HALF)
                    dve.tensor_copy(place_f[:, bs], place[:, bs, 0:TOP]).then_inc(own["step"], 1)
                    dve.wait_ge(own["step"], step + 1)
                    dve.wait_ge(own["number"], 1)
                    for k in range(TOP):
                        dve.tensor_tensor(hit[:, bs, k, :], number[:].unsqueeze(1).broadcast_to([P, HALF, EXPERTS]),
                                          place_f[:, bs, k:k + 1].broadcast_to([P, HALF, EXPERTS]), ALU.is_equal).then_inc(own["step"], 1)
                elif stage == 3:
                    dve.wait_ge(own["step"], step + TOP + 1)
                    dve.tensor_reduce(member[:, bs], hit[:, bs].rearrange("p b j e -> p b e j"), AX.X, ALU.add).then_inc(own["step"], 1)
                elif stage == 4:
                    dve.wait_ge(own["step"], step + TOP + 2)
                    dve.tensor_tensor(kept[:, bs], score[:, bs], member[:, bs], ALU.mult).then_inc(own["step"], 1)
                    dve.wait_ge(own["step"], step + TOP + 3)
                    dve.tensor_reduce(total[:, bs], kept[:, bs], AX.X, ALU.add).then_inc(own["step"], 1)
                elif stage == 5:
                    dve.wait_ge(own["step"], step + TOP + 4)
                    dve.tensor_scalar(floor[:, bs], total[:, bs], 1e-8, None, ALU.max).then_inc(own["step"], 1)
                    dve.wait_ge(own["step"], step + TOP + 5)
                    dve.reciprocal(inverse[:, bs], floor[:, bs]).then_inc(own["step"], 1)
                else:
                    dve.wait_ge(own["step"], step + TOP + 6)
                    for b in batches:
                        dve.tensor_scalar(gate[:, b], kept[:, b, :].unsqueeze(2).broadcast_to([P, EXPERTS, P // EXPERTS]),
                                          inverse[:, b:b + 1], None, ALU.mult).then_inc(own["gate"], 1)

            dve.tensor_scalar(base[:], t["moments"][:, :, 1], EPS, None, ALU.add).then_inc(own["base"], 1)
            for n, (first, last) in enumerate(((0, TILES), (TILES, NB))):
                dve.wait_ge(own["rstd"], n + 1)
                dve.scalar_tensor_tensor(out=shift[:, first:last], in0=t["moments"][:, first:last, 0], scalar=-1.0,
                                         in1=t["rstd"][:, first:last], op0=ALU.mult, op1=ALU.mult).then_inc(own["shift"], 1)
            for i in range(STEPS):
                if i < NB and on_dve(i):
                    if i >= SLOTS:
                        dve.wait_ge(s["turned"], i - SLOTS + 1)
                    dve.tensor_scalar(normed[:, i % SLOTS], t["x"][:, i, :], t["moments"][:, i, 0:1], t["rstd"][:, i:i + 1],
                                      ALU.subtract, ALU.mult).then_inc(own["normed"], 1)
                n = i - 2
                if 0 <= n < NB:
                    dve.wait_ge(s["high"], n + 1)
                    dve.tensor_tensor(x_t[:, 1, :, n * P:(n + 1) * P], turned[:, n % SLOTS, :, 0:P],
                                      x_t[:, 0, :, n * P:(n + 1) * P], ALU.subtract).then_inc(s["low"], 1)
                if HALF + 4 <= i < HALF + 4 + GATE_STAGES:
                    gate_stage(0, i - HALF - 4)
            for stage in range(GATE_STAGES):
                gate_stage(1, stage)


def row(x, b):
    return x[:, b, :] if isinstance(b, int) else x[:, ds(b, 1), :].rearrange("p o d -> p (o d)")


def stage_order(i, b):
    if isinstance(b, int) and b >= NB - TILES:
        return 3 * (NB - TILES) + i * TILES + b - (NB - TILES)
    return 3 * b + i


def y_order(b, i):
    if isinstance(b, int) and b >= NB - TILES:
        q = b - (NB - TILES)
        return 3 * (NB - TILES) + (2 * q + i if i < 2 else 2 * TILES + q)
    return 3 * b + i


class SecondAttention:

    def __init__(self, ctx, nc, t, w):
        def sb(name, shape):
            return ctx.enter_context(nc.sbuf_tensor(name, shape, F32))

        self.t, self.w, self.s = t, w, Sems(nc, "mix")
        self.sums = sb("sums_all", [P, NB, D])
        self.y = sb("y", [P, TILES, D])
        self.stats = sb("mix_stats", [P, 3, TILES, 6])
        self.moments = sb("mix_moments", [P, 3, TILES, 2])
        self.base = sb("mix_base", [P, 3, TILES])
        self.rstd = sb("mix_rstd", [P, 2, TILES])
        self.power = sb("mix_power", [P, 1])
        for n in ["added", "rows_in", "power", "stats", "moments", "base", "rstd", "y", "beta", "mixed", "kept", "dve_seen"]:
            self.s[n]

    def dve_stage(self, dve, stage, b, q):
        t, w, s = self.t, self.w, self.s
        sums, y, stats, moments, base, rstd = self.sums, self.y, self.stats, self.moments, self.base, self.rstd

        def take_moments(i, rows):
            dve.bn_stats(stats[:, i, q, :], rows).then_inc(s["stats"], 1)
            wait_alone(dve, s["stats"], order(i) + 1, s["dve_seen"])
            dve.bn_aggr(moments[:, i, q, :], stats[:, i, q, :]).then_inc(s["moments"], 1)
            dve.wait_ge(s["moments"], order(i) + 1)
            dve.tensor_scalar(base[:, i, q:q + 1], moments[:, i, q, 1:2], EPS, None, ALU.add).then_inc(s["base"], 1)

        def order(i):
            return stage_order(i, b)

        x, yq = row(t["x"], b), y[:, q, :]
        if stage == 0:
            wait_alone(dve, s["added"], b + 2, s["dve_seen"])
            take_moments(0, x)
        elif stage == 1:
            dve.wait_ge(s["rstd"], order(0) + 1)
            dve.tensor_scalar(yq, x, moments[:, 0, q, 0:1], rstd[:, 0, q:q + 1], ALU.subtract, ALU.mult).then_inc(s["y"], 1)
            dve.wait_ge(s["y"], y_order(b, 0) + 1)
            dve.tensor_tensor(yq, yq, row(sums, b), ALU.add).then_inc(s["y"], 1)
            dve.wait_ge(s["y"], y_order(b, 1) + 1)
            take_moments(1, yq)
        else:
            dve.wait_ge(s["rstd"], order(1) + 1)
            dve.scalar_tensor_tensor(out=yq, in0=yq, scalar=moments[:, 1, q, 0:1], in1=w["gamma"][:],
                                     op0=ALU.subtract, op1=ALU.mult).then_inc(s["y"], 1)
            dve.wait_ge(s["y"], y_order(b, 2) + 1)
            dve.wait_ge(s["beta"], b + 1)
            dve.scalar_tensor_tensor(out=x, in0=yq, scalar=rstd[:, 1, q:q + 1], in1=x,
                                     op0=ALU.mult, op1=ALU.add).then_inc(s["mixed"], 1)
            wait_alone(dve, s["mixed"], b + 1, s["dve_seen"])
            take_moments(2, x)
            dve.tensor_copy(row(t["moments"], b), moments[:, 2, q, :]).then_inc(s["kept"], 1)

    def pool_stage(self, pool, stage, b, q):
        t, w, s, base, rstd = self.t, self.w, self.s, self.base, self.rstd
        if stage == 1:
            x = row(t["x"], b)
            pool.wait_ge(s["y"], y_order(b, 0) + 1)
            pool.tensor_tensor(x, x, w["beta"][:], ALU.add).then_inc(s["beta"], 1)
        out = rstd[:, stage, q:q + 1] if stage < 2 else t["rstd"][:, ds(b, 1)]
        pool.wait_ge(s["base"], stage_order(stage, b) + 1)
        pool.tensor_tensor(out, base[:, stage, q:q + 1], self.power[:], ALU.pow).then_inc(s["rstd"], 1)


def experts_phase(nc, dram, t, w, x_t, gates, scratch, mixer):
    UNITS = 3 + ROUTED_K
    AHEAD = 3
    with ExitStack() as ctx:
        s = Sems(nc, "moe")
        m = mixer.s

        def sb(name, shape, dt=F32):
            return ctx.enter_context(nc.sbuf_tensor(name, shape, dt))

        relu = sb("relu", [P, 4, CHUNK])
        gated = sb("gated", [P, 3, CHUNK])
        hidden = sb("hidden", [P, 4, 2, CHUNK], F16)
        gate_part = sb("gate_part", [P, 2, TOKENS], F16)
        grown = sb("grown", [P, NB])
        shift = sb("moe_shift", [P, NB])
        bias = sb("shared_bias", [P, D])
        QUARTER = INTER // 4
        stage = sb("stage2", [P, 2 * C * QUARTER + INTER_K * D // 4 + D])
        ps_h = ctx.enter_context(nc.psum_tensor("ps_h", [P, 4, CHUNK], F32))
        ps_o = ctx.enter_context(nc.psum_tensor("ps_o", [P, TILES, 2 * D], F32))
        for n in ["gate_high", "gate_low", "up_mm", "relu", "gated", "high", "low", "down_mm",
                  "mlp_in", "mlp_high", "mlp_low", "seen", "grown", "with_norm", "with_bias"]:
            s[n]
        block = ctx.enter_context(nc.Block())

        def mlp_quarter(j):
            moves, cuts = [], []
            for k, name in enumerate(("gate", "up")):
                v = stage[:, k * C * QUARTER:(k + 1) * C * QUARTER].rearrange("p (c f) -> p c f", c=C)
                moves.append((v, dram[f"L1_ffn_{name}_w"].rearrange("(p c) f -> p c f", c=C)[:, :, ds(j * QUARTER, QUARTER)]))
                for c in range(C):
                    dst = [w[name][:, a, c].rearrange("p (i h q) -> p h q i", i=INTER_K, h=4)[:, ds(j, 1)]
                           .rearrange("p h q i -> p (h q) i") for a in range(2)]
                    cuts.append((v[:, c].rearrange("p (q i) -> p q i", i=INTER_K), dst))
            at, n = 2 * C * QUARTER, INTER_K * D // 4
            v = stage[:, at:at + n]
            moves.append((v, dram["L1_ffn_down_w"].rearrange("(p i) d -> p (i d)", p=P)[:, ds(j * n, n)]))
            cuts.append((v, [w["down"][:, a, ds(j * n, n)] for a in range(2)]))
            v = stage[:, at + n:at + n + D]
            moves.append((v, dram["L1_ffn_up_embed"].rearrange("(k p) d -> k p d", p=P)[ds(j, 1)].rearrange("k p d -> (k p) d")))
            cuts.append((v, [w["table_up"][:, a, ds(j, 1)].rearrange("p k d -> p (k d)") for a in range(2)]))
            return moves, cuts

        MLP_CUTS = 2 * C + 2
        GROWTH_AT = (0, 1, 2, 21)
        CUTS_AT = {21: range(0, C), 22: range(C, 2 * C), 23: range(2 * C, 2 * C + 1), 24: range(2 * C + 1, MLP_CUTS)}

        class Tile:

            def __init__(self, j, base, v):
                self.n = j * UNITS + v * 3 + base
                self.buf = (base - 1) % 3 if base else 3
                self.rows = P if base >= 3 else SHARED_M[base]
                self.shared = base if base < 3 else None
                self.routed = v * 3 + (base - 3) if base >= 3 else None

        def tiles(eng, j, body, mix=None):
            for base in range(3):
                body(base, 0)
            if mix is not None:
                with eng.Fori(0, TILES) as v:
                    for base in range(3, 6):
                        body(base, v)
                        mix(base - 3, (j - 1) * TILES + v, 0)
            with eng.Fori(TILES if mix is not None else 0, 6) as v:
                for base in range(3, 6):
                    body(base, v)
            for base in range(21, UNITS):
                body(base, 0)

        @block.sync
        def _(sp):
            sp.dma_start(mixer.sums[:], scratch["summary"].partition_broadcast(P)).then_inc(m["rows_in"], 16)
            for name in ("gamma", "beta"):
                sp.dma_start(w[name][:], dram["L1_xattn_" + name].partition_broadcast(P)).then_inc(m["rows_in"], 16)
            with sp.Fori(0, CHUNKS) as j:
                wait_alone(sp, s["mlp_low"], (j + 1) * MLP_CUTS, s["seen"])
                for dst, src in mlp_quarter(j)[0]:
                    sp.dma_start(dst, src).then_inc(s["mlp_in"], 16)

        @block.tensor
        def _(pe):
            pe.sem_inc(s["down_mm"], AHEAD)

            def up(i, j):
                pe.wait_ge(s["relu"], i.n + 1)
                rows = i.rows
                for k, (a, b) in enumerate(HIGH_LOW):
                    for c in range(C):
                        if i.shared is None:
                            lhs = w["w1"][:, a, c, ds(i.routed * P, P)]
                        else:
                            lhs = w["ws1"][:, a, c, i.shared * P:i.shared * P + rows]
                        mm = pe.matmul(ps_h[0:rows, i.buf, :], lhs, x_t[:, b, c, ds(j * CHUNK, CHUNK)],
                                       start=(k == 0 and c == 0), stop=(k == 2 and c == C - 1))
                mm.then_inc(s["up_mm"], 1)

            def down(i, j, first=False, last=False):
                pe.wait_ge(s["low"], i.n + 1 + AHEAD)
                rows = i.rows
                for q in range(TILES):
                    if first:
                        for k, (a, b) in enumerate(HIGH_LOW):
                            pe.matmul(ps_o[:, q, 0:D], gate_part[:, a, ds(j * CHUNK + q * P, P)], w["b2"][:, b, :],
                                      start=(k == 0), stop=False, skip_group_check=True)
                    for k, (a, b) in enumerate(HIGH_LOW):
                        rhs = w["w2"][:, b, ds(i.routed * D, D)] if i.shared is None else w["ws2"][0:rows, b, i.shared, :]
                        mm = pe.matmul(ps_o[:, q, 0:D], hidden[0:rows, i.buf, a, q * P:(q + 1) * P], rhs,
                                       start=False, stop=(last and k == 2), skip_group_check=True)
                mm.then_inc(s["down_mm"], 1)

            def chunk(j, last):
                def body(base, v):
                    if base + 2 < UNITS:
                        up(Tile(j, base + 2, v), j)
                    elif not last:
                        up(Tile(j + 1, base + 2 - UNITS, 0), j + 1)
                    if base == 0:
                        pe.wait_ge(m["added"], j * TILES + 1)
                    down(Tile(j, base, v), j, first=(base == 0), last=(base == UNITS - 1))

                tiles(pe, j, body)

            for base in range(2):
                up(Tile(0, base, 0), 0)
            pe.wait_ge(s["gate_low"], 1)
            with pe.Fori(0, CHUNKS - 1) as j:
                chunk(j, last=False)
            chunk(CHUNKS - 1, last=True)

        @block.scalar
        def _(act):
            act.activation(gate_part[:, 0, :], gates[:], ACT.Copy).then_inc(s["gate_high"], 1)
            act.sem_inc(s["relu"], AHEAD)

            def relu_of(i):
                act.wait_ge(s["up_mm"], i.n + 1)
                act.wait_ge(s["low"], i.n + 1)
                rows = i.rows
                bias = w["bs1"][0:rows, i.shared:i.shared + 1] if i.shared is not None else w["b1"][:, ds(i.routed, 1)]
                act.activation(relu[0:rows, i.buf, :], ps_h[0:rows, i.buf, :], ACT.Relu, bias=bias, scale=DOWN).then_inc(s["relu"], 1)

            def high(i, j):
                rows = i.rows
                act.wait_ge(s["down_mm"], i.n + 1)
                if i.shared is None:
                    act.wait_ge(s["gated"], j * ROUTED_K + i.routed + 1)
                else:
                    act.wait_ge(s["relu"], i.n + 1 + AHEAD)
                src = gated if i.shared is None else relu
                act.activation(hidden[0:rows, i.buf, 0, :], src[0:rows, i.buf, :], ACT.Copy).then_inc(s["high"], 1)

            with act.Fori(0, CHUNKS) as j:
                relu_of(Tile(j, 0, 0))

                def body(base, v):
                    if base + 1 < UNITS:
                        relu_of(Tile(j, base + 1, v))
                    high(Tile(j, base, v), j)
                    if base in GROWTH_AT:
                        act.wait_ge(s["grown"], 3)
                        b = j * TILES + GROWTH_AT.index(base)
                        act.activation(row(t["x"], b), row(t["x"], b), ACT.Identity, scale=grown[:, ds(b, 1)],
                                       bias=shift[:, ds(b, 1)]).then_inc(s["with_norm"], 1)
                    for c in CUTS_AT.get(base, ()):
                        act.wait_ge(s["mlp_in"], 64 * (j + 1))
                        src, dst = mlp_quarter(j)[1][c]
                        act.activation(dst[0], src, ACT.Copy, scale=UP).then_inc(s["mlp_high"], 1)

                tiles(act, j, body)

        @block.vector
        def _(dve):
            dve.wait_ge(s["gate_high"], 1)
            dve.tensor_tensor(gate_part[:, 1, :], gates[:], gate_part[:, 0, :], ALU.subtract).then_inc(s["gate_low"], 1)

            def chunk(j, mixes):
                def body(base, v):
                    i = Tile(j, base, v)
                    if i.shared is None:
                        dve.wait_ge(s["relu"], i.n + 1 + AHEAD)
                        dve.wait_ge(s["low"], i.n + 1)
                        dve.tensor_tensor(gated[:, i.buf, :], relu[:, i.buf, :], gates[:, ds(j * CHUNK, CHUNK)],
                                          ALU.mult).then_inc(s["gated"], 1)
                    for c in CUTS_AT.get(base, ()):
                        dve.wait_ge(s["mlp_high"], MLP_CUTS * j + c + 1)
                        src, dst = mlp_quarter(j)[1][c]
                        dve.scalar_tensor_tensor(out=dst[1], in0=src, scalar=UP, in1=dst[0],
                                                 op0=ALU.mult, op1=ALU.subtract).then_inc(s["mlp_low"], 1)

                tiles(dve, j, body, mixes)
                dve.wait_ge(s["down_mm"], j * UNITS + (UNITS + AHEAD))
                dve.wait_ge(s["with_bias"], (j + 1) * TILES)
                for q in range(TILES):
                    x = row(t["x"], j * TILES + q)
                    dve.scalar_tensor_tensor(out=x, in0=ps_o[:, q, 0:D], scalar=DOWN, in1=x,
                                             op0=ALU.mult, op1=ALU.add).then_inc(m["added"], 1)

            dve.tensor_scalar(grown[:], t["rstd"][:], 1.0, None, ALU.add).then_inc(s["grown"], 1)
            dve.scalar_tensor_tensor(out=shift[:], in0=t["moments"][:, :, 0], scalar=-1.0, in1=t["rstd"][:],
                                     op0=ALU.mult, op1=ALU.mult).then_inc(s["grown"], 1)
            dve.tensor_tensor(bias[:], w["bs2"][:, 0], w["bs2"][:, 1], ALU.add).then_inc(s["grown"], 1)
            dve.wait_ge(m["rows_in"], 48)
            dve.wait_ge(s["grown"], 3)
            chunk(0, None)
            with dve.Fori(1, CHUNKS) as j:
                chunk(j, lambda stage, b, q: mixer.dve_stage(dve, stage, b, q))
            dve.wait_ge(m["added"], 1 + NB)
            dve.wait_ge(s["mlp_low"], MLP_CUTS * (CHUNKS + 1))

        @block.gpsimd
        def _(pool):
            pool.sem_inc(s["low"], AHEAD)
            pool.sem_inc(m["added"], 1)

            pool.sem_inc(s["mlp_low"], MLP_CUTS)
            pool.memset(mixer.power[:], -0.5).then_inc(m["power"], 1)
            pool.wait_ge(m["power"], 1)
            pool.wait_ge(m["rows_in"], 48)

            def chunk(j, mixes):
                def body(base, v):
                    i = Tile(j, base, v)
                    pool.wait_ge(s["high"], i.n + 1)
                    src = gated if i.shared is None else relu
                    pool.tensor_tensor(hidden[0:i.rows, i.buf, 1, :], src[0:i.rows, i.buf, :], hidden[0:i.rows, i.buf, 0, :],
                                       ALU.subtract).then_inc(s["low"], 1)
                    if base in GROWTH_AT:
                        b = j * TILES + GROWTH_AT.index(base)
                        pool.wait_ge(s["with_norm"], b + 1)
                        pool.tensor_tensor(row(t["x"], b), row(t["x"], b), bias[:], ALU.add).then_inc(s["with_bias"], 1)

                tiles(pool, j, body, mixes)

            chunk(0, None)
            with pool.Fori(1, CHUNKS) as j:
                chunk(j, lambda stage, b, q: mixer.pool_stage(pool, stage, b, q))


def query_phase(nc, t, w, x_t, s, mixer, routing, best):
    SLOTS = 3
    STEPS = NB + 9
    SETS = 2 * TOKENS // P // CHUNKS
    done = NB
    with ExitStack() as ctx:
        def sb(name, shape, dt=F32):
            return ctx.enter_context(nc.sbuf_tensor(name, shape, dt))

        q = sb("q_line", [P, 2 * TOKENS], F16)
        normed = sb("normed1", [P, SLOTS, D])
        shift = sb("query_shift", [P, NB])
        turned = ctx.enter_context(nc.psum_tensor("turned1", [P, SLOTS, C, D], F32))
        ps_q = ctx.enter_context(nc.psum_tensor("ps_q", [P, 2, CHUNK], F32))
        ps_r = ctx.enter_context(nc.psum_tensor("ps_r", [P, 2, CHUNK], F32))
        own = Sems(nc, "query")
        for n in ["query_mm", "high", "low", "key_mm", "out", "best", "shift"]:
            own[n]
        block = ctx.enter_context(nc.Block())
        line = q[:].rearrange("p (n r) -> p r n", r=2)

        def chunk_at(i, lag):
            j = (i - lag) // TILES
            return j if (i - lag) % TILES == 0 and 0 <= j < CHUNKS else None

        @block.tensor
        def _(pe):
            for i in range(STEPS):
                if i < NB:
                    if i >= SLOTS:
                        pe.wait_ge(s["low"], done + i - SLOTS + 1)
                    pe.wait_ge(s["normed"], on_act(NB) + i + 1)
                    for c in range(C):
                        turn = pe.transpose(turned[:, i % SLOTS, c, 0:P], normed[:, i % SLOTS, c::C], t["ident"][:])
                    turn.then_inc(s["turned"], 1)
                j = chunk_at(i, 10)
                if j is not None:
                    pe.wait_ge(own["low"], 2 * j + 2)
                    if j >= 2:
                        pe.wait_ge(own["out"], j - 1)
                    for n in range(SETS):
                        tile = j * SETS + n
                        for a in range(2):
                            mm = pe.matmul(ps_r[:, j % 2, n * KEYS:(n + 1) * KEYS], q[:, tile * P:(tile + 1) * P],
                                           w["keys"][:, a, tile // NB, :], start=(a == 0), stop=(a == 1))
                    mm.then_inc(own["key_mm"], 1)
                j = chunk_at(i, 6)
                if j is not None:
                    pe.wait_ge(s["low"], done + TILES * (j + 1))
                    for r in range(2):
                        if j > 0:
                            pe.wait_ge(own["low"], 2 * j + r - 1)
                        for k, (a, b) in enumerate(HIGH_LOW):
                            for c in range(C):
                                mm = pe.matmul(ps_q[:, r, :], w["query"][:, a, c, r, :], x_t[:, b, c, j * CHUNK:(j + 1) * CHUNK],
                                               start=(k == 0 and c == 0), stop=(k == 2 and c == C - 1))
                        mm.then_inc(own["query_mm"], 1)

        @block.scalar
        def _(act):
            for i in range(STEPS):
                if i < NB:
                    act.wait_ge(own["shift"], 1 if i < NB - TILES else 2)
                    if i >= SLOTS:
                        act.wait_ge(s["turned"], done + i - SLOTS + 1)
                    act.activation(normed[:, i % SLOTS], t["x"][:, i, :], ACT.Identity, scale=t["rstd"][:, i:i + 1],
                                   bias=shift[:, i:i + 1]).then_inc(s["normed"], 1)
                n = i - 2
                if 0 <= n < NB:
                    act.wait_ge(s["turned"], done + n + 1)
                    act.activation(x_t[:, 0, :, n * P:(n + 1) * P], turned[:, n % SLOTS, :, 0:P], ACT.Copy).then_inc(s["high"], 1)
                j = chunk_at(i, 8)
                if j is not None:
                    for r in range(2):
                        act.wait_ge(own["query_mm"], 2 * j + r + 1)
                        act.activation(line[:, r, j * CHUNK:(j + 1) * CHUNK], ps_q[:, r, :], ACT.Copy, scale=DOWN).then_inc(own["high"], 1)
                j = chunk_at(i, 11)
                if j is not None:
                    act.wait_ge(own["key_mm"], j + 1)
                    act.activation(routing[:, j * SETS:(j + 1) * SETS, :], ps_r[:, j % 2, :].rearrange("p (g k) -> p g k", g=SETS),
                                   ACT.Copy, scale=DOWN).then_inc(own["out"], 1)
            act.wait_ge(own["high"], 2 * CHUNKS)
            act.wait_ge(own["out"], CHUNKS)

        @block.gpsimd
        def _(pool):
            for stage in range(3):
                for slot in range(TILES):
                    mixer.pool_stage(pool, stage, NB - TILES + slot, slot)

        @block.vector
        def _(dve):
            def take_shift(first, last):
                dve.scalar_tensor_tensor(out=shift[:, first:last], in0=t["moments"][:, first:last, 0], scalar=-1.0,
                                         in1=t["rstd"][:, first:last], op0=ALU.mult, op1=ALU.mult).then_inc(own["shift"], 1)

            take_shift(0, NB - TILES)
            for i in range(STEPS):
                if i < 3 * TILES:
                    mixer.dve_stage(dve, i // TILES, NB - TILES + i % TILES, i % TILES)
                if i == 3 * TILES:
                    dve.wait_ge(mixer.s["kept"], NB)
                    dve.wait_ge(mixer.s["rstd"], 3 * NB)
                    take_shift(NB - TILES, NB)
                n = i - 2
                if 0 <= n < NB:
                    dve.wait_ge(s["high"], done + n + 1)
                    dve.tensor_tensor(x_t[:, 1, :, n * P:(n + 1) * P], turned[:, n % SLOTS, :, 0:P],
                                      x_t[:, 0, :, n * P:(n + 1) * P], ALU.subtract).then_inc(s["low"], 1)
                j = chunk_at(i, 9)
                if j is not None:
                    for r in range(2):
                        dve.wait_ge(own["high"], 2 * j + r + 1)
                        part = line[KDIM:P, r, j * CHUNK:(j + 1) * CHUNK]
                        dve.scalar_tensor_tensor(out=part, in0=ps_q[KDIM:P, r, :], scalar=DOWN, in1=part,
                                                 op0=ALU.mult, op1=ALU.subtract).then_inc(own["low"], 1)
                j = chunk_at(i, 12)
                if j is not None:
                    dve.wait_ge(own["out"], j + 1)
                    for n in range(j * SETS, (j + 1) * SETS):
                        dve.max(best[:, n, :], routing[:, n, :]).then_inc(own["best"], 1)
            dve.wait_ge(own["best"], 2 * NB)
            dve.wait_ge(own["low"], 2 * CHUNKS)


def ffn_phase(nc, dram, t, w, x_t, routing, best):
    with ExitStack() as ctx:
        s = Sems(nc, "ffn")

        def sb(name, shape, dt=F32):
            return ctx.enter_context(nc.sbuf_tensor(name, shape, dt))

        pairs = sb("pairs", [P, NB, 8, 8])
        top = sb("top", [P, NB, 8])
        lowered = sb("lowered", [P, NB, 8])
        exps = sb("exps", [P, NB, 8])
        total = sb("total3", [P, NB])
        inverse = sb("inverse3", [P, NB])
        key_exp = sb("key_exp", [P, 2 * NB, KEYS])
        pair_sum = sb("pair_sum", [P, KEYS // 8, KEYS])
        pair_exp = sb("pair_exp", [P, KEYS // 8, KEYS])
        picks = sb("picks", [P, TABLE])
        listed = sb("listed", [P, 1])
        act_g = sb("act_g", [P, 2, CHUNK])
        prod = sb("prod", [P, 2, CHUNK])
        hidden = sb("hidden2", [P, 2, 2, CHUNK], F16)
        act_e = sb("act_e", [P, 2, TABLE])
        weight = sb("weight2", [P, 2, TABLE])
        weight_t = sb("weight_t", [P, 2, 2, TABLE_K, P], F16)
        ps_g = ctx.enter_context(nc.psum_tensor("ps_g", [P, 2, 2, CHUNK], F32))
        ps_e = ctx.enter_context(nc.psum_tensor("ps_e", [P, 2, TABLE], F32))
        ps_o = ctx.enter_context(nc.psum_tensor("ps_out", [P, TILES // 2, 2, D], F32))
        for n in ["gate_mm", "up_mm", "act_g", "prod", "high", "low", "down_mm", "table_mm", "act_e", "weight",
                  "turned", "wt_high", "wt_low", "row_mm", "added", "stored", "seen",
                  "key_low", "pairs", "top", "lowered", "exps", "total", "pair_sum", "pair_exp", "picks"]:
            s[n]
        block = ctx.enter_context(nc.Block())
        K = INTER_K

        @block.tensor
        def _(pe):
            def product(out, lhs, rhs, start, stop):
                for k, (a, b) in enumerate(HIGH_LOW):
                    for c in range(C):
                        mm = pe.matmul(out, lhs(a, c), rhs(b, c), start=(start and k == 0 and c == 0), stop=(stop and k == 2 and c == C - 1))
                return mm

            def up(i, j):
                n = j * K + i
                pe.wait_ge(s["prod"], n + 1)
                for which, name in ((0, "gate"), (1, "up")):
                    product(ps_g[:, i % 2, which, :], lambda a, c: w[name][:, a, c, i * P:(i + 1) * P],
                            lambda b, c: x_t[:, b, c, ds(j * CHUNK, CHUNK)], True, True).then_inc(s[name + "_mm"], 1)

            def down(i, j):
                n = j * K + i
                pe.wait_ge(s["low"], n + 2)
                if i == 0:
                    pe.wait_ge(s["added"], j * TILES + 1)
                for q in range(TILES):
                    for k, (a, b) in enumerate(HIGH_LOW):
                        mm = pe.matmul(ps_o[:, q // 2, q % 2, :], hidden[:, i % 2, a, q * P:(q + 1) * P],
                                       w["down"][:, b, i * D:(i + 1) * D], start=(i == 0 and k == 0 and q % 2 == 0),
                                       stop=False, skip_group_check=True)
                mm.then_inc(s["down_mm"], 1)

            def table(q, j):
                n = j * TILES + q
                pe.wait_ge(s["wt_low"], n + 1)
                product(ps_e[:, q % 2, :], lambda a, c: x_t[:, a, c, ds(j * CHUNK + q * P, P)],
                        lambda b, c: w["table_down"][:, b, c, :], True, True).then_inc(s["table_mm"], 1)

            def turn(q, j):
                pe.wait_ge(s["weight"], j * TILES + q + 2)
                for k in range(TABLE_K):
                    mm = pe.transpose(ps_e[:, q % 2, k * P:(k + 1) * P], weight[:, q % 2, k * P:(k + 1) * P], t["ident"][:])
                mm.then_inc(s["turned"], 1)

            def rows(q, j):
                pe.wait_ge(s["wt_low"], j * TILES + q + 3)
                for k, (a, b) in enumerate(HIGH_LOW):
                    for i in range(TABLE_K):
                        mm = pe.matmul(ps_o[:, q // 2, q % 2, :], weight_t[:, q % 2, a, i, :], w["table_up"][:, b, i, :],
                                       start=False, stop=(q % 2 == 1 and k == 2 and i == TABLE_K - 1), skip_group_check=True)
                mm.then_inc(s["row_mm"], 1)

            with pe.Fori(0, CHUNKS) as j:
                up(0, j)
                for i in range(K):
                    if i % 2 == 0:
                        table(i // 2, j)
                    if i + 1 < K:
                        up(i + 1, j)
                    if i % 2 == 1:
                        turn(i // 2, j)
                    down(i, j)
                    if i % 2 == 0 and i > 0:
                        rows(i // 2 - 1, j)
                rows(TILES - 1, j)

        @block.scalar
        def _(act):
            act.wait_ge(s["lowered"], 1)
            act.activation(exps[:], lowered[:], ACT.Exp).then_inc(s["exps"], 1)
            act.wait_ge(s["key_low"], 1)
            act.activation(key_exp[:], key_exp[:], ACT.Exp).then_inc(s["exps"], 1)
            with act.Fori(0, CHUNKS) as j:
                for i in range(K):
                    n = j * K + i
                    act.wait_ge(s["gate_mm"], n + 1)
                    act.wait_ge(s["prod"], n + 1)
                    act.activation(act_g[:, i % 2, :], ps_g[:, i % 2, 0, :], ACT.Silu, scale=DOWN).then_inc(s["act_g"], 1)
                    act.wait_ge(s["prod"], n + 3)
                    act.wait_ge(s["down_mm"], n + 1)
                    act.activation(hidden[:, i % 2, 0, :], prod[:, i % 2, :], ACT.Copy).then_inc(s["high"], 1)
                    if i % 2 == 0:
                        q = i // 2
                        m = j * TILES + q
                        act.wait_ge(s["table_mm"], m + 1)
                        act.wait_ge(s["weight"], m + 1)
                        act.activation(act_e[:, q % 2, :], ps_e[:, q % 2, :], ACT.Silu, scale=DOWN).then_inc(s["act_e"], 1)
                    if i % 2 == 1:
                        q = i // 2
                        m = j * TILES + q
                        act.wait_ge(s["turned"], m + 2)
                        act.wait_ge(s["row_mm"], m + 1)
                        act.activation(weight_t[:, q % 2, 0].rearrange("p k n -> p (k n)"), ps_e[:, q % 2, :], ACT.Copy).then_inc(s["wt_high"], 1)

        @block.vector
        def _(dve):
            dve.sem_inc(s["prod"], 2)
            dve.sem_inc(s["down_mm"], 2)
            dve.sem_inc(s["row_mm"], 2)
            dve.sem_inc(s["wt_low"], 2)
            dve.sem_inc(s["added"], 1)
            dve.sem_inc(s["weight"], 1)
            dve.sem_inc(s["turned"], 1)
            dve.sem_inc(s["low"], 1)
            for i in range(8):
                dve.tensor_tensor(pairs[:, :, i, :], best[:, NB:2 * NB, :], best[:, 0:NB, i:i + 1].broadcast_to([P, NB, 8]),
                                  ALU.add).then_inc(s["pairs"], 1)
            dve.wait_ge(s["pairs"], 8)
            for b in range(NB):
                dve.max(top[:, b, :], pairs[:, b]).then_inc(s["top"], 1)
            dve.wait_ge(s["top"], NB)
            dve.tensor_tensor(lowered[:], top[:], top[:, :, 0:1].broadcast_to([P, NB, 8]), ALU.subtract).then_inc(s["lowered"], 1)
            dve.wait_ge(s["exps"], 1)
            dve.tensor_reduce(total[:], exps[:], AX.X, ALU.add).then_inc(s["total"], 1)
            dve.wait_ge(s["total"], 1)
            dve.reciprocal(inverse[:], total[:]).then_inc(s["total"], 1)
            dve.wait_ge(s["total"], 2)
            dve.wait_ge(s["exps"], 2)

            def table_pairs(line, m):
                first = line[:, ds(m, 1), 0:KEYS // 8].rearrange("p o i -> p (o i)")
                second = line[:, ds(m + NB, 1), :].rearrange("p o k -> p (o k)")
                return (first.unsqueeze(2).broadcast_to([P, KEYS // 8, KEYS]),
                        second.unsqueeze(1).broadcast_to([P, KEYS // 8, KEYS]))

            with dve.Fori(0, CHUNKS) as j:
                for i in range(K):
                    n = j * K + i
                    dve.wait_ge(s["act_g"], n + 1)
                    dve.wait_ge(s["up_mm"], n + 1)
                    dve.wait_ge(s["low"], n + 1)
                    dve.scalar_tensor_tensor(out=prod[:, i % 2, :], in0=ps_g[:, i % 2, 1, :], scalar=DOWN, in1=act_g[:, i % 2, :],
                                             op0=ALU.mult, op1=ALU.mult).then_inc(s["prod"], 1)
                    if i % 2 == 0:
                        q = i // 2
                        m = j * TILES + q
                        dve.tensor_tensor(pair_sum[:], *table_pairs(routing, m), ALU.add).then_inc(s["pair_sum"], 1)
                        dve.tensor_tensor(pair_exp[:], *table_pairs(key_exp, m), ALU.mult).then_inc(s["pair_exp"], 1)
                        dve.wait_ge(s["pair_sum"], m + 1)
                        dve.wait_ge(s["pair_exp"], m + 1)
                        dve.scalar_tensor_tensor(out=picks[:, 0:TABLE - 1], in0=pair_sum[:].rearrange("p i j -> p (i j)")[:, 0:TABLE - 1],
                                                 scalar=top[:, ds(m, 1), 7:8].rearrange("p o k -> p (o k)"),
                                                 in1=pair_exp[:].rearrange("p i j -> p (i j)")[:, 0:TABLE - 1], op0=ALU.is_ge, op1=ALU.mult,
                                                 accum_out=listed[:]).then_inc(s["picks"], 1)
                        dve.wait_ge(s["picks"], 2 * m + 1)
                        dve.tensor_tensor(picks[:, TABLE - 1:TABLE], total[:, ds(m, 1)], listed[:], ALU.subtract).then_inc(s["picks"], 1)
                        dve.wait_ge(s["picks"], 2 * m + 2)
                        dve.wait_ge(s["act_e"], m + 1)
                        dve.wait_ge(s["turned"], m + 1)
                        dve.scalar_tensor_tensor(out=weight[:, q % 2, :], in0=picks[:],
                                                 scalar=inverse[:, ds(m, 1)], in1=act_e[:, q % 2, :],
                                                 op0=ALU.mult, op1=ALU.mult).then_inc(s["weight"], 1)
                    if i % 2 == 1:
                        q = i // 2
                        m = j * TILES + q
                        dve.wait_ge(s["wt_high"], m + 1)
                        dve.tensor_tensor(weight_t[:, q % 2, 1].rearrange("p k n -> p (k n)"), ps_e[:, q % 2, :],
                                          weight_t[:, q % 2, 0].rearrange("p k n -> p (k n)"), ALU.subtract).then_inc(s["wt_low"], 1)
                dve.wait_ge(s["row_mm"], j * TILES + TILES + 2)
                for q in range(TILES):
                    x = t["x"][:, ds(j * TILES + q, 1), :].rearrange("p o d -> p (o d)")
                    dve.scalar_tensor_tensor(out=x, in0=ps_o[:, q // 2, q % 2, :], scalar=DOWN, in1=x,
                                             op0=ALU.mult, op1=ALU.add).then_inc(s["added"], 1)

        @block.gpsimd
        def _(pool):
            pool.tensor_tensor(key_exp[:], routing[:], best[:, :, 0:1].broadcast_to([P, 2 * NB, KEYS]), ALU.subtract).then_inc(s["key_low"], 1)
            with pool.Fori(0, CHUNKS) as j:
                for i in range(K):
                    n = j * K + i
                    pool.wait_ge(s["high"], n + 1)
                    pool.tensor_tensor(hidden[:, i % 2, 1, :], prod[:, i % 2, :], hidden[:, i % 2, 0, :], ALU.subtract).then_inc(s["low"], 1)

        @block.sync
        def _(sp):
            with sp.Fori(0, CHUNKS) as j:
                wait_alone(sp, s["added"], j * TILES + (TILES + 1), s["seen"])
                sp.dma_start(dram["out"][ds(j * TILES, TILES)].rearrange("b p d -> p b d"), t["x"][:, ds(j * TILES, TILES), :]).then_inc(s["stored"], 16)
            sp.wait_ge(s["stored"], 16 * CHUNKS)


def two_layers(nc, dram):
    scratch = scratch_tensors(nc)
    with ExitStack() as ctx:
        t = lasting_tensors(ctx, nc)
        w = weight_tensors(ctx, nc)
        turn = Sems(nc, "turn")
        for n in ["normed", "turned", "high", "low"]:
            turn[n]
        with ExitStack() as inner:
            attention = dict(t, **attention_tensors(inner, nc))
            setup_phase(nc, dram, attention, scratch, w)
            sems = Sems(nc, "att")
            attention_phase(nc, dram, attention, scratch, w, sems)
            sems.clear()
        w.update(mlp_tensors(ctx, nc))
        x_t = ctx.enter_context(nc.sbuf_tensor("x_t", [P, 2, C, TOKENS], F16))
        mixer = SecondAttention(ctx, nc, t, w)
        with nc.sbuf_tensor("gates", [P, TOKENS], F32) as gates:
            route_phase(nc, t, w, x_t, turn, gates)
            experts_phase(nc, dram, t, w, x_t, gates, scratch, mixer)
        with (nc.sbuf_tensor("routing", [P, 2 * NB, KEYS], F32) as routing,
              nc.sbuf_tensor("best_keys", [P, 2 * NB, 8], F32) as best):
            query_phase(nc, t, w, x_t, turn, mixer, routing, best)
            ffn_phase(nc, dram, t, w, x_t, routing, best)


INPUTS = [
    "x", "ctx_2048", "mask_Bx1x2048_fk1", "L0_xattn_Wq", "L0_xattn_bq", "L0_xattn_Wk",
    "L0_xattn_bk", "L0_xattn_Wv", "L0_xattn_bv", "L0_ffn_shared_w1", "L0_ffn_shared_b1",
    "L0_ffn_shared_w2", "L0_ffn_shared_b2", "L0_ffn_routed_w1", "L0_ffn_routed_b1",
    "L0_ffn_routed_w2", "L0_ffn_routed_b2", "L0_ffn_centroids", "L0_ffn_bias", "L1_xattn_decay",
    "L1_xattn_W_in", "L1_xattn_b_in", "L1_xattn_W_out", "L1_xattn_b_out", "L1_xattn_gamma",
    "L1_xattn_beta", "L1_ffn_W_q", "L1_ffn_keys", "L1_ffn_down_embed", "L1_ffn_up_embed",
    "L1_ffn_gate_w", "L1_ffn_up_w", "L1_ffn_down_w"]


def kernel(**inputs):
    import numpy as np
    import concourse.bacc as bacc
    from concourse.bass_utils import run_bass_kernel_spmd

    nc = bacc.Bacc("TRN2", target_bir_lowering=False, num_devices=1)
    arrays, dram = {}, {}
    for name in INPUTS:
        a = np.ascontiguousarray(inputs[name])
        if a.ndim == 0:
            a = a.reshape(1)
        arrays[f"in_{name}_dram"] = a
        dram[name] = nc.dram_tensor(f"in_{name}_dram", a.shape, mybir.dt.from_np(a.dtype), kind="ExternalInput").ap()
    dram["out"] = nc.dram_tensor("out_0_dram", (NB, P, D), F32, kind="ExternalOutput").ap()
    two_layers(nc, dram)
    return run_bass_kernel_spmd(nc, [arrays], core_ids=[0]).results[0]["out_0_dram"]
```
